# Optimizing a Trainium2 kernel written in Bass

```python
import numpy as np
import jax
import jax.numpy as jnp

def _softmax(x, axis=-1):
    return jax.nn.softmax(x, axis=axis)

def _gelu(x):
    return jax.nn.gelu(x, approximate=True)

def _silu(x):
    return jax.nn.silu(x)

def _sigmoid(x):
    return jax.nn.sigmoid(x)

def _layernorm(x, axis=-1, eps=1e-05):
    m = jnp.mean(x, axis=axis, keepdims=True)
    v = jnp.var(x, axis=axis, keepdims=True)
    return (x - m) / jnp.sqrt(v + eps)

def _scatter_add(tgt, idx, src, axis=0):
    return tgt.at[idx].add(src)

def _segment_sum(src, seg, n):
    return jax.ops.segment_sum(src, seg, n)
kernel_name = 'mk_early_fusion_d1_tok_img768_r4_f15a4a'

def setup_inputs(seed: int=0):
    np.random.seed(seed)
    _w = jnp.asarray

    def _rec_inputs():
        import jax
        import jax.numpy as jnp
        _rk = jax.random.key(seed)
        x = -9.30917e-05 + 1.0002 * jax.random.normal(jax.random.fold_in(_rk, 1), (64, 3, 224, 224), jnp.float32)
        txt = -0.000192023 + 1.00029 * jax.random.normal(jax.random.fold_in(_rk, 2), (64, 128, 192), jnp.float32)
        return (x, txt)
    x, txt = _rec_inputs()

    def _L0_tok_setup():
        import jax, jax.numpy as jnp
        import numpy as np
        PATCH = 16
        EPS = 1e-05

        def _shift(x, pad_spec):
            l, r, t, b = pad_spec
            H, W = (x.shape[2], x.shape[3])
            xp = jnp.pad(x, ((0, 0), (0, 0), (max(t, 0), max(b, 0)), (max(l, 0), max(r, 0))))
            h0 = -t if t < 0 else 0
            w0 = -l if l < 0 else 0
            return xp[:, :, h0:h0 + H, w0:w0 + W]
        key = jax.random.key(seed)
        k1, k2 = jax.random.split(key)
        B, C, H, Wd = (32, 3, 224, 224)
        patch_dim = PATCH * PATCH * 5 * C
        dim = 192
        x = jax.random.normal(k1, (B, C, H, Wd), dtype=jnp.float32)
        ln_gamma = jnp.ones((patch_dim,), dtype=jnp.float32)
        ln_beta = jnp.zeros((patch_dim,), dtype=jnp.float32)
        W = jax.random.normal(k2, (patch_dim, dim), dtype=jnp.float32) * patch_dim ** (-0.5)
        b = jnp.zeros((dim,), dtype=jnp.float32)
        return {'x': x, 'ln_gamma': ln_gamma, 'ln_beta': ln_beta, 'W': W, 'b': b}
    _L0_tok_all = _L0_tok_setup()
    _L0_tok_in = {k: v for k, v in _L0_tok_all.items() if k in ('ln_gamma', 'ln_beta', 'W', 'b')}
    del _L0_tok_all

    def _L0_attn_setup():
        import jax, jax.numpy as jnp
        import numpy as np
        N_HEAD = 12
        N_EMBD = 192
        BLOCK = 512
        THETA = 10000.0

        def _rope_tables(head_dim, end, theta=THETA):
            half = head_dim // 2
            freqs = 1.0 / theta ** (jnp.arange(0, head_dim, 2, dtype=jnp.float32) / head_dim)
            t = jnp.arange(end, dtype=jnp.float32)
            ang = jnp.outer(t, freqs)
            return (jnp.cos(ang), jnp.sin(ang))

        def _apply_rope(x, cos, sin):
            B, H, T, hd = x.shape
            xr = x.reshape(B, H, T, hd // 2, 2)
            x0, x1 = (xr[..., 0], xr[..., 1])
            c = cos[None, None, :T, :]
            s = sin[None, None, :T, :]
            o0 = x0 * c - x1 * s
            o1 = x0 * s + x1 * c
            return jnp.stack([o0, o1], axis=-1).reshape(B, H, T, hd)
        key = jax.random.key(seed)
        ks = jax.random.split(key, 9)
        B, T, C = (2, 512, N_EMBD)
        std = 0.02
        return {'x': jax.random.normal(ks[0], (B, T, C), jnp.float32), 'norm_scale': jnp.ones((C,), jnp.float32), 'norm_bias': jnp.zeros((C,), jnp.float32), 'W_attn': jax.random.normal(ks[1], (C, 3 * C), jnp.float32) * std, 'b_attn': jax.random.normal(ks[2], (3 * C,), jnp.float32) * std, 'W_proj': jax.random.normal(ks[3], (C, C), jnp.float32) * std, 'b_proj': jax.random.normal(ks[4], (C,), jnp.float32) * std, 'sinks': jax.random.normal(ks[5], (N_HEAD,), jnp.float32) * 0.5, 'rezero': jax.random.normal(ks[6], (1,), jnp.float32) * 0.1}
    _L0_attn_all = _L0_attn_setup()
    _L0_attn_in = {k: v for k, v in _L0_attn_all.items() if k in ('norm_scale', 'norm_bias', 'W_attn', 'b_attn', 'W_proj', 'b_proj', 'sinks', 'rezero')}
    del _L0_attn_all

    def _L0_ffn_setup():
        import jax, jax.numpy as jnp
        import numpy as np
        EPS_NORM = 1e-05
        RMS_EPS = 1e-05

        def _l2_normalize(v):
            n = jnp.sqrt(jnp.sum(v * v, axis=-1, keepdims=True))
            return v / jnp.maximum(n, EPS_NORM)

        def _rms_norm(x, weight, eps):
            ms = jnp.mean(x * x, axis=-1, keepdims=True)
            return x * jax.lax.rsqrt(ms + eps) * weight
        key = jax.random.key(seed)
        ks = jax.random.split(key, 6)
        B, T, D = (8, 1024, 192)
        S, F = (64, 768)
        x = jax.random.normal(ks[0], (B, T, D), dtype=jnp.float32)
        slots = 0.02 * jax.random.normal(ks[1], (S, D), dtype=jnp.float32)
        scale = jnp.ones((S,), dtype=jnp.float32)
        fc1_weight = 0.02 * jax.random.normal(ks[2], (S, D, F), dtype=jnp.float32)
        fc1_bias = jnp.zeros((S, F), dtype=jnp.float32)
        fc2_weight = 0.02 * jax.random.normal(ks[3], (S, F, D), dtype=jnp.float32)
        fc2_bias = jnp.zeros((S, D), dtype=jnp.float32)
        norm_weight = jnp.ones((D,), dtype=jnp.float32)
        return {'x': x, 'slots': slots, 'scale': scale, 'fc1_weight': fc1_weight, 'fc1_bias': fc1_bias, 'fc2_weight': fc2_weight, 'fc2_bias': fc2_bias, 'norm_weight': norm_weight}
    _L0_ffn_all = _L0_ffn_setup()
    _L0_ffn_in = {k: v for k, v in _L0_ffn_all.items() if k in ('slots', 'scale', 'fc1_weight', 'fc1_bias', 'fc2_weight', 'fc2_bias', 'norm_weight')}
    del _L0_ffn_all
    return {'x': x, 'txt': txt, 'L0_tok_ln_gamma': _L0_tok_in['ln_gamma'], 'L0_tok_ln_beta': _L0_tok_in['ln_beta'], 'L0_tok_W': _L0_tok_in['W'], 'L0_tok_b': _L0_tok_in['b'], 'L0_attn_norm_scale': _L0_attn_in['norm_scale'], 'L0_attn_norm_bias': _L0_attn_in['norm_bias'], 'L0_attn_W_attn': _L0_attn_in['W_attn'], 'L0_attn_b_attn': _L0_attn_in['b_attn'], 'L0_attn_W_proj': _L0_attn_in['W_proj'], 'L0_attn_b_proj': _L0_attn_in['b_proj'], 'L0_attn_sinks': _L0_attn_in['sinks'], 'L0_attn_rezero': _L0_attn_in['rezero'], 'L0_ffn_slots': _L0_ffn_in['slots'], 'L0_ffn_scale': _L0_ffn_in['scale'], 'L0_ffn_fc1_weight': _L0_ffn_in['fc1_weight'], 'L0_ffn_fc1_bias': _L0_ffn_in['fc1_bias'], 'L0_ffn_fc2_weight': _L0_ffn_in['fc2_weight'], 'L0_ffn_fc2_bias': _L0_ffn_in['fc2_bias'], 'L0_ffn_norm_weight': _L0_ffn_in['norm_weight']}

def reference(x, txt, L0_tok_ln_gamma, L0_tok_ln_beta, L0_tok_W, L0_tok_b, L0_attn_norm_scale, L0_attn_norm_bias, L0_attn_W_attn, L0_attn_b_attn, L0_attn_W_proj, L0_attn_b_proj, L0_attn_sinks, L0_attn_rezero, L0_ffn_slots, L0_ffn_scale, L0_ffn_fc1_weight, L0_ffn_fc1_bias, L0_ffn_fc2_weight, L0_ffn_fc2_bias, L0_ffn_norm_weight):
    import jax
    import jax.numpy as jnp

    def _L0_tok_ref(x, ln_gamma, ln_beta, W, b):
        import jax, jax.numpy as jnp
        import numpy as np
        PATCH = 16
        EPS = 1e-05

        def _shift(x, pad_spec):
            l, r, t, b = pad_spec
            H, W = (x.shape[2], x.shape[3])
            xp = jnp.pad(x, ((0, 0), (0, 0), (max(t, 0), max(b, 0)), (max(l, 0), max(r, 0))))
            h0 = -t if t < 0 else 0
            w0 = -l if l < 0 else 0
            return xp[:, :, h0:h0 + H, w0:w0 + W]
        shifts = [(1, -1, 0, 0), (-1, 1, 0, 0), (0, 0, 1, -1), (0, 0, -1, 1)]
        xs = jnp.concatenate([x] + [_shift(x, s) for s in shifts], axis=1)
        B, C5, H, Wd = xs.shape
        h, w = (H // PATCH, Wd // PATCH)
        t = xs.reshape(B, C5, h, PATCH, w, PATCH)
        t = t.transpose(0, 2, 4, 3, 5, 1)
        t = t.reshape(B, h * w, PATCH * PATCH * C5)
        mu = jnp.mean(t, axis=-1, keepdims=True)
        var = jnp.var(t, axis=-1, keepdims=True)
        tn = (t - mu) * jax.lax.rsqrt(var + EPS) * ln_gamma + ln_beta
        return jnp.einsum('bnp,pd->bnd', tn, W) + b

    def _L0_attn_ref(x, norm_scale, norm_bias, W_attn, b_attn, W_proj, b_proj, sinks, rezero):
        import jax, jax.numpy as jnp
        import numpy as np
        N_HEAD = 12
        N_EMBD = 192
        BLOCK = 512
        THETA = 10000.0

        def _rope_tables(head_dim, end, theta=THETA):
            half = head_dim // 2
            freqs = 1.0 / theta ** (jnp.arange(0, head_dim, 2, dtype=jnp.float32) / head_dim)
            t = jnp.arange(end, dtype=jnp.float32)
            ang = jnp.outer(t, freqs)
            return (jnp.cos(ang), jnp.sin(ang))

        def _apply_rope(x, cos, sin):
            B, H, T, hd = x.shape
            xr = x.reshape(B, H, T, hd // 2, 2)
            x0, x1 = (xr[..., 0], xr[..., 1])
            c = cos[None, None, :T, :]
            s = sin[None, None, :T, :]
            o0 = x0 * c - x1 * s
            o1 = x0 * s + x1 * c
            return jnp.stack([o0, o1], axis=-1).reshape(B, H, T, hd)
        B, T, C = x.shape
        H = N_HEAD
        hd = C // H
        xn = norm_scale * x + norm_bias
        qkv = xn @ W_attn + b_attn
        q, k, v = jnp.split(qkv, 3, axis=-1)
        q = q.reshape(B, T, H, hd).transpose(0, 2, 1, 3)
        k = k.reshape(B, T, H, hd).transpose(0, 2, 1, 3)
        v = v.reshape(B, T, H, hd).transpose(0, 2, 1, 3)
        cos, sin = _rope_tables(hd, T)
        q = _apply_rope(q, cos, sin)
        k = _apply_rope(k, cos, sin)
        scale = 1.0 / jnp.sqrt(jnp.float32(hd))
        att = jnp.einsum('bhqd,bhkd->bhqk', q, k) * scale
        causal = jnp.tril(jnp.ones((T, T), dtype=bool))
        att = jnp.where(causal[None, None], att, -jnp.inf)
        sink_col = jnp.broadcast_to(sinks.reshape(1, H, 1, 1), (B, H, T, 1))
        att = jnp.concatenate([sink_col, att], axis=-1)
        att = jax.nn.softmax(att, axis=-1)[..., 1:]
        y = jnp.einsum('bhqk,bhkd->bhqd', att, v)
        y = y.transpose(0, 2, 1, 3).reshape(B, T, C)
        y = (y @ W_proj + b_proj) * rezero
        return y

    def _L0_ffn_ref(x, slots, scale, fc1_weight, fc1_bias, fc2_weight, fc2_bias, norm_weight):
        import jax, jax.numpy as jnp
        import numpy as np
        EPS_NORM = 1e-05
        RMS_EPS = 1e-05

        def _l2_normalize(v):
            n = jnp.sqrt(jnp.sum(v * v, axis=-1, keepdims=True))
            return v / jnp.maximum(n, EPS_NORM)

        def _rms_norm(x, weight, eps):
            ms = jnp.mean(x * x, axis=-1, keepdims=True)
            return x * jax.lax.rsqrt(ms + eps) * weight
        xn = _rms_norm(x, norm_weight, RMS_EPS)
        tok = _l2_normalize(xn)
        sl = _l2_normalize(slots) * scale[:, None]
        logits = jnp.einsum('sd,btd->bst', sl, tok)
        dispatch_w = jax.nn.softmax(logits, axis=-1)
        combine_w = jax.nn.softmax(logits, axis=-2)
        y = jnp.einsum('btd,bst->bsd', xn, dispatch_w)
        y = jnp.einsum('sio,bsi->bso', fc1_weight, y) + fc1_bias
        y = jax.nn.gelu(y, approximate=False)
        y = jnp.einsum('sio,bsi->bso', fc2_weight, y) + fc2_bias
        out = jnp.einsum('bsd,bst->btd', y, combine_w)
        return out
    h = _L0_tok_ref(x, L0_tok_ln_gamma, L0_tok_ln_beta, L0_tok_W, L0_tok_b)
    h = jnp.concatenate([h, txt], axis=1)
    h = h + _L0_attn_ref(_layernorm(h, axis=-1), L0_attn_norm_scale, L0_attn_norm_bias, L0_attn_W_attn, L0_attn_b_attn, L0_attn_W_proj, L0_attn_b_proj, L0_attn_sinks, L0_attn_rezero)
    h = h + _L0_ffn_ref(_layernorm(h, axis=-1), L0_ffn_slots, L0_ffn_scale, L0_ffn_fc1_weight, L0_ffn_fc1_bias, L0_ffn_fc2_weight, L0_ffn_fc2_bias, L0_ffn_norm_weight)
    return h

_drawn_inputs = setup_inputs


def setup_inputs(seed=0):
    import zlib

    import numpy as np

    out = dict(_drawn_inputs(seed))
    spreads = {'L0_tok_ln_gamma': (1.0, 0.2),
     'L0_tok_ln_beta': (0.0, 0.1),
     'L0_tok_b': (0.0, 0.1),
     'L0_attn_norm_scale': (1.0, 0.6),
     'L0_attn_norm_bias': (0.0, 0.8),
     'L0_ffn_scale': (1.0, 0.6),
     'L0_ffn_fc1_bias': (0.0, 0.8),
     'L0_ffn_fc2_bias': (0.0, 0.711),
     'L0_ffn_norm_weight': (1.0, 0.6)}
    factors = {'L0_attn_W_attn': 8.0,
     'L0_attn_b_attn': 8.0,
     'L0_attn_W_proj': 8.0,
     'L0_attn_b_proj': 26.287,
     'L0_attn_sinks': 40.705,
     'L0_ffn_slots': 8.0,
     'L0_ffn_fc1_weight': 8.0,
     'L0_ffn_fc2_weight': 8.0}
    for name, (base, spread) in spreads.items():
        noise = np.random.default_rng([zlib.crc32(name.encode()), seed]).standard_normal(out[name].shape)
        drawn = base * np.exp(spread * noise) if base else spread * noise
        out[name] = jnp.asarray(drawn.astype(out[name].dtype))
    for name, factor in factors.items():
        out[name] = (out[name] * factor).astype(out[name].dtype)
    return out
```

```python
from contextlib import ExitStack

import concourse.bass as bass
from concourse import mybir

F32 = mybir.dt.float32
BF16 = mybir.dt.bfloat16
ACT = mybir.ActivationFunctionType
ALU = mybir.AluOpType
AX = mybir.AxisListType

B = 64
C = 3
IMG = 224
PATCH = 16
GRID = IMG // PATCH
D = 192
HALF = D // 2
TXT = 128
PATCHES = GRID * GRID
T = PATCHES + TXT
TILE = PATCHES // 2
KP = PATCH * PATCH * 5 * C
ROWS = C * (PATCH + 2)
WIN2 = 9
EPS = 1e-5

NH = 12
HD = D // NH
PAIR = HD // 2
PARTS = 3
K_PART = [0, 0, 0, 1, 1, 2]
Q_PART = [0, 1, 2, 0, 1, 0]
SLOTS = len(K_PART)
SINK_ROW = SLOTS * HD
MAX_ROW = SINK_ROW + PARTS
STACK = MAX_ROW + PARTS
KEYS = T + 1
KTILES = [(0, 128, 0), (128, 128, 127), (256, KEYS - 256, 255)]
QTILES = [(0, 68), (68, 128), (196, 128)]
TTILES = [(0, TILE), (TILE, TILE), (2 * TILE, TXT)]
GROUPS = [(TILE, 0, 2), (TXT, 2, 3)]
STRIP = 32
EXPC = 295
MASKED = -1e30

NS = 64
F = 768
FC = F // 128
SQ, SE = 2, 2

SC, BK4, BK5, BK6, BK7 = 0, 4, 5, 6, 7


def early_fusion_kernel(nc, x, txt, gamma, beta, W, bias, nscale, nbias, Wa, ba, Wproj, bp, sinks, rezero, slots, scale,
                        fc1, b1, fc2, b2, nw, ident_c, causal_c, cos_c, sin_c, mult_c, out):
    wscr = nc.dram_tensor("centred_weights", (KP, D), F32, kind="Internal").ap()
    himg = nc.dram_tensor("residual_image", (2 * B, TILE, D), F32, kind="Internal").ap()
    htxt = nc.dram_tensor("residual_text", (B, TXT, D), F32, kind="Internal").ap()
    cscr = nc.dram_tensor("combine_weights", (B, NS, T), F32, kind="Internal").ap()
    oscr = nc.dram_tensor("expert_outputs", (B, NS, D), F32, kind="Internal").ap()

    with ExitStack() as ctx:
        def sb(name, shape, dt=F32, c=ctx):
            return c.enter_context(nc.sbuf_tensor(name, shape, dt))

        ps = ctx.enter_context(nc.psum_tensor("ps", [128, 8, 512], F32))
        ident = sb("ident", [128, 128])
        y_all = sb("y_all", [HALF + 1, 2, NS, B])

        with ExitStack() as layers:
            window_w = sb("window_w", [2 * ROWS, WIN2, D + 1], F32, layers)
            hb = sb("hb", [128, D], F32, layers)
            wqk = sb("wqk", [HALF + 1, 2, SQ * SE, HALF], F32, layers)
            wv = sb("wv", [HALF + 1, 2, D], F32, layers)
            wp = sb("wp", [HALF + 1, 2, D], F32, layers)
            nwb = sb("nwb", [128, D], F32, layers)
            slots_t = sb("slots_t", [HALF, 2, NS], F32, layers)
            sink_p = sb("sink_p", [1, PARTS, NH], BF16, layers)
            ident_b = sb("ident_b", [128, 128], BF16, layers)
            causal = sb("causal", [128, 128], BF16, layers)
            cos_t = sb("cos_t", [HALF, T], F32, layers)
            sin_t = sb("sin_t", [HALF, T], F32, layers)

            KN = KP // 128
            QROW = PATCH * 5 * C
            with ExitStack() as work:
                def tmp(name, shape, dt=F32):
                    return work.enter_context(nc.sbuf_tensor(name, shape, dt))

                def sem(name):
                    return work.enter_context(nc.semaphore(name))

                wn = tmp("wn", [128, KN, D])
                gm, bt = tmp("gm", [128, KN]), tmp("bt", [128, KN])
                wmean = tmp("wmean", [128, 128])
                biasb = tmp("biasb", [128, D])
                wa = tmp("wa", [HALF, 2, 3 * D])
                ns, nb = tmp("ns", [HALF, 2]), tmp("nb", [HALF, 2])
                bar = tmp("bar", [1, 3 * D])
                brow = tmp("brow", [1, SQ * SE, HALF])
                bvrow = tmp("bvrow", [1, D])
                rz = tmp("rz", [HALF + 1, 1])
                sl, slsq = tmp("sl", [NS, D]), tmp("slsq", [NS, D])
                scl, sn = tmp("scl", [NS, 1]), tmp("sn", [NS, 1])
                half_c = tmp("half_c", [NS, 1])
                sink_r = tmp("sink_r", [1, NH])
                sink_rest = tmp("sink_rest", [1, NH])
                causal_f = tmp("causal_f", [128, 128])
                shifted = [tmp(f"shifted{s}", [ROWS, PATCH, D]) for s in range(5)]
                acc = tmp("acc", [ROWS, PATCH + 2, D])

                loaded, zeroed, scaled, sums = sem("loaded"), sem("zeroed"), sem("scaled"), sem("sums")
                centred, stored, shifts_in = sem("centred"), sem("stored"), sem("shifts_in")
                window_sum, placed, bias_mm, bias_rows = sem("window_sum"), sem("placed"), sem("bias_mm"), sem("bias_rows")
                slot_sq, slot_norm, slot_ready, slot_mm = sem("slot_sq"), sem("slot_norm"), sem("slot_ready"), sem("slot_mm")

                def row(v):
                    return v.rearrange("(o d) -> o d", o=1)

                with nc.Block() as block:
                    @block.sync
                    def _(sp):
                        loads = [
                            (wn[:], W.rearrange("(p k) d -> p k d", k=KN)),
                            (gm[:], gamma.rearrange("(p k) -> p k", k=KN)),
                            (bt[:], beta.rearrange("(p k) -> p k", k=KN)),
                            (biasb[:], row(bias).broadcast_to((128, D))),
                            (wa[:], Wa.rearrange("(c p) n -> p c n", c=2)),
                            (bar[:], row(ba)),
                            (wp[0:HALF], Wproj.rearrange("(c p) n -> p c n", c=2)),
                            (wp[HALF:HALF + 1, 0, :], row(bp)),
                            (rz[:], row(rezero).broadcast_to((HALF + 1, 1))),
                            (nwb[:], row(nw).broadcast_to((128, D))),
                            (sl[:], slots),
                            (scl[:], scale.rearrange("(s o) -> s o", o=1)),
                            (sink_r[:], row(sinks)),
                            (ident[:], ident_c), (causal_f[:], causal_c),
                            (cos_t[:], cos_c), (sin_t[:], sin_c),
                        ]
                        for dst, src in loads:
                            sp.dma_start(dst, src).then_inc(loaded, 16)
                        for dst, src in ((ns, nscale), (nb, nbias)):
                            sp.dma_start(dst[:], src.rearrange("(c p) -> p c", c=2),
                                         allow_slow_non_contiguous=True).then_inc(loaded, 16)
                        sp.dma_start(window_w[:, :, D:D + 1], mult_c.unsqueeze(2), allow_slow_non_contiguous=True).then_inc(loaded, 16)
                        sp.wait_ge(loaded, 16 * 20)
                        sp.wait_ge(centred, 1)
                        sp.dma_start(wscr.rearrange("(p k) d -> p k d", k=KN), wn[:]).then_inc(stored, 16)
                        sp.wait_ge(stored, 16)
                        sp.wait_ge(zeroed, 2)
                        wv5 = wscr.rearrange("(r q s c) d -> s c r q d", r=PATCH, s=5, c=C)
                        n = 0
                        for s in range(5):
                            lo, hi = {3: (0, PATCH - 1), 4: (1, PATCH)}.get(s, (0, PATCH))
                            dr = {3: 1, 4: -1}.get(s, 0)
                            for c in range(C):
                                sp.dma_start(shifted[s][PATCH * c + lo:PATCH * c + hi], wv5[s, c, lo + dr:hi + dr]
                                             ).then_inc(shifts_in, 16)
                                n += 1
                        top = C * PATCH
                        sp.dma_start(shifted[3][top:top + C], wv5[3, :, 0]).then_inc(shifts_in, 16)
                        sp.dma_start(shifted[4][top + C:top + 2 * C], wv5[4, :, PATCH - 1]).then_inc(shifts_in, 16)
                        sp.wait_ge(shifts_in, 16 * (n + 2))
                        sp.wait_ge(window_sum, 1)
                        sp.dma_start(window_w[0:ROWS, :, 0:D], acc[:, 0:WIN2]).then_inc(placed, 16)
                        sp.dma_start(window_w[ROWS:2 * ROWS, :, 0:D], acc[:, WIN2:2 * WIN2]).then_inc(placed, 16)
                        sp.wait_ge(bias_rows, 1)
                        sp.dma_start(wqk[HALF:HALF + 1, 0], brow[:]).then_inc(placed, 16)
                        sp.dma_start(wv[HALF:HALF + 1, 0], bvrow[:]).then_inc(placed, 16)
                        sp.wait_ge(placed, 64)

                    @block.gpsimd
                    def _(pool):
                        pool.memset(wmean[:], 1.0 / KP)
                        pool.memset(half_c[:], 0.5)
                        for s in range(5):
                            pool.memset(shifted[s][:], 0.0)
                        pool.memset(acc[:], 0.0).then_inc(zeroed, 1)
                        pool.drain().then_inc(zeroed, 1)
                        pool.wait_ge(slot_sq, 1)
                        pool.tensor_tensor(sn[:], sn[:], half_c[:], ALU.pow).then_inc(slot_norm, 1)

                    @block.vector
                    def _(dve):
                        dve.wait_ge(loaded, 16 * 20)
                        dve.tensor_tensor_reduce(out=slsq[:], in0=sl[:], in1=sl[:], scale=1.0, scalar=0.0, op0=ALU.mult,
                                                 op1=ALU.add, accum_out=sn[:]).then_inc(slot_sq, 1)
                        dve.tensor_scalar(wp[:, 0, :], wp[:, 0, :], rz[:, 0:1], None, ALU.mult)
                        dve.tensor_scalar(wp[0:HALF, 1, :], wp[0:HALF, 1, :], rz[0:HALF, 0:1], None, ALU.mult)
                        dve.tensor_copy(ident_b[:], ident[:])
                        dve.tensor_copy(causal[:], causal_f[:])
                        dve.wait_ge(sums, 1)
                        dve.tensor_tensor(hb[:], ps[:, 0, 0:D], biasb[:], ALU.add)
                        dve.tensor_tensor(wn[:], wn[:], gm[:].unsqueeze(2).broadcast_to((128, KN, D)), ALU.mult
                                          ).then_inc(scaled, 1)
                        dve.wait_ge(slot_norm, 1)
                        dve.tensor_scalar(sn[:], sn[:], 1e-5, None, ALU.max)
                        dve.drain()
                        dve.reciprocal(sn[:], sn[:])
                        dve.drain()
                        dve.tensor_scalar(sl[:], sl[:], sn[:, 0:1], scl[:, 0:1], ALU.mult, ALU.mult).then_inc(slot_ready, 1)
                        dve.wait_ge(bias_mm, 1)
                        dve.tensor_tensor(bar[:, 0:512], ps[0:1, 2, :], bar[:, 0:512], ALU.add)
                        dve.tensor_tensor(bar[:, 512:3 * D], ps[0:1, 3, 0:3 * D - 512], bar[:, 512:3 * D], ALU.add)
                        for c in range(2):
                            dve.tensor_scalar(wa[:, c, :], wa[:, c, :], ns[:, c:c + 1], None, ALU.mult)
                        dve.drain()
                        for side in range(2):
                            k = 0.25 if side == 0 else 1.0
                            for e in range(2):
                                for c in range(2):
                                    src = wa[:, c, D * side:D * side + D].rearrange("p (h i e) -> p i h e", h=NH, e=2)[:, :, :, e]
                                    dve.tensor_scalar(wqk[0:HALF, c, 2 * side + e, :].rearrange("p (i h) -> p i h", h=NH),
                                                      src, k, None, ALU.mult)
                                src = bar[:, D * side:D * side + D].rearrange("p (h i e) -> p i h e", h=NH, e=2)[:, :, :, e]
                                dve.tensor_scalar(brow[:, 2 * side + e, :].rearrange("p (i h) -> p i h", h=NH), src, k, None,
                                                  ALU.mult)
                        dve.tensor_copy(wv[0:HALF], wa[:, :, 2 * D:3 * D])
                        dve.tensor_copy(bvrow[:], bar[:, 2 * D:3 * D])
                        dve.tensor_copy(sink_p[:, 0], sink_r[:])
                        dve.drain()
                        dve.tensor_tensor(sink_rest[:], sink_r[:], sink_p[:, 0], ALU.subtract)
                        dve.drain()
                        dve.tensor_copy(sink_p[:, 1], sink_rest[:])
                        dve.drain()
                        dve.tensor_tensor(sink_p[:, 2], sink_rest[:], sink_p[:, 1], ALU.subtract).then_inc(bias_rows, 1)
                        dve.wait_ge(sums, 2)
                        mean = ps[:, 1, 0:D].unsqueeze(1).broadcast_to((128, KN, D))
                        dve.tensor_tensor(wn[:], wn[:], mean, ALU.subtract).then_inc(centred, 1)
                        dve.wait_ge(slot_mm, 1)
                        dve.tensor_copy(slots_t[:], ps[0:HALF, 4, 0:2 * NS].rearrange("p (c s) -> p c s", c=2))
                        dve.wait_ge(shifts_in, 16 * 17)
                        for s, col in ((0, 1), (1, 0), (2, 2), (3, 1), (4, 1)):
                            dve.drain()
                            last = dve.tensor_tensor(acc[:, col:col + PATCH], acc[:, col:col + PATCH], shifted[s][:], ALU.add)
                        last.then_inc(window_sum, 1)

                    @block.tensor
                    def _(pe):
                        pe.wait_ge(loaded, 16 * 20)
                        pe.wait_ge(zeroed, 1)
                        for k in range(KN):
                            mm = pe.matmul(ps[:, 0, 0:D], bt[:, k:k + 1].broadcast_to((128, 128)), wn[:, k, :],
                                           start=(k == 0), stop=(k == KN - 1))
                        mm.then_inc(sums, 1)
                        for bank, lo, hi in ((2, 0, 512), (3, 512, 3 * D)):
                            for c in range(2):
                                mm = pe.matmul(ps[0:1, bank, 0:hi - lo], nb[:, c:c + 1], wa[:, c, lo:hi], start=(c == 0),
                                               stop=(c == 1))
                        mm.then_inc(bias_mm, 1)
                        pe.wait_ge(scaled, 1)
                        for k in range(KN):
                            mm = pe.matmul(ps[:, 1, 0:D], wmean[:], wn[:, k, :], start=(k == 0), stop=(k == KN - 1))
                        mm.then_inc(sums, 1)
                        pe.wait_ge(slot_ready, 1)
                        for c in range(2):
                            mm = pe.transpose(ps[0:HALF, 4, NS * c:NS * (c + 1)], sl[:, HALF * c:HALF * (c + 1)],
                                              ident[0:NS, 0:NS])
                        mm.then_inc(slot_mm, 1)

            with ExitStack() as work:
                def tmp(name, shape, dt=F32):
                    return work.enter_context(nc.sbuf_tensor(name, shape, dt))

                xw = [tmp(f"xw{i}", [2 * ROWS, GRID, IMG]) for i in range(2)]
                xw_flat = [t[:].rearrange("p i w -> p (i w)") for t in xw]
                xsq = tmp("xsq", [2 * ROWS, GRID * IMG])
                h_new = [tmp(f"h_new{i}", [128, 3, D]) for i in range(2)]
                h_held = tmp("h_held", [128, 3, D])
                h1 = tmp("h1", [128, 3, D])
                xhat = tmp("xhat", [128, 3, D])
                z = tmp("z", [128, 3, D])
                ynorm = xhat
                xt = tmp("xt", [HALF + 1, 2, KEYS])
                zt = tmp("zt", [HALF, 2, T])
                yt = tmp("yt", [HALF + 1, 2, T])
                by_cos, by_sin = tmp("by_cos", [HALF, SQ, SE, T]), tmp("by_sin", [HALF, SQ, SE, T])
                rot = tmp("rot", [HALF, SQ, SE, T])
                rest = by_cos
                part = [tmp(f"part{i}", [HALF, SQ, SE, T], BF16) for i in range(PARTS)]
                kst = [tmp(f"kst{i}", [128, NH, 3 * 128], BF16) for i in range(2)]
                qst = [tmp(f"qst{i}", [128, NH, T], BF16) for i in range(2)]
                vaug = [tmp(f"vaug{i}", [128, 3, NH, STRIP]) for i in range(2)]
                prob = tmp("prob", [128, 8, 2 * EXPC])
                yraw = tmp("yraw", [128, 3, T])
                negmax, mrest = tmp("negmax", [128, 3, NH]), tmp("mrest", [128, 3, NH])
                mpart = tmp("mpart", [128, 3, PARTS, NH], BF16)
                mt = tmp("mt", [PARTS * NH, T], BF16)
                rden = tmp("rden", [128, 3, NH])
                stat1, rstd1 = tmp("stat1", [TILE, 4]), tmp("rstd1", [TILE, 2])
                bn, mv1, mv2 = tmp("bn", [128, 3, 6]), tmp("mv1", [128, 3, 2]), tmp("mv2", [128, 3, 2])
                bn2 = tmp("bn2", [128, 3, 6])
                rstd2 = tmp("rstd2", [128, 3])
                zss, alpha, beta_t = tmp("zss", [128, 3]), tmp("alpha", [128, 3]), tmp("beta_t", [128, 3])
                pw = tmp("pw", [128, 3])
                neg_half, pos_half, neg_one = (tmp(n, [128, 3]) for n in ("neg_half", "pos_half", "neg_one"))
                logit, lexp = tmp("logit", [128, 3, NS]), tmp("lexp", [128, 3, NS])
                lmax, lsum, lrec = tmp("lmax", [128, 3]), tmp("lsum", [128, 3]), tmp("lrec", [128, 3])
                comb = tmp("comb", [NS, T])
                dexp, dmax, dsum, drec = tmp("dexp", [NS, T]), tmp("dmax", [NS, 1]), tmp("dsum", [NS, 1]), tmp("drec", [NS, 1])
                disp = tmp("disp", [128, 3, NS])

                class Signal:

                    def __init__(self, name, per):
                        self.sem, self.per = work.enter_context(nc.semaphore(name)), per

                    def wait(self, engine, batch, k=None, apart=False):
                        k = self.per if k is None else k
                        if isinstance(batch, int):
                            if batch < 0:
                                return
                            if batch >= B:
                                batch, k = B - 1, self.per
                        if apart:
                            engine.wait_ge(prepared, 1)
                        engine.wait_ge(self.sem, batch * self.per + k)

                x_in, txt_in, held, stack_in = Signal("x_in", 160), Signal("txt_in", 16), Signal("held", 16), Signal("stack_in", 16 * 24)
                max_in, h_out, c_out = Signal("max_in", 16), Signal("h_out", 32), Signal("c_out", 16)
                zt_mm, s_mm, embed_mm, l_mm, lt_mm, ct_mm = Signal("zt_mm", 1), Signal("s_mm", NH), Signal("embed_mm", 1), Signal("l_mm", 1), Signal("lt_mm", 1), Signal("ct_mm", 1)
                mt_mm, d_mm, xt_mm, ym_mm, st_mm, pv_mm = Signal("mt_mm", 1), Signal("d_mm", 1), Signal("xt_mm", 1), Signal("ym_mm", 1), Signal("st_mm", NH), Signal("pv_mm", 3)
                yr_mm, qk_mm, yt_mm, v_mm, proj_mm = Signal("yr_mm", 3), Signal("qk_mm", 2), Signal("yt_mm", 1), Signal("v_mm", 1), Signal("proj_mm", 1)
                zt_ready, ce_ready, de_ready, ct_ready, sq_ready, xt_ready = Signal("zt_ready", 1), Signal("ce_ready", 1), Signal("de_ready", 1), Signal("ct_ready", 1), Signal("sq_ready", 1), Signal("xt_ready", 1)
                ym_ready, exp_ready, pv_ready, yt_ready, v_ready, zs_ready = Signal("ym_ready", 1), Signal("exp_ready", NH), Signal("pv_ready", 3), Signal("yt_ready", 1), Signal("v_ready", 1), Signal("zs_ready", 1)
                p1_ready, p2_ready = Signal("p1_ready", 2), Signal("p2_ready", 2)
                max_ready, mpart_ready, mt_ready, l_scaled, lmax_ready, c_ready, dmax_ready = Signal("max_ready", NH), Signal("mpart_ready", 1), Signal("mt_ready", 1), Signal("l_scaled", 1), Signal("lmax_ready", 1), Signal("c_ready", 1), Signal("dmax_ready", 1)
                dn_ready, dp_ready, stat_ready, ln1_ready, xhat_ready = Signal("dn_ready", 1), Signal("dp_ready", 1), Signal("stat_ready", 1), Signal("ln1_ready", 1), Signal("xhat_ready", 1)
                yn_ready, rope_ready, h1_ready, ln2_ready, z_ready = Signal("yn_ready", 3), Signal("rope_ready", 2), Signal("h1_ready", 1), Signal("ln2_ready", 1), Signal("z_ready", 1)
                rot_ready, rest_ready, p3_ready, rstd1_ready, rstd2_ready, beta_ready = Signal("rot_ready", 2), Signal("rest_ready", 2), Signal("p3_ready", 2), Signal("rstd1_ready", 1), Signal("rstd2_ready", 1), Signal("beta_ready", 1)

                prepared, sinks_in = work.enter_context(nc.semaphore("prepared")), work.enter_context(nc.semaphore("sinks_in"))
                with nc.Block() as block:
                    @block.vector
                    def _(dve):
                        for t in (*xw, *kst, *qst, *vaug, xt, yt, *h_new, mv1, mv2, negmax, zss, stat1):
                            dve.memset(t[:], 0.0)
                        dve.memset(neg_half[:], -0.5)
                        dve.memset(pos_half[:], 0.5)
                        dve.memset(neg_one[:], -1.0)
                        for t in (lmax, lsum, mrest, rstd2):
                            dve.memset(t[:], 1.0)
                        dve.drain()
                        for i in range(2):
                            dve.memset(kst[i][SINK_ROW:128, :, 0:KEYS], 1.0)
                            dve.memset(qst[i][SINK_ROW:MAX_ROW], 1.0)
                            dve.memset(vaug[i][:, :, :, HD:HD + 1], 1.0)
                        dve.memset(xt[HALF:HALF + 1, 0, 1:KEYS], 1.0)
                        dve.memset(yt[HALF:HALF + 1, 0], 1.0)
                        dve.memset(y_all[HALF:HALF + 1, 0], 1.0)
                        dve.drain()
                        for i in range(2):
                            last = dve.memset(kst[i][SINK_ROW:MAX_ROW], 0.0)
                        last.then_inc(prepared, 1)

                    @block.sync
                    def _(sp):
                        sp.wait_ge(prepared, 1)
                        for i in range(2):
                            sp.dma_start(kst[i][SINK_ROW:MAX_ROW, :, 0:1], sink_p[:],
                                         allow_slow_non_contiguous=True).then_inc(sinks_in, 16)
                        sp.wait_ge(sinks_in, 32)

                def run(step, engine):
                    for b in range(-3, 3):
                        step(b, b % 2)
                    with engine.Fori(3, B - 4, 2) as b:
                        step(b, 1)
                        step(b + 1, 0)
                    for b in (B - 3, B - 2, B - 1, B):
                        step(b, b % 2)

                def has(batch):
                    return not isinstance(batch, int) or 0 <= batch < B

                block = work.enter_context(nc.Block())

                @block.sync
                def _(sp):
                    def one(t):
                        return t if isinstance(t, slice) else bass.ds(t, 1)

                    def load_image(b, i):
                        embed_mm.wait(sp, b - 2)
                        x_in.wait(sp, b - 1)
                        xb = x[one(b)].rearrange("o c (i r) w -> (o c) r i w", r=PATCH)
                        top = C * PATCH
                        for r0, c0, w0, wn_ in ((0, 1, 0, 216), (ROWS, 0, 8, 216)):
                            for c in range(C):
                                sp.dma_start(xw[i][r0 + PATCH * c:r0 + PATCH * (c + 1), :, c0:c0 + wn_],
                                             xb[c, :, :, w0:w0 + wn_]).then_inc(x_in.sem, 16)
                            sp.dma_start(xw[i][r0 + top:r0 + top + C, 1:GRID, c0:c0 + wn_],
                                         xb[:, PATCH - 1, 0:GRID - 1, w0:w0 + wn_]).then_inc(x_in.sem, 16)
                            sp.dma_start(xw[i][r0 + top + C:r0 + top + 2 * C, 0:GRID - 1, c0:c0 + wn_],
                                         xb[:, 0, 1:GRID, w0:w0 + wn_]).then_inc(x_in.sem, 16)

                    def stack(b, i, p, ready):
                        for slot in range(SLOTS):
                            for side, st, which in ((0, qst[i], Q_PART), (1, kst[i], K_PART)):
                                if which[slot] != p:
                                    continue
                                for e in range(SE):
                                    r = HD * slot + PAIR * e
                                    dst = st[r:r + PAIR] if side == 0 else st[r:r + PAIR, :, 1:KEYS]
                                    sp.dma_start(dst, part[p][:, side, e, :]).then_inc(stack_in.sem, 16)

                    def step(b, i):
                        if has(b + 3):
                            load_image(b + 3, 1 - i)
                        if has(b):
                            xhat_ready.wait(sp, b)
                            h1_ready.wait(sp, b - 1, apart=True)
                            sp.dma_start(h_held[:], h_new[i][:]).then_inc(held.sem, 16)
                            held.wait(sp, b)
                        if has(b + 2):
                            txt_in.wait(sp, b + 1)
                            xhat_ready.wait(sp, b)
                            sp.dma_start(h_new[i][:, 2, :], txt[one(b + 2)].rearrange("o t d -> (o t) d")).then_inc(txt_in.sem, 16)
                        if has(b + 1):
                            stack_in.wait(sp, b)
                            st_mm.wait(sp, b - 1)
                            for p, ready in enumerate((p1_ready, p2_ready, p3_ready)):
                                ready.wait(sp, b + 1)
                                stack(b + 1, 1 - i, p, ready)
                        if has(b):
                            mt_ready.wait(sp, b)
                            max_in.wait(sp, b - 1)
                            st_mm.wait(sp, b - 2)
                            sp.dma_start(qst[i][MAX_ROW:STACK], mt[:]).then_inc(max_in.sem, 16)
                        if has(b - 1):
                            ct_ready.wait(sp, b - 1)
                            c_out.wait(sp, b - 2)
                            sp.dma_start(cscr[one(b - 1)].rearrange("o s t -> (o s) t"), comb[:]).then_inc(c_out.sem, 16)
                        if has(b):
                            h1_ready.wait(sp, b)
                            h_out.wait(sp, b - 1)
                            sp.dma_start(himg[bass.ds(2 * b, 2)].rearrange("k p d -> p k d"), h1[0:TILE, 0:2]).then_inc(h_out.sem, 16)
                            sp.dma_start(htxt[one(b)].rearrange("o p d -> (o p) d"), h1[:, 2]).then_inc(h_out.sem, 16)

                    run(step, sp)
                    c_out.wait(sp, B - 1)
                    h_out.wait(sp, B - 1)

                @block.tensor
                def _(pe):
                    def embed(b, i, n):
                        if n == 0:
                            x_in.wait(pe, b)
                            sq_ready.wait(pe, b)
                            zt_ready.wait(pe, b - 3)
                            h1_ready.wait(pe, b - 3)
                        kind, half, q = n // 18, n // 9 % 2, n % 9
                        lo = TILE * PATCH * half + q
                        src = xsq if kind else xw_flat[i]
                        dst = ps[0:TILE, BK7, 2 * (D + 1) + half:2 * (D + 1) + half + 1] if kind else \
                            ps[0:TILE, BK7, half * (D + 1):(half + 1) * (D + 1)]
                        mm = pe.matmul(dst, src[:, lo:lo + PATCH * (TILE - 1) + 1:PATCH],
                                       window_w[:, q, D:D + 1] if kind else window_w[:, q, :],
                                       start=(q == 0), stop=(q == WIN2 - 1))
                        if n == 35:
                            mm.then_inc(embed_mm.sem, 1)

                    def scores(b, i, h):
                        bank = SC + 2 * (h % 2)
                        if h == 0:
                            stack_in.wait(pe, b)
                        if h < 2:
                            rope_ready.wait(pe, b + 1, h + 1)
                        else:
                            max_ready.wait(pe, b, h - 1)
                        for q, bk, col in ((2, bank, 0), (0, bank + 1, 0), (1, bank + 1, QTILES[0][1] + 1)):
                            q0, nq = QTILES[q]
                            keys = q0 + nq + 1
                            pe.matmul(ps[0:nq, bk, col:col + keys], qst[i][0:MAX_ROW, h, q0:q0 + nq],
                                      kst[i][0:MAX_ROW, h, 0:keys], start=True, stop=False)
                            mm = pe.matmul(ps[0:nq, bk, col + q0 + 1:col + keys], ident_b[:, 0:nq], causal[:, 0:nq],
                                           start=False, stop=True)
                        mm.then_inc(s_mm.sem, 1)

                    def scores_t(b, i, h):
                        bank = SC + 2 * (h % 2)
                        if h == 0:
                            max_in.wait(pe, b)
                        if h < 2:
                            max_ready.wait(pe, b, NH - 1 + h)
                        else:
                            exp_ready.wait(pe, b, h - 1)
                        k0, k1, k2 = (kst[i][0:STACK, h, 128 * k:128 * (k + 1)] for k in range(3))
                        q = qst[i][0:STACK, h]
                        n0 = T - EXPC
                        c1, c2 = n0, n0 + T - KTILES[1][2]
                        pe.matmul(ps[:, bank, 0:EXPC], k0, q[:, 0:EXPC], start=True, stop=False)
                        pe.matmul(ps[:, bank, 0:127], causal[:], ident_b[:, 1:128], start=False, stop=True)
                        pe.matmul(ps[:, bank + 1, 0:n0], k0, q[:, EXPC:T], start=True, stop=True)
                        pe.matmul(ps[:, bank + 1, c1:c2], k1, q[:, KTILES[1][2]:T], start=True, stop=False)
                        pe.matmul(ps[:, bank + 1, c1:c1 + 128], causal[:], ident_b[:], start=False, stop=True)
                        pe.matmul(ps[:, bank + 1, c2:EXPC], k2, q[:, KTILES[2][2]:T], start=True, stop=False)
                        pe.matmul(ps[:, bank + 1, c2:EXPC], causal[:], ident_b[:, 0:EXPC - c2], start=False,
                                  stop=True).then_inc(st_mm.sem, 1)

                    def values(b, i, g):
                        exp_ready.wait(pe, b, 4 * g + 4)
                        if g == 0:
                            v_ready.wait(pe, b)
                            dp_ready.wait(pe, b - 1)
                            de_ready.wait(pe, b - 1)
                        else:
                            pv_ready.wait(pe, b, g)
                        col = 0
                        for k, (_, nk, q0) in enumerate(KTILES):
                            for s in range(4):
                                h = 4 * g + s
                                mm = pe.matmul(ps[STRIP * s:STRIP * (s + 1), BK6, q0:T], vaug[i][0:nk, k, h, :],
                                               prob[0:nk, h % 8, col:col + T - q0], start=(k == 0), stop=(k == 2),
                                               skip_group_check=True)
                            col += T - q0
                        mm.then_inc(pv_mm.sem, 1)

                    def turn(dst_banks, src, n_src=None):
                        for c in range(2):
                            for t, (t0, nt) in enumerate(TTILES):
                                mm = pe.transpose(ps[0:HALF, dst_banks[c], t0:t0 + nt],
                                                  src[0:nt, t, HALF * c:HALF * (c + 1)], ident[0:nt, 0:nt])
                        return mm

                    def step(b, i):
                        j = 1 - i
                        moe, att, front = has(b - 1), has(b), has(b + 2)
                        if moe:
                            z_ready.wait(pe, b - 1)
                            turn((BK5, BK7), z).then_inc(zt_mm.sem, 1)
                        todo = list(range(36)) if front else []
                        for h in range(NH):
                            if att:
                                scores(b, i, h)
                            if h >= 2:
                                for n in todo[:4]:
                                    embed(b + 2, i, n)
                                todo = todo[4:]
                            if moe and h == 3:
                                zt_ready.wait(pe, b - 1)
                                for t, (t0, nt) in enumerate(TTILES):
                                    for c in range(2):
                                        mm = pe.matmul(ps[0:nt, BK5, NS * t:NS * (t + 1)], zt[:, c, t0:t0 + nt],
                                                       slots_t[:, c, :], start=(c == 0), stop=(c == 1))
                                mm.then_inc(l_mm.sem, 1)
                            if moe and h == 6:
                                v_ready.wait(pe, b + 1, apart=True)
                                l_scaled.wait(pe, b - 1)
                                for t, (t0, nt) in enumerate(TTILES):
                                    mm = pe.transpose(ps[0:NS, BK6, t0:t0 + nt], logit[0:nt, t, :], ident[0:nt, 0:nt])
                                mm.then_inc(lt_mm.sem, 1)
                            if moe and h == 9:
                                c_ready.wait(pe, b - 1, apart=True)
                                for t, (t0, nt) in enumerate(TTILES):
                                    mm = pe.transpose(ps[0:NS, BK4, t0:t0 + nt], lexp[0:nt, t, :], ident[0:nt, 0:nt])
                                mm.then_inc(ct_mm.sem, 1)
                        if att:
                            mpart_ready.wait(pe, b, apart=True)
                            for q, (q0, nq) in enumerate(QTILES):
                                mm = pe.transpose(ps[0:PARTS * NH, BK5, :].bitcast(BF16)[:, q0:q0 + nq],
                                                  mpart[0:nq, q].rearrange("p a h -> p (a h)"), ident_b[0:nq, 0:nq])
                            mm.then_inc(mt_mm.sem, 1)
                        if moe:
                            dn_ready.wait(pe, b - 1, apart=True)
                            for t, (t0, nt) in enumerate(TTILES):
                                mm = pe.transpose(ps[0:nt, BK6, NS * t:NS * (t + 1)], dexp[:, t0:t0 + nt],
                                                  ident[0:NS, 0:NS])
                            mm.then_inc(d_mm.sem, 1)
                        if front:
                            xhat_ready.wait(pe, b + 2)
                            ct_ready.wait(pe, b - 1)
                            v_ready.wait(pe, b + 1)
                            turn((BK4, BK7), xhat).then_inc(xt_mm.sem, 1)
                        if moe:
                            dp_ready.wait(pe, b - 1)
                            mt_ready.wait(pe, b)
                            for c in range(2):
                                for t, (t0, nt) in enumerate(TTILES):
                                    mm = pe.matmul(ps[0:HALF, BK5, NS * c:NS * (c + 1)],
                                                   z[0:nt, t, HALF * c:HALF * (c + 1)], disp[0:nt, t, :],
                                                   start=(t == 0), stop=(t == 2))
                            mm.then_inc(ym_mm.sem, 1)
                        if att:
                            for h in range(NH):
                                scores_t(b, i, h)
                                if h in (5, 9):
                                    values(b, i, h // 4 - 1)
                            values(b, i, 2)
                            pv_ready.wait(pe, b)
                            for t, (t0, nt) in enumerate(TTILES):
                                if t == 0:
                                    xt_ready.wait(pe, b + 2)
                                    ym_ready.wait(pe, b - 1)
                                    ct_ready.wait(pe, b - 1)
                                for g in range(3):
                                    mm = pe.transpose(ps[0:nt, (BK4, BK5, BK7)[t], 128 * g:128 * (g + 1)],
                                                      yraw[:, g, t0:t0 + nt], ident[:])
                                mm.then_inc(yr_mm.sem, 1)
                        for side in range(2):
                            if front:
                                if side == 0:
                                    xt_ready.wait(pe, b + 2)
                                exp_ready.wait(pe, b, NH - 1 + side)
                                for e in range(SE):
                                    for c in range(2):
                                        k = HALF + 1 - c
                                        mm = pe.matmul(ps[0:HALF, SC + 2 * side + e, 0:T], wqk[0:k, c, 2 * side + e, :],
                                                       xt[0:k, c, 1:KEYS], start=(c == 0), stop=(c == 1))
                                mm.then_inc(qk_mm.sem, 1)
                            if att and side == 0:
                                yn_ready.wait(pe, b)
                                turn((BK6, BK4), ynorm).then_inc(yt_mm.sem, 1)
                        if front:
                            yt_ready.wait(pe, b)
                            for t, (k0, nk, _) in enumerate(KTILES):
                                for c in range(2):
                                    k = HALF + 1 - c
                                    mm = pe.matmul(ps[0:nk, (BK6, BK6, BK4)[t], D * (t % 2):D * (t % 2) + D],
                                                   xt[0:k, c, k0:k0 + nk], wv[0:k, c, :], start=(c == 0), stop=(c == 1))
                            mm.then_inc(v_mm.sem, 1)
                        if att:
                            yt_ready.wait(pe, b)
                            for t, (t0, nt) in enumerate(TTILES):
                                for c in range(2):
                                    k = HALF + 1 - c
                                    mm = pe.matmul(ps[0:nt, (BK5, BK5, BK7)[t], D * (t % 2):D * (t % 2) + D],
                                                   yt[0:k, c, t0:t0 + nt], wp[0:k, c, :], start=(c == 0), stop=(c == 1))
                            mm.then_inc(proj_mm.sem, 1)

                    run(step, pe)

                @block.scalar
                def _(act):
                    def fn(out_, in_, f, **kw):
                        return nc.scalar.activation(out_, in_, f, **kw)

                    def split(b, which, done):
                        src, dst, need = ((rot, part[0], rot_ready), (rest, part[1], rest_ready))[which]
                        for side in range(2):
                            need.wait(act, b, side + 1)
                            if side == 0:
                                stack_in.wait(act, b - 1)
                            fn(dst[:, side], src[:, side], ACT.Copy).then_inc(done.sem, 1)

                    def step(b, i):
                        moe, att, front, mid = has(b - 1), has(b), has(b + 2), has(b + 1)
                        if moe:
                            zt_mm.wait(act, b - 1)
                            fn(zt[:, 0], ps[0:HALF, BK5, 0:T], ACT.Copy)
                            fn(zt[:, 1], ps[0:HALF, BK7, 0:T], ACT.Copy).then_inc(zt_ready.sem, 1)
                        if mid:
                            split(b + 1, 0, p1_ready)
                        if moe:
                            lmax_ready.wait(act, b - 1)
                            for t, (_, nt) in enumerate(TTILES):
                                last = fn(lexp[0:nt, t, :], logit[0:nt, t, :], ACT.Exp, bias=lmax[0:nt, t:t + 1],
                                          accum_out=lsum[0:nt, t:t + 1])
                            last.then_inc(ce_ready.sem, 1)
                        if mid:
                            split(b + 1, 1, p2_ready)
                        if moe:
                            dmax_ready.wait(act, b - 1)
                            fn(dexp[:], ps[0:NS, BK6, 0:T], ACT.Exp, bias=dmax[:, 0:1],
                               accum_out=dsum[:, 0:1]).then_inc(de_ready.sem, 1)
                            ct_mm.wait(act, b - 1)
                            c_out.wait(act, b - 2)
                            fn(comb[:], ps[0:NS, BK4, 0:T], ACT.Copy).then_inc(ct_ready.sem, 1)
                        if has(b + 3):
                            x_in.wait(act, b + 3)
                            embed_mm.wait(act, b + 2)
                            fn(xsq[:], xw_flat[1 - i], ACT.Square).then_inc(sq_ready.sem, 1)
                        if front:
                            xt_mm.wait(act, b + 2)
                            v_mm.wait(act, b + 1)
                            fn(xt[0:HALF, 0, 1:KEYS], ps[0:HALF, BK4, 0:T], ACT.Copy)
                            fn(xt[0:HALF, 1, 1:KEYS], ps[0:HALF, BK7, 0:T], ACT.Copy).then_inc(xt_ready.sem, 1)
                        if moe:
                            ym_mm.wait(act, b - 1)
                            fn(y_all[0:HALF, :, :, bass.ds(b - 1, 1)],
                               ps[0:HALF, BK5, 0:2 * NS].rearrange("p (c s o) -> p c s o", c=2, o=1), ACT.Copy).then_inc(ym_ready.sem, 1)
                        if att:
                            for h in range(NH):
                                st_mm.wait(act, b, h + 1)
                                if h >= 8:
                                    pv_mm.wait(act, b, 1)
                                elif h % 4 == 0:
                                    pv_mm.wait(act, b - 1)
                                fn(prob[:, h % 8, :].rearrange("p (a q) -> p a q", a=2),
                                   ps[:, SC + 2 * (h % 2):SC + 2 * (h % 2) + 2, 0:EXPC], ACT.Exp).then_inc(exp_ready.sem, 1)
                                if h in (6, 10):
                                    heads_out(b, h // 4 - 1)
                            heads_out(b, 2)
                            yt_mm.wait(act, b)
                            fn(yt[0:HALF, 0], ps[0:HALF, BK6, 0:T], ACT.Copy)
                            fn(yt[0:HALF, 1], ps[0:HALF, BK4, 0:T], ACT.Copy).then_inc(yt_ready.sem, 1)
                        if front:
                            v_mm.wait(act, b + 2)
                            fn(vaug[i][:, 0:2, :, 0:HD], ps[:, BK6, 0:2 * D].rearrange("p (k h d) -> p k h d", k=2, h=NH),
                               ACT.Copy)
                            nk = KTILES[2][1]
                            fn(vaug[i][0:nk, 2, :, 0:HD], ps[0:nk, BK4, 0:D].rearrange("p (h d) -> p h d", h=NH),
                               ACT.Copy).then_inc(v_ready.sem, 1)
                        if att:
                            z_ready.wait(act, b, apart=True)
                            beta_ready.wait(act, b - 1)
                            for t, (_, nt) in enumerate(TTILES):
                                act.drain()
                                last = fn(lexp[0:nt].rearrange("p t s -> p (t s)"), z[0:nt, t, :], ACT.Square, accum_out=zss[0:nt, t:t + 1])
                            last.then_inc(zs_ready.sem, 1)

                    def heads_out(b, g):
                        pv_mm.wait(act, b, g + 1)
                        if g == 0:
                            yr_mm.wait(act, b - 1)
                        fn(yraw[:, g, :], ps[:, BK6, 0:T], ACT.Copy).then_inc(pv_ready.sem, 1)

                    run(step, act)

                @block.vector
                def _(dve):
                    def over(tile):
                        return [tile[0:n, a:z_] for n, a, z_ in GROUPS]

                    def norm_stats(src, bnt, mv):
                        for t, (_, nt) in enumerate(TTILES):
                            dve.bn_stats(bnt[0:nt, t, :], src[0:nt, t, :])
                        dve.drain()
                        for t, (_, nt) in enumerate(TTILES):
                            last = dve.bn_aggr(mv[0:nt, t, :], bnt[0:nt, t, :])
                        return last

                    def step(b, i):
                        moe, att, front = has(b - 1), has(b), has(b + 2)
                        for h in range(NH):
                            if att:
                                bank = SC + 2 * (h % 2)
                                s_mm.wait(dve, b, h + 1)
                                for q, bk, col in ((2, bank, 0), (0, bank + 1, 0), (1, bank + 1, QTILES[0][1] + 1)):
                                    q0, nq = QTILES[q]
                                    last = dve.tensor_reduce(negmax[0:nq, q, h:h + 1], ps[0:nq, bk, col:col + q0 + nq + 1],
                                                             AX.X, ALU.max, negate=True)
                                last.then_inc(max_ready.sem, 1)
                            if moe and h == 4:
                                l_mm.wait(dve, b - 1)
                                beta_ready.wait(dve, b - 1)
                                for n, t0, t1 in GROUPS:
                                    last = dve.tensor_tensor(logit[0:n, t0:t1], ps[0:n, BK5, NS * t0:NS * t1].rearrange(
                                        "p (t s) -> p t s", s=NS), beta_t[0:n, t0:t1].unsqueeze(2).broadcast_to(
                                        (n, t1 - t0, NS)), ALU.mult)
                                last.then_inc(l_scaled.sem, 1)
                                dve.drain()
                                for n, t0, t1 in GROUPS:
                                    last = dve.tensor_reduce(lmax[0:n, t0:t1], logit[0:n, t0:t1], AX.X, ALU.max, negate=True)
                                last.then_inc(lmax_ready.sem, 1)
                            if moe and h == 7:
                                ce_ready.wait(dve, b - 1)
                                dve.reciprocal(lrec[:], lsum[:])
                                lt_mm.wait(dve, b - 1)
                                dve.tensor_reduce(dmax[:], ps[0:NS, BK6, 0:T], AX.X, ALU.max, negate=True).then_inc(dmax_ready.sem, 1)
                                dve.drain()
                                for n, t0, t1 in GROUPS:
                                    last = dve.tensor_tensor(lexp[0:n, t0:t1], lexp[0:n, t0:t1], lrec[0:n, t0:t1].unsqueeze(
                                        2).broadcast_to((n, t1 - t0, NS)), ALU.mult)
                                last.then_inc(c_ready.sem, 1)
                        if att:
                            mt_mm.wait(dve, b - 1, apart=True)
                            dve.drain()
                            dve.tensor_copy(mpart[:, :, 0], negmax[:])
                            dve.drain()
                            dve.tensor_tensor(mrest[:], negmax[:], mpart[:, :, 0], ALU.subtract)
                            dve.drain()
                            dve.tensor_copy(mpart[:, :, 1], mrest[:])
                            dve.drain()
                            dve.tensor_tensor(mpart[:, :, 2], mrest[:], mpart[:, :, 1], ALU.subtract).then_inc(mpart_ready.sem, 1)
                        if front:
                            embed_mm.wait(dve, b + 2)
                            rstd1_ready.wait(dve, b + 1)
                            dve.tensor_copy(stat1[:, 0:2], ps[0:TILE, BK7, 0:2 * (D + 1)].rearrange(
                                "p (k d) -> p k d", k=2)[:, :, D])
                            dve.tensor_copy(stat1[:, 2:4], ps[0:TILE, BK7, 2 * (D + 1):2 * (D + 1) + 2]).then_inc(stat_ready.sem, 1)
                        if moe:
                            de_ready.wait(dve, b - 1)
                            dve.reciprocal(drec[:], dsum[:])
                            dve.drain()
                            dve.tensor_scalar(dexp[:], dexp[:], drec[:, 0:1], None, ALU.mult).then_inc(dn_ready.sem, 1)
                        if att:
                            mt_mm.wait(dve, b)
                            max_in.wait(dve, b - 1)
                            dve.tensor_copy(mt[:], ps[0:PARTS * NH, BK5, :].bitcast(BF16)[:, 0:T]).then_inc(mt_ready.sem, 1)
                        if front:
                            rstd1_ready.wait(dve, b + 2)
                            held.wait(dve, b)
                            for t in range(2):
                                dve.scalar_tensor_tensor(out=h_new[i][0:TILE, t], in0=ps[0:TILE, BK7, (D + 1) * t:(D + 1) * t + D],
                                                         scalar=rstd1[:, t:t + 1], in1=hb[0:TILE], op0=ALU.mult, op1=ALU.add)
                            dve.drain()
                            txt_in.wait(dve, b + 2)
                            rstd2_ready.wait(dve, b + 1)
                            norm_stats(h_new[i], bn, mv1).then_inc(ln1_ready.sem, 1)
                        if moe:
                            d_mm.wait(dve, b - 1)
                            for n, t0, t1 in GROUPS:
                                last = dve.tensor_tensor(disp[0:n, t0:t1], ps[0:n, BK6, NS * t0:NS * t1].rearrange(
                                    "p (t s) -> p t s", s=NS), alpha[0:n, t0:t1].unsqueeze(2).broadcast_to(
                                    (n, t1 - t0, NS)), ALU.mult)
                            last.then_inc(dp_ready.sem, 1)
                        if front:
                            rstd2_ready.wait(dve, b + 2)
                            xt_mm.wait(dve, b + 1)
                            for t, (_, nt) in enumerate(TTILES):
                                last = dve.tensor_scalar(xhat[0:nt, t], h_new[i][0:nt, t], mv1[0:nt, t, 0:1],
                                                         rstd2[0:nt, t:t + 1], ALU.subtract, ALU.mult)
                            last.then_inc(xhat_ready.sem, 1)
                        if att:
                            for t, (_, nt) in enumerate(TTILES):
                                heads = ps[0:nt, (BK4, BK5, BK7)[t], 0:3 * 128].rearrange("p (h e) -> p h e", h=NH)
                                yr_mm.wait(dve, b, t + 1)
                                dve.reciprocal(rden[0:nt, t], heads[:, :, HD])
                                dve.drain()
                                dve.tensor_tensor(ynorm[0:nt, t].rearrange("p (h e) -> p h e", h=NH), heads[:, :, 0:HD],
                                                  rden[0:nt, t].unsqueeze(2).broadcast_to((nt, NH, HD)), ALU.mult
                                                  ).then_inc(yn_ready.sem, 1)
                        if front:
                            for side in range(2):
                                qk_mm.wait(dve, b + 2, side + 1)
                                if side == 0:
                                    rot_ready.wait(dve, b + 1)
                                    p3_ready.wait(dve, b + 1)
                                for table, dst in ((cos_t, by_cos), (sin_t, by_sin)):
                                    last = dve.tensor_tensor(dst[:, side], ps[0:HALF, SC + 2 * side:SC + 2 * side + 2, 0:T],
                                                             table[:].unsqueeze(1).broadcast_to((HALF, SE, T)), ALU.mult)
                                last.then_inc(rope_ready.sem, 1)
                        if att:
                            proj_mm.wait(dve, b)
                            held.wait(dve, b)
                            h_out.wait(dve, b - 1)
                            dve.tensor_tensor(h1[0:TILE, 0:2], ps[0:TILE, BK5, 0:2 * D].rearrange("p (t d) -> p t d", t=2),
                                              h_held[0:TILE, 0:2], ALU.add)
                            dve.tensor_tensor(h1[:, 2], ps[:, BK7, 0:D], h_held[:, 2], ALU.add).then_inc(h1_ready.sem, 1)
                            beta_ready.wait(dve, b - 1, apart=True)
                            dve.drain()
                            norm_stats(h1, bn2, mv2).then_inc(ln2_ready.sem, 1)
                            dve.drain()
                            ym_mm.wait(dve, b - 1)
                            zs_ready.wait(dve, b - 1)
                            for t, (_, nt) in enumerate(TTILES):
                                last = dve.scalar_tensor_tensor(out=z[0:nt, t], in0=h1[0:nt, t], scalar=mv2[0:nt, t, 0:1],
                                                                in1=nwb[0:nt], op0=ALU.subtract, op1=ALU.mult)
                            last.then_inc(z_ready.sem, 1)

                    run(step, dve)

                @block.gpsimd
                def _(pool):
                    def power(dst, src, e):
                        pool.drain()
                        return pool.tensor_tensor(dst, src, e, ALU.pow)

                    def step(b, i):
                        moe, att, front, mid = has(b - 1), has(b), has(b + 2), has(b + 1)
                        if mid:
                            for side in range(2):
                                p1_ready.wait(pool, b + 1, side + 1)
                                pool.tensor_tensor(rest[:, side], rot[:, side], part[0][:, side], ALU.subtract
                                                   ).then_inc(rest_ready.sem, 1)
                            stack_in.wait(pool, b)
                            for side in range(2):
                                p2_ready.wait(pool, b + 1, side + 1)
                                pool.tensor_tensor(part[2][:, side], rest[:, side], part[1][:, side], ALU.subtract
                                                   ).then_inc(p3_ready.sem, 1)
                        if front:
                            stat_ready.wait(pool, b + 2)
                            pool.tensor_tensor(rstd1[:], stat1[:, 0:2], stat1[:, 0:2], ALU.mult)
                            pool.drain()
                            pool.tensor_tensor(rstd1[:], stat1[:, 2:4], rstd1[:], ALU.subtract)
                            pool.drain()
                            pool.tensor_scalar(rstd1[:], rstd1[:], 0.0, EPS, ALU.max, ALU.add)
                            power(rstd1[:], rstd1[:], neg_half[0:TILE, 0:2]).then_inc(rstd1_ready.sem, 1)
                            ln1_ready.wait(pool, b + 2, apart=True)
                            pool.tensor_scalar(rstd2[:], mv1[:, :, 1], EPS, 1.0, ALU.add, ALU.mult)
                            power(rstd2[:], rstd2[:], neg_half[:]).then_inc(rstd2_ready.sem, 1)
                            for side in range(2):
                                rope_ready.wait(pool, b + 2, side + 1)
                                pool.tensor_tensor(rot[:, side, 0], by_cos[:, side, 0], by_sin[:, side, 1], ALU.subtract)
                                pool.tensor_tensor(rot[:, side, 1], by_sin[:, side, 0], by_cos[:, side, 1], ALU.add
                                                   ).then_inc(rot_ready.sem, 1)
                        if att:
                            ln2_ready.wait(pool, b, apart=True)
                            dp_ready.wait(pool, b - 1)
                            var = mv2[:, :, 1]
                            pool.tensor_scalar(alpha[:], var, EPS, 1.0, ALU.add, ALU.mult)
                            power(alpha[:], alpha[:], neg_half[:])
                            pool.drain()
                            pool.tensor_tensor(pw[:], alpha[:], alpha[:], ALU.mult)
                            pool.drain()
                            pool.tensor_tensor(pw[:], var, pw[:], ALU.mult)
                            pool.drain()
                            pool.tensor_scalar(pw[:], pw[:], EPS, 1.0, ALU.add, ALU.mult)
                            power(pw[:], pw[:], neg_half[:])
                            pool.drain()
                            pool.tensor_tensor(alpha[:], alpha[:], pw[:], ALU.mult)
                            zs_ready.wait(pool, b, apart=True)
                            power(pw[:], zss[:], pos_half[:])
                            pool.drain()
                            pool.tensor_tensor(pw[:], pw[:], alpha[:], ALU.mult)
                            pool.drain()
                            pool.tensor_scalar(pw[:], pw[:], 1e-5, 0.0, ALU.max, ALU.add)
                            power(pw[:], pw[:], neg_one[:])
                            pool.drain()
                            pool.tensor_tensor(beta_t[:], pw[:], alpha[:], ALU.mult).then_inc(beta_ready.sem, 1)

                    run(step, pool)

        with ExitStack() as work:
            RING = 4
            w1 = [work.enter_context(nc.sbuf_tensor(f"w1_{i}", [HALF + 1, 2, F], F32)) for i in range(RING)]
            w2 = [work.enter_context(nc.sbuf_tensor(f"w2_{i}", [128, FC, D], F32)) for i in range(RING)]
            act_t = [work.enter_context(nc.sbuf_tensor(f"act_t{i}", [128, FC, B], F32)) for i in range(RING)]
            pair_out = [work.enter_context(nc.sbuf_tensor(f"pair_out{i}", [2 * B, D], F32)) for i in range(2)]
            w_in = [work.enter_context(nc.semaphore(f"w_in{i}")) for i in range(RING)]
            o_out = [work.enter_context(nc.semaphore(f"o_out{i}")) for i in range(2)]
            up_mm, gelu_ready, down_mm, pair_ready = (work.enter_context(nc.semaphore(n)) for n in
                                                      ("up_mm", "gelu_ready", "down_mm", "pair_ready"))
            block = work.enter_context(nc.Block())

            def one(s):
                return bass.ds(s, 1)

            def turns(engine, turn):
                turn(0, True)
                with engine.Fori(RING, NS - RING + 1, RING) as s:
                    turn(s, False)

            @block.sync
            def _(sp):
                def load(s, k):
                    sp.dma_start(w1[k][0:HALF], fc1[one(s)].rearrange("o (c p) f -> p (o c) f", c=2)).then_inc(w_in[k], 16)
                    sp.dma_start(w1[k][HALF:HALF + 1, 0, :], b1[one(s)]).then_inc(w_in[k], 16)
                    sp.dma_start(w2[k][:], fc2[one(s)].rearrange("o (c p) d -> p (o c) d", c=FC)).then_inc(w_in[k], 16)

                for k in range(RING):
                    load(k, k)
                with sp.Fori(0, NS - 2 * RING + 1, RING) as s:
                    for k in range(RING):
                        if k % 2 == 0:
                            sp.wait_ge(down_mm, s // 2 + k // 2 + 1)
                        load(s + RING + k, k)

            @block.tensor
            def _(pe):
                def turn(s, first):
                    for k in range(RING):
                        pe.wait_ge(w_in[k], 12 * s + 48)
                        if k == 0 and not first:
                            pe.wait_ge(gelu_ready, s)
                        for f in range(FC):
                            for c in range(2):
                                kk = HALF + 1 - c
                                mm = pe.matmul(ps[:, k, B * f:B * (f + 1)], w1[k][0:kk, c, 128 * f:128 * (f + 1)],
                                               y_all[0:kk, c, one(s + k), :].rearrange("p o b -> p (o b)"),
                                               start=(c == 0), stop=(c == 1))
                        mm.then_inc(up_mm, 1)
                        if k % 2 == 1:
                            pe.wait_ge(gelu_ready, s + k + 1)
                            pair = k // 2
                            if not first:
                                pe.wait_ge(pair_ready, s // 2 + pair)
                            for f in range(FC):
                                for j in range(2):
                                    mm = pe.matmul(ps[B * j:B * (j + 1), 4 + pair, 0:D], act_t[k - 1 + j][:, f, :],
                                                   w2[k - 1 + j][:, f, :], start=(f == 0), stop=(f == FC - 1),
                                                   skip_group_check=True)
                            mm.then_inc(down_mm, 1)

                turns(pe, turn)

            @block.scalar
            def _(act):
                def turn(s, first):
                    for k in range(RING):
                        act.wait_ge(up_mm, s + k + 1)
                        if k % 2 == 0 and not first:
                            act.wait_ge(down_mm, (s + k - 2) // 2)
                        nc.scalar.activation(act_t[k][:].rearrange("p f b -> p (f b)"), ps[:, k, 0:FC * B], ACT.Gelu
                                             ).then_inc(gelu_ready, 1)

                turns(act, turn)

            @block.vector
            def _(dve):
                def turn(s, first):
                    for pair in range(2):
                        dve.wait_ge(down_mm, s // 2 + pair + 1)
                        if not first:
                            dve.wait_ge(o_out[pair], 8 * s)
                        dve.tensor_copy(pair_out[pair][:], ps[:, 4 + pair, 0:D]).then_inc(pair_ready, 1)

                turns(dve, turn)

            @block.gpsimd
            def _(pool):
                def turn(s, first):
                    for pair in range(2):
                        pool.wait_ge(pair_ready, s // 2 + pair + 1)
                        for j in range(2):
                            pool.dma_start(oscr[:, one(s + 2 * pair + j), :].rearrange("b o d -> b (o d)"),
                                           pair_out[pair][B * j:B * (j + 1)]).then_inc(o_out[pair], 16)

                turns(pool, turn)
                for pair in range(2):
                    pool.wait_ge(o_out[pair], 8 * NS)

        with ExitStack() as work:
            N4 = 4
            h_i = [work.enter_context(nc.sbuf_tensor(f"h_i{i}", [TILE, 2 * N4, D], F32)) for i in range(2)]
            h_t = [work.enter_context(nc.sbuf_tensor(f"h_t{i}", [TXT, N4, D], F32)) for i in range(2)]
            cw = [work.enter_context(nc.sbuf_tensor(f"cw{i}", [NS, N4, T], F32)) for i in range(2)]
            ow = [work.enter_context(nc.sbuf_tensor(f"ow{i}", [NS, N4, D], F32)) for i in range(2)]
            b2_t = work.enter_context(nc.sbuf_tensor("b2_t", [NS, D], F32))
            in_sem = [work.enter_context(nc.semaphore(f"group_in{i}")) for i in range(2)]
            out_sem = [work.enter_context(nc.semaphore(f"group_out{i}")) for i in range(2)]
            b2_in, biased, mix_mm, summed = (work.enter_context(nc.semaphore(n)) for n in
                                             ("b2_in", "biased", "mix_mm", "summed"))
            block = work.enter_context(nc.Block())

            @block.sync
            def _(sp):
                sp.dma_start(b2_t[:], b2).then_inc(b2_in, 16)

                def load(b, k):
                    sp.dma_start(h_i[k][:], himg[bass.ds(2 * b, 2 * N4)].rearrange("k p d -> p k d")).then_inc(in_sem[k], 16)
                    sp.dma_start(h_t[k][:], htxt[bass.ds(b, N4)].rearrange("k p d -> p k d")).then_inc(in_sem[k], 16)
                    sp.dma_start(cw[k][:], cscr[bass.ds(b, N4)].rearrange("k s t -> s k t")).then_inc(in_sem[k], 16)
                    sp.dma_start(ow[k][:], oscr[bass.ds(b, N4)].rearrange("k s d -> s k d")).then_inc(in_sem[k], 16)

                load(0, 0)
                load(N4, 1)
                with sp.Fori(2 * N4, B - 2 * N4 + 1, 2 * N4) as b:
                    for k in range(2):
                        sp.wait_ge(out_sem[k], 10 * b)
                        load(b + N4 * k, k)

            @block.vector
            def _(dve):
                dve.wait_ge(b2_in, 16)
                with dve.Fori(0, B - 2 * N4 + 1, 2 * N4) as b:
                    for k in range(2):
                        dve.wait_ge(in_sem[k], 8 * b + 64)
                        dve.tensor_tensor(ow[k][:], ow[k][:], b2_t[:].unsqueeze(1).broadcast_to((NS, N4, D)), ALU.add
                                          ).then_inc(biased, 1)
                        for n in range(N4):
                            dve.wait_ge(mix_mm, b + N4 * k + n + 1)
                            bk = 2 * (n % 2)
                            dve.tensor_tensor(h_i[k][:, 2 * n:2 * n + 2], ps[0:TILE, bk, 0:2 * D].rearrange(
                                "p (t d) -> p t d", t=2), h_i[k][:, 2 * n:2 * n + 2], ALU.add)
                            dve.tensor_tensor(h_t[k][:, n], ps[:, bk + 1, 0:D], h_t[k][:, n], ALU.add).then_inc(summed, 1)

            @block.tensor
            def _(pe):
                def groups(b, first):
                    for k in range(2):
                        pe.wait_ge(biased, b // N4 + k + 1)
                        for n in range(N4):
                            if not (first and k == 0 and n < 2):
                                pe.wait_ge(summed, b + N4 * k + n - 1)
                            bk = 2 * (n % 2)
                            for t, (t0, nt) in enumerate(TTILES):
                                mm = pe.matmul(ps[0:nt, bk + t // 2, D * (t % 2):D * (t % 2) + D],
                                               cw[k][:, n, t0:t0 + nt], ow[k][:, n, :], start=True, stop=True)
                            mm.then_inc(mix_mm, 1)

                groups(0, True)
                with pe.Fori(2 * N4, B - 2 * N4 + 1, 2 * N4) as b:
                    groups(b, False)

            @block.scalar
            def _(act):
                with act.Fori(0, B - 2 * N4 + 1, 2 * N4) as b:
                    for k in range(2):
                        act.wait_ge(summed, b + N4 * (k + 1))
                        act.dma_start(out[bass.ds(b + N4 * k, N4), PATCHES:T].rearrange("k p d -> p k d"), h_t[k][:]
                                      ).then_inc(out_sem[k], 16)
                        for n in range(N4):
                            act.dma_start(out[bass.ds(b + N4 * k + n, 1), 0:PATCHES].rearrange(
                                "o (t p) d -> p (o t) d", t=2), h_i[k][:, 2 * n:2 * n + 2]).then_inc(out_sem[k], 16)
                for k in range(2):
                    act.wait_ge(out_sem[k], 10 * B)


_INS = ['x', 'txt', 'L0_tok_ln_gamma', 'L0_tok_ln_beta', 'L0_tok_W', 'L0_tok_b', 'L0_attn_norm_scale',
        'L0_attn_norm_bias', 'L0_attn_W_attn', 'L0_attn_b_attn', 'L0_attn_W_proj', 'L0_attn_b_proj', 'L0_attn_sinks',
        'L0_attn_rezero', 'L0_ffn_slots', 'L0_ffn_scale', 'L0_ffn_fc1_weight', 'L0_ffn_fc1_bias', 'L0_ffn_fc2_weight',
        'L0_ffn_fc2_bias', 'L0_ffn_norm_weight']


def _constants():
    import numpy as np

    half = np.arange(PAIR, dtype=np.float32) * 2 / np.float32(HD)
    freqs = (np.float32(1.0) / np.power(np.float32(10000.0), half)).astype(np.float32)
    angle = (np.arange(T, dtype=np.float32)[:, None] * freqs).astype(np.float32)
    by_pair = np.repeat(angle.T, NH, axis=0)
    i = np.arange(128)
    mult = np.zeros((ROWS, 2 * WIN2), np.float32)
    for c in range(C):
        for r in range(-1, PATCH + 1):
            p = C * PATCH + c if r < 0 else C * PATCH + C + c if r == PATCH else c * PATCH + r
            for q in range(-1, PATCH + 1):
                near = ((r, q), (r, q + 1), (r, q - 1), (r + 1, q), (r - 1, q))
                mult[p, q + 1] = sum(0 <= u < PATCH and 0 <= v < PATCH for u, v in near)
    mult = np.concatenate([mult[:, :WIN2], mult[:, WIN2:]]) / np.float32(KP)
    return {"ident": np.eye(128, dtype=np.float32),
            "causal": np.where(i[None, :] > i[:, None], np.float32(MASKED), np.float32(0.0)),
            "cos": np.cos(by_pair).astype(np.float32), "sin": np.sin(by_pair).astype(np.float32),
            "mult": mult.astype(np.float32)}


def kernel(**inputs):
    import numpy as _np
    import concourse.bacc as _bacc
    from concourse.bass_utils import run_bass_kernel_spmd as _run

    nc = _bacc.Bacc("TRN2", target_bir_lowering=False, num_devices=1)
    arrays, args = {}, []
    for name, a in [(n, inputs[n]) for n in _INS] + list(_constants().items()):
        a = _np.ascontiguousarray(a)
        arrays[f"in_{name}_dram"] = a
        args.append(nc.dram_tensor(f"in_{name}_dram", a.shape, mybir.dt.from_np(a.dtype), kind="ExternalInput").ap())
    args.append(nc.dram_tensor("out_0_dram", (B, T, D), F32, kind="ExternalOutput").ap())
    early_fusion_kernel(nc, *args)
    r = _run(nc, [arrays], core_ids=[0])
    return r.results[0]["out_0_dram"]
```

```python
from contextlib import ExitStack

import concourse.bass as bass
from concourse import mybir

F32 = mybir.dt.float32
BF16 = mybir.dt.bfloat16
ACT = mybir.ActivationFunctionType
ALU = mybir.AluOpType
AX = mybir.AxisListType

B = 64
C = 3
IMG = 224
PATCH = 16
GRID = IMG // PATCH
D = 192
HALF = D // 2
TXT = 128
PATCHES = GRID * GRID
T = PATCHES + TXT
TILE = PATCHES // 2
KP = PATCH * PATCH * 5 * C
ROWS = C * (PATCH + 2)
WIN2 = 9
EPS = 1e-5

NH = 12
HD = D // NH
PAIR = HD // 2
PARTS = 3
K_PART = [0, 0, 0, 1, 1, 2]
Q_PART = [0, 1, 2, 0, 1, 0]
SLOTS = len(K_PART)
SINK_ROW = SLOTS * HD
MAX_ROW = SINK_ROW + PARTS
STACK = MAX_ROW + PARTS
KEYS = T + 1
KTILES = [(0, 128, 0), (128, 128, 127), (256, KEYS - 256, 255)]
QTILES = [(0, 68), (68, 128), (196, 128)]
TTILES = [(0, TILE), (TILE, TILE), (2 * TILE, TXT)]
GROUPS = [(TILE, 0, 2), (TXT, 2, 3)]
STRIP = 32
EMBED_AT = [0, 5, 1, 0, 2, 0, 0, 0, 1, 0, 0, 4,
            1, 1, 1, 1, 1, 0, 0, 0, 0, 0, 0, 0]
EXPC = 295
MASKED = -1e30

NS = 64
F = 768
FC = F // 128
SQ, SE = 2, 2

SC, BK4, BK5, BK6, BK7 = 0, 4, 5, 6, 7


def early_fusion_kernel(nc, x, txt, gamma, beta, W, bias, nscale, nbias, Wa, ba, Wproj, bp, sinks, rezero, slots, scale,
                        fc1, b1, fc2, b2, nw, ident_c, causal_c, cos_c, sin_c, mult_c, out):
    wscr = nc.dram_tensor("centred_weights", (KP, D), F32, kind="Internal").ap()
    himg = nc.dram_tensor("residual_image", (2 * B, TILE, D), F32, kind="Internal").ap()
    htxt = nc.dram_tensor("residual_text", (B, TXT, D), F32, kind="Internal").ap()
    cscr = nc.dram_tensor("combine_weights", (B, NS, T), F32, kind="Internal").ap()
    oscr = nc.dram_tensor("expert_outputs", (B, NS, D), F32, kind="Internal").ap()

    with ExitStack() as ctx:
        def sb(name, shape, dt=F32, c=ctx):
            return c.enter_context(nc.sbuf_tensor(name, shape, dt))

        ps = ctx.enter_context(nc.psum_tensor("ps", [128, 8, 512], F32))
        ident = sb("ident", [128, 128])
        y_all = sb("y_all", [HALF + 1, 2, NS, B])

        with ExitStack() as layers:
            window_w = sb("window_w", [2 * ROWS, WIN2, D + 1], F32, layers)
            hb = sb("hb", [128, D], F32, layers)
            wqk = sb("wqk", [HALF + 1, 2, SQ * SE, HALF], F32, layers)
            wv = sb("wv", [HALF + 1, 2, D], F32, layers)
            wp = sb("wp", [HALF + 1, 2, D], F32, layers)
            nwb = sb("nwb", [128, D], F32, layers)
            slots_t = sb("slots_t", [HALF, 2, NS], F32, layers)
            sink_p = sb("sink_p", [1, PARTS, NH], BF16, layers)
            ident_b = sb("ident_b", [128, 128], BF16, layers)
            causal = sb("causal", [128, 128], BF16, layers)
            cos_t = sb("cos_t", [HALF, T], F32, layers)
            sin_t = sb("sin_t", [HALF, T], F32, layers)

            KN = KP // 128
            QROW = PATCH * 5 * C
            with ExitStack() as work:
                def tmp(name, shape, dt=F32):
                    return work.enter_context(nc.sbuf_tensor(name, shape, dt))

                def sem(name):
                    return work.enter_context(nc.semaphore(name))

                wn = tmp("wn", [128, KN, D])
                gm, bt = tmp("gm", [128, KN]), tmp("bt", [128, KN])
                wmean = tmp("wmean", [128, 128])
                biasb = tmp("biasb", [128, D])
                wa = tmp("wa", [HALF, 2, 3 * D])
                ns, nb = tmp("ns", [HALF, 2]), tmp("nb", [HALF, 2])
                bar = tmp("bar", [1, 3 * D])
                brow = tmp("brow", [1, SQ * SE, HALF])
                bvrow = tmp("bvrow", [1, D])
                rz = tmp("rz", [HALF + 1, 1])
                sl, slsq = tmp("sl", [NS, D]), tmp("slsq", [NS, D])
                scl, sn = tmp("scl", [NS, 1]), tmp("sn", [NS, 1])
                half_c = tmp("half_c", [NS, 1])
                sink_r = tmp("sink_r", [1, NH])
                sink_rest = tmp("sink_rest", [1, NH])
                causal_f = tmp("causal_f", [128, 128])
                shifted = [tmp(f"shifted{s}", [ROWS, PATCH, D]) for s in range(5)]
                acc = tmp("acc", [ROWS, PATCH + 2, D])

                loaded, zeroed, scaled, sums = sem("loaded"), sem("zeroed"), sem("scaled"), sem("sums")
                centred, stored, shifts_in = sem("centred"), sem("stored"), sem("shifts_in")
                window_sum, placed, bias_mm, bias_rows = sem("window_sum"), sem("placed"), sem("bias_mm"), sem("bias_rows")
                slot_sq, slot_norm, slot_ready, slot_mm = sem("slot_sq"), sem("slot_norm"), sem("slot_ready"), sem("slot_mm")

                def row(v):
                    return v.rearrange("(o d) -> o d", o=1)

                with nc.Block() as block:
                    @block.sync
                    def _(sp):
                        loads = [
                            (wn[:], W.rearrange("(p k) d -> p k d", k=KN)),
                            (gm[:], gamma.rearrange("(p k) -> p k", k=KN)),
                            (bt[:], beta.rearrange("(p k) -> p k", k=KN)),
                            (biasb[:], row(bias).broadcast_to((128, D))),
                            (wa[:], Wa.rearrange("(c p) n -> p c n", c=2)),
                            (bar[:], row(ba)),
                            (wp[0:HALF], Wproj.rearrange("(c p) n -> p c n", c=2)),
                            (wp[HALF:HALF + 1, 0, :], row(bp)),
                            (rz[:], row(rezero).broadcast_to((HALF + 1, 1))),
                            (nwb[:], row(nw).broadcast_to((128, D))),
                            (sl[:], slots),
                            (scl[:], scale.rearrange("(s o) -> s o", o=1)),
                            (sink_r[:], row(sinks)),
                            (ident[:], ident_c), (causal_f[:], causal_c),
                            (cos_t[:], cos_c), (sin_t[:], sin_c),
                        ]
                        for dst, src in loads:
                            sp.dma_start(dst, src).then_inc(loaded, 16)
                        for dst, src in ((ns, nscale), (nb, nbias)):
                            sp.dma_start(dst[:], src.rearrange("(c p) -> p c", c=2),
                                         allow_slow_non_contiguous=True).then_inc(loaded, 16)
                        sp.dma_start(window_w[:, :, D:D + 1], mult_c.unsqueeze(2), allow_slow_non_contiguous=True).then_inc(loaded, 16)
                        sp.wait_ge(loaded, 16 * 20)
                        sp.wait_ge(centred, 1)
                        sp.dma_start(wscr.rearrange("(p k) d -> p k d", k=KN), wn[:]).then_inc(stored, 16)
                        sp.wait_ge(stored, 16)
                        sp.wait_ge(zeroed, 2)
                        wv5 = wscr.rearrange("(r q s c) d -> s c r q d", r=PATCH, s=5, c=C)
                        n = 0
                        for s in range(5):
                            lo, hi = {3: (0, PATCH - 1), 4: (1, PATCH)}.get(s, (0, PATCH))
                            dr = {3: 1, 4: -1}.get(s, 0)
                            for c in range(C):
                                sp.dma_start(shifted[s][PATCH * c + lo:PATCH * c + hi], wv5[s, c, lo + dr:hi + dr]
                                             ).then_inc(shifts_in, 16)
                                n += 1
                        top = C * PATCH
                        sp.dma_start(shifted[3][top:top + C], wv5[3, :, 0]).then_inc(shifts_in, 16)
                        sp.dma_start(shifted[4][top + C:top + 2 * C], wv5[4, :, PATCH - 1]).then_inc(shifts_in, 16)
                        sp.wait_ge(shifts_in, 16 * (n + 2))
                        sp.wait_ge(window_sum, 1)
                        sp.dma_start(window_w[0:ROWS, :, 0:D], acc[:, 0:WIN2]).then_inc(placed, 16)
                        sp.dma_start(window_w[ROWS:2 * ROWS, :, 0:D], acc[:, WIN2:2 * WIN2]).then_inc(placed, 16)
                        sp.wait_ge(bias_rows, 1)
                        sp.dma_start(wqk[HALF:HALF + 1, 0], brow[:]).then_inc(placed, 16)
                        sp.dma_start(wv[HALF:HALF + 1, 0], bvrow[:]).then_inc(placed, 16)
                        sp.wait_ge(placed, 64)

                    @block.gpsimd
                    def _(pool):
                        pool.memset(wmean[:], 1.0 / KP)
                        pool.memset(half_c[:], 0.5)
                        for s in range(5):
                            pool.memset(shifted[s][:], 0.0)
                        pool.memset(acc[:], 0.0).then_inc(zeroed, 1)
                        pool.drain().then_inc(zeroed, 1)
                        pool.wait_ge(slot_sq, 1)
                        pool.tensor_tensor(sn[:], sn[:], half_c[:], ALU.pow).then_inc(slot_norm, 1)

                    @block.vector
                    def _(dve):
                        dve.wait_ge(loaded, 16 * 20)
                        dve.tensor_tensor_reduce(out=slsq[:], in0=sl[:], in1=sl[:], scale=1.0, scalar=0.0, op0=ALU.mult,
                                                 op1=ALU.add, accum_out=sn[:]).then_inc(slot_sq, 1)
                        dve.tensor_scalar(wp[:, 0, :], wp[:, 0, :], rz[:, 0:1], None, ALU.mult)
                        dve.tensor_scalar(wp[0:HALF, 1, :], wp[0:HALF, 1, :], rz[0:HALF, 0:1], None, ALU.mult)
                        dve.tensor_copy(ident_b[:], ident[:])
                        dve.tensor_copy(causal[:], causal_f[:])
                        dve.wait_ge(sums, 1)
                        dve.tensor_tensor(hb[:], ps[:, 0, 0:D], biasb[:], ALU.add)
                        dve.tensor_tensor(wn[:], wn[:], gm[:].unsqueeze(2).broadcast_to((128, KN, D)), ALU.mult
                                          ).then_inc(scaled, 1)
                        dve.wait_ge(slot_norm, 1)
                        dve.tensor_scalar(sn[:], sn[:], 1e-5, None, ALU.max)
                        dve.drain()
                        dve.reciprocal(sn[:], sn[:])
                        dve.drain()
                        dve.tensor_scalar(sl[:], sl[:], sn[:, 0:1], scl[:, 0:1], ALU.mult, ALU.mult).then_inc(slot_ready, 1)
                        dve.wait_ge(bias_mm, 1)
                        dve.tensor_tensor(bar[:, 0:512], ps[0:1, 2, :], bar[:, 0:512], ALU.add)
                        dve.tensor_tensor(bar[:, 512:3 * D], ps[0:1, 3, 0:3 * D - 512], bar[:, 512:3 * D], ALU.add)
                        for c in range(2):
                            dve.tensor_scalar(wa[:, c, :], wa[:, c, :], ns[:, c:c + 1], None, ALU.mult)
                        dve.drain()
                        for side in range(2):
                            k = 0.25 if side == 0 else 1.0
                            for e in range(2):
                                for c in range(2):
                                    src = wa[:, c, D * side:D * side + D].rearrange("p (h i e) -> p i h e", h=NH, e=2)[:, :, :, e]
                                    dve.tensor_scalar(wqk[0:HALF, c, 2 * side + e, :].rearrange("p (i h) -> p i h", h=NH),
                                                      src, k, None, ALU.mult)
                                src = bar[:, D * side:D * side + D].rearrange("p (h i e) -> p i h e", h=NH, e=2)[:, :, :, e]
                                dve.tensor_scalar(brow[:, 2 * side + e, :].rearrange("p (i h) -> p i h", h=NH), src, k, None,
                                                  ALU.mult)
                        dve.tensor_copy(wv[0:HALF], wa[:, :, 2 * D:3 * D])
                        dve.tensor_copy(bvrow[:], bar[:, 2 * D:3 * D])
                        dve.tensor_copy(sink_p[:, 0], sink_r[:])
                        dve.drain()
                        dve.tensor_tensor(sink_rest[:], sink_r[:], sink_p[:, 0], ALU.subtract)
                        dve.drain()
                        dve.tensor_copy(sink_p[:, 1], sink_rest[:])
                        dve.drain()
                        dve.tensor_tensor(sink_p[:, 2], sink_rest[:], sink_p[:, 1], ALU.subtract).then_inc(bias_rows, 1)
                        dve.wait_ge(sums, 2)
                        mean = ps[:, 1, 0:D].unsqueeze(1).broadcast_to((128, KN, D))
                        dve.tensor_tensor(wn[:], wn[:], mean, ALU.subtract).then_inc(centred, 1)
                        dve.wait_ge(slot_mm, 1)
                        dve.tensor_copy(slots_t[:], ps[0:HALF, 4, 0:2 * NS].rearrange("p (c s) -> p c s", c=2))
                        dve.wait_ge(shifts_in, 16 * 17)
                        for s, col in ((0, 1), (1, 0), (2, 2), (3, 1), (4, 1)):
                            dve.drain()
                            last = dve.tensor_tensor(acc[:, col:col + PATCH], acc[:, col:col + PATCH], shifted[s][:], ALU.add)
                        last.then_inc(window_sum, 1)

                    @block.tensor
                    def _(pe):
                        pe.wait_ge(loaded, 16 * 20)
                        pe.wait_ge(zeroed, 1)
                        for k in range(KN):
                            mm = pe.matmul(ps[:, 0, 0:D], bt[:, k:k + 1].broadcast_to((128, 128)), wn[:, k, :],
                                           start=(k == 0), stop=(k == KN - 1))
                        mm.then_inc(sums, 1)
                        for bank, lo, hi in ((2, 0, 512), (3, 512, 3 * D)):
                            for c in range(2):
                                mm = pe.matmul(ps[0:1, bank, 0:hi - lo], nb[:, c:c + 1], wa[:, c, lo:hi], start=(c == 0),
                                               stop=(c == 1))
                        mm.then_inc(bias_mm, 1)
                        pe.wait_ge(scaled, 1)
                        for k in range(KN):
                            mm = pe.matmul(ps[:, 1, 0:D], wmean[:], wn[:, k, :], start=(k == 0), stop=(k == KN - 1))
                        mm.then_inc(sums, 1)
                        pe.wait_ge(slot_ready, 1)
                        for c in range(2):
                            mm = pe.transpose(ps[0:HALF, 4, NS * c:NS * (c + 1)], sl[:, HALF * c:HALF * (c + 1)],
                                              ident[0:NS, 0:NS])
                        mm.then_inc(slot_mm, 1)

            with ExitStack() as work:
                def tmp(name, shape, dt=F32):
                    return work.enter_context(nc.sbuf_tensor(name, shape, dt))

                xw = [tmp(f"xw{i}", [2 * ROWS, GRID, IMG]) for i in range(2)]
                xw_flat = [t[:].rearrange("p i w -> p (i w)") for t in xw]
                strips, per_strip = tmp("strips", [128, PATCHES]), tmp("per_strip", [128, 1])
                xsq = tmp("xsq", [2 * ROWS, GRID * IMG])
                h_new = [tmp(f"h_new{i}", [128, 3, D]) for i in range(2)]
                h_held = tmp("h_held", [128, 3, D])
                h1 = tmp("h1", [128, 3, D])
                xhat = tmp("xhat", [128, 3, D])
                z = tmp("z", [128, 3, D])
                ynorm = xhat
                xt = tmp("xt", [HALF + 1, 2, KEYS])
                zt = tmp("zt", [HALF, 2, T])
                yt = tmp("yt", [HALF + 1, 2, T])
                by_cos, by_sin = tmp("by_cos", [HALF, SQ, SE, T]), tmp("by_sin", [HALF, SQ, SE, T])
                rot = tmp("rot", [HALF, SQ, SE, T])
                rest = by_cos
                part = [tmp(f"part{i}", [HALF, SQ, SE, T], BF16) for i in range(PARTS)]
                kst = [tmp(f"kst{i}", [128, NH, 3 * 128], BF16) for i in range(2)]
                qst = [tmp(f"qst{i}", [128, NH, T], BF16) for i in range(2)]
                vaug = [tmp(f"vaug{i}", [128, 3, NH, STRIP]) for i in range(2)]
                prob = tmp("prob", [128, 8, 2 * EXPC])
                yraw = tmp("yraw", [128, 3, T])
                negmax, mrest = tmp("negmax", [128, 3, NH]), tmp("mrest", [128, 3, NH // 2])
                mpart = [tmp(f"mpart{g}", [128, 3, PARTS, NH // 2], BF16) for g in range(2)]
                mt = [tmp(f"mt{g}", [PARTS * NH // 2, T], BF16) for g in range(2)]
                rden = tmp("rden", [128, 3, NH])
                stat1, rstd1 = tmp("stat1", [TILE, 4]), tmp("rstd1", [TILE, 2])
                bn, mv1, mv2 = tmp("bn", [128, 3, 6]), tmp("mv1", [128, 3, 2]), tmp("mv2", [128, 3, 2])
                bn2 = tmp("bn2", [128, 3, 6])
                rstd2 = tmp("rstd2", [128, 3])
                zss, alpha, beta_t = tmp("zss", [128, 3]), tmp("alpha", [128, 3]), tmp("beta_t", [128, 3])
                pw = tmp("pw", [128, 3])
                neg_half, pos_half, neg_one, eps = (tmp(n, [128, 3]) for n in ("neg_half", "pos_half", "neg_one", "eps"))
                zero = tmp("zero", [128, 3, NH // 2])
                logit, lexp = tmp("logit", [128, 3, NS]), tmp("lexp", [128, 3, NS])
                lmax, lsum, lrec = tmp("lmax", [128, 3]), tmp("lsum", [128, 3]), tmp("lrec", [128, 3])
                comb = tmp("comb", [NS, T])
                dexp, dmax, dsum, drec = tmp("dexp", [NS, T]), tmp("dmax", [NS, 1]), tmp("dsum", [NS, 1]), tmp("drec", [NS, 1])
                disp = tmp("disp", [128, 3, NS])

                class Signal:

                    def __init__(self, name, per):
                        self.sem, self.per = work.enter_context(nc.semaphore(name)), per

                    def wait(self, engine, batch, k=None, apart=False):
                        k = self.per if k is None else k
                        if isinstance(batch, int):
                            if batch < 0:
                                return
                            if batch >= B:
                                batch, k = B - 1, self.per
                        if apart:
                            engine.wait_ge(prepared, 1)
                        engine.wait_ge(self.sem, batch * self.per + k)

                x_in, txt_in, held, stack_in = Signal("x_in", 160), Signal("txt_in", 16), Signal("held", 16), Signal("stack_in", 16 * 24)
                max_in = [Signal(f"max_in{g}", 16) for g in range(2)]
                h_out, c_out = Signal("h_out", 32), Signal("c_out", 16)
                zt_mm, s_mm, embed_mm, strips_mm, squares_mm, l_mm, lt_mm, ct_mm = Signal("zt_mm", 1), Signal("s_mm", NH), Signal("embed_mm", 1), Signal("strips_mm", 1), Signal("squares_mm", 1), Signal("l_mm", 1), Signal("lt_mm", 1), Signal("ct_mm", 1)
                mt_mm, d_mm, xt_mm, ym_mm, st_mm, pv_mm = Signal("mt_mm", 2), Signal("d_mm", 1), Signal("xt_mm", 1), Signal("ym_mm", 1), Signal("st_mm", NH), Signal("pv_mm", 3)
                yr_mm, qk_mm, yt_mm, v_mm, proj_mm = Signal("yr_mm", 3), Signal("qk_mm", 2), Signal("yt_mm", 1), Signal("v_mm", 1), Signal("proj_mm", 1)
                zt_ready, ce_ready, de_ready, ct_ready, sq_ready, xt_ready = Signal("zt_ready", 1), Signal("ce_ready", 1), Signal("de_ready", 1), Signal("ct_ready", 1), Signal("sq_ready", 1), Signal("xt_ready", 1)
                ym_ready, exp_ready, pv_ready, yt_ready, v_ready, zs_ready = Signal("ym_ready", 1), Signal("exp_ready", NH), Signal("pv_ready", 3), Signal("yt_ready", 1), Signal("v_ready", 1), Signal("zs_ready", 1)
                strips_ready = Signal("strips_ready", 1)
                p1_ready, p2_ready = Signal("p1_ready", 2), Signal("p2_ready", 2)
                max_ready, mpart_ready, mt_ready, l_scaled, lmax_ready, c_ready, dmax_ready = Signal("max_ready", NH), Signal("mpart_ready", 2), [Signal(f"mt_ready{g}", 1) for g in range(2)], Signal("l_scaled", 1), Signal("lmax_ready", 1), Signal("c_ready", 1), Signal("dmax_ready", 1)
                dn_ready, dp_ready, stat_ready, ln1_ready, xhat_ready = Signal("dn_ready", 1), Signal("dp_ready", 1), Signal("stat_ready", 1), Signal("ln1_ready", 1), Signal("xhat_ready", 1)
                yn_ready, rope_ready, h1_ready, ln2_ready, z_ready = Signal("yn_ready", 3), Signal("rope_ready", 2), Signal("h1_ready", 1), Signal("ln2_ready", 1), Signal("z_ready", 1)
                rot_ready, rest_ready, p3_ready, rstd1_ready, rstd2_ready, beta_ready = Signal("rot_ready", 2), Signal("rest_ready", 2), Signal("p3_ready", 2), Signal("rstd1_ready", 1), Signal("rstd2_ready", 1), Signal("beta_ready", 1)

                prepared, sinks_in = work.enter_context(nc.semaphore("prepared")), work.enter_context(nc.semaphore("sinks_in"))
                with nc.Block() as block:
                    @block.vector
                    def _(dve):
                        for t in (*xw, *kst, *qst, *vaug, xt, yt, *h_new, mv1, mv2, negmax, zss, stat1):
                            dve.memset(t[:], 0.0)
                        dve.memset(neg_half[:], -0.5)
                        dve.memset(eps[:], EPS)
                        dve.memset(zero[:], 0.0)
                        dve.memset(per_strip[:], 1.0 / STRIP)
                        dve.memset(pos_half[:], 0.5)
                        dve.memset(neg_one[:], -1.0)
                        for t in (lmax, lsum, mrest, rstd2):
                            dve.memset(t[:], 1.0)
                        dve.drain()
                        for i in range(2):
                            dve.memset(kst[i][SINK_ROW:128, :, 0:KEYS], 1.0)
                            dve.memset(qst[i][SINK_ROW:MAX_ROW], 1.0)
                            dve.memset(vaug[i][:, :, :, HD:HD + 1], 1.0)
                        dve.memset(xt[HALF:HALF + 1, 0, 1:KEYS], 1.0)
                        dve.memset(yt[HALF:HALF + 1, 0], 1.0)
                        dve.memset(y_all[HALF:HALF + 1, 0], 1.0)
                        dve.drain()
                        for i in range(2):
                            last = dve.memset(kst[i][SINK_ROW:MAX_ROW], 0.0)
                        last.then_inc(prepared, 1)

                    @block.sync
                    def _(sp):
                        sp.wait_ge(prepared, 1)
                        for i in range(2):
                            sp.dma_start(kst[i][SINK_ROW:MAX_ROW, :, 0:1], sink_p[:],
                                         allow_slow_non_contiguous=True).then_inc(sinks_in, 16)
                        sp.wait_ge(sinks_in, 32)

                def run(step, engine):
                    for b in range(-3, 3):
                        step(b, b % 2)
                    with engine.Fori(3, B - 4, 2) as b:
                        step(b, 1)
                        step(b + 1, 0)
                    for b in (B - 3, B - 2, B - 1, B):
                        step(b, b % 2)

                def has(batch):
                    return not isinstance(batch, int) or 0 <= batch < B

                block = work.enter_context(nc.Block())

                @block.sync
                def _(sp):
                    def one(t):
                        return t if isinstance(t, slice) else bass.ds(t, 1)

                    def load_image(b, i):
                        embed_mm.wait(sp, b - 2)
                        x_in.wait(sp, b - 1)
                        xb = x[one(b)].rearrange("o c (i r) w -> (o c) r i w", r=PATCH)
                        top = C * PATCH
                        for r0, c0, w0, wn_ in ((0, 1, 0, 216), (ROWS, 0, 8, 216)):
                            for c in range(C):
                                sp.dma_start(xw[i][r0 + PATCH * c:r0 + PATCH * (c + 1), :, c0:c0 + wn_],
                                             xb[c, :, :, w0:w0 + wn_]).then_inc(x_in.sem, 16)
                            sp.dma_start(xw[i][r0 + top:r0 + top + C, 1:GRID, c0:c0 + wn_],
                                         xb[:, PATCH - 1, 0:GRID - 1, w0:w0 + wn_]).then_inc(x_in.sem, 16)
                            sp.dma_start(xw[i][r0 + top + C:r0 + top + 2 * C, 0:GRID - 1, c0:c0 + wn_],
                                         xb[:, 0, 1:GRID, w0:w0 + wn_]).then_inc(x_in.sem, 16)

                    def store_maxima(b, i, g):
                        mt_ready[g].wait(sp, b)
                        max_in[g].wait(sp, b - 1)
                        st_mm.wait(sp, b - 2)
                        sp.dma_start(qst[i][MAX_ROW:STACK, NH // 2 * g:NH // 2 * (g + 1), :], mt[g][:]).then_inc(max_in[g].sem, 16)

                    def stack(b, i, p, side):
                        st, which = ((qst[i], Q_PART), (kst[i], K_PART))[side]
                        for slot in range(SLOTS):
                            if which[slot] == p:
                                for e in range(SE):
                                    r = HD * slot + PAIR * e
                                    dst = st[r:r + PAIR] if side == 0 else st[r:r + PAIR, :, 1:KEYS]
                                    sp.dma_start(dst, part[p][:, side, e, :]).then_inc(stack_in.sem, 16)

                    def step(b, i):
                        if has(b):
                            xhat_ready.wait(sp, b)
                            h1_ready.wait(sp, b - 1, apart=True)
                            sp.dma_start(h_held[:], h_new[i][:]).then_inc(held.sem, 16)
                        if has(b + 1):
                            stack_in.wait(sp, b)
                            st_mm.wait(sp, b - 1)
                            p1_ready.wait(sp, b + 1)
                            stack(b + 1, 1 - i, 0, 0)
                            stack(b + 1, 1 - i, 0, 1)
                        if has(b):
                            store_maxima(b, i, 0)
                        if has(b + 2):
                            held.wait(sp, b)
                            txt_in.wait(sp, b + 1)
                            xhat_ready.wait(sp, b)
                            sp.dma_start(h_new[i][:, 2, :], txt[one(b + 2)].rearrange("o t d -> (o t) d")).then_inc(txt_in.sem, 16)
                        if has(b + 1):
                            p2_ready.wait(sp, b + 1)
                            stack(b + 1, 1 - i, 1, 0)
                        if has(b):
                            store_maxima(b, i, 1)
                        if has(b + 1):
                            stack(b + 1, 1 - i, 1, 1)
                            p3_ready.wait(sp, b + 1)
                            stack(b + 1, 1 - i, 2, 0)
                            stack(b + 1, 1 - i, 2, 1)
                        if has(b + 3):
                            load_image(b + 3, 1 - i)
                        if has(b - 1):
                            ct_ready.wait(sp, b - 1)
                            c_out.wait(sp, b - 2)
                            sp.dma_start(cscr[one(b - 1)].rearrange("o s t -> (o s) t"), comb[:]).then_inc(c_out.sem, 16)
                        if has(b):
                            h1_ready.wait(sp, b)
                            h_out.wait(sp, b - 1)
                            sp.dma_start(himg[bass.ds(2 * b, 2)].rearrange("k p d -> p k d"), h1[0:TILE, 0:2]).then_inc(h_out.sem, 16)
                            sp.dma_start(htxt[one(b)].rearrange("o p d -> (o p) d"), h1[:, 2]).then_inc(h_out.sem, 16)

                    run(step, sp)
                    c_out.wait(sp, B - 1)
                    h_out.wait(sp, B - 1)

                @block.tensor
                def _(pe):
                    def embed(b, i, n):
                        if n == 0:
                            x_in.wait(pe, b)
                            h1_ready.wait(pe, b - 3)
                        half, q = divmod(n, WIN2)
                        lo = TILE * PATCH * half + q
                        mm = pe.matmul(ps[0:TILE, BK7, half * (D + 1):(half + 1) * (D + 1)],
                                       xw_flat[i][:, lo:lo + PATCH * (TILE - 1) + 1:PATCH], window_w[:, q, :],
                                       start=(q == 0), stop=(q == WIN2 - 1))
                        if n == 2 * WIN2 - 1:
                            mm.then_inc(embed_mm.sem, 1)

                    def square_strips(b, columns):
                        if columns[0] == 0:
                            sq_ready.wait(pe, b)
                            v_ready.wait(pe, b - 1)
                            zt_ready.wait(pe, b - 3)
                        for q in columns:
                            s = q % 4
                            mm = pe.matmul(ps[STRIP * s:STRIP * (s + 1), BK4, 0:PATCHES],
                                           window_w[:, q, D:D + 1].broadcast_to((2 * ROWS, STRIP)),
                                           xsq[:, q:q + PATCH * (PATCHES - 1) + 1:PATCH], start=(q < 4), stop=(q + 4 >= WIN2),
                                           skip_group_check=True)
                        if q == WIN2 - 1:
                            mm.then_inc(strips_mm.sem, 1)

                    def square_sums(b):
                        strips_ready.wait(pe, b)
                        for half in range(2):
                            col = 2 * (D + 1) + half
                            mm = pe.matmul(ps[0:TILE, BK7, col:col + 1], strips[:, TILE * half:TILE * (half + 1)],
                                           per_strip[:], start=True, stop=True)
                        mm.then_inc(squares_mm.sem, 1)

                    def scores(b, i, h):
                        bank = SC + 2 * (h % 2)
                        if h == 0:
                            stack_in.wait(pe, b)
                        if h < 2:
                            rope_ready.wait(pe, b + 1, h + 1)
                        else:
                            max_ready.wait(pe, b, h - 1)
                        for q, bk, col in ((2, bank, 0), (0, bank + 1, 0), (1, bank + 1, QTILES[0][1] + 1)):
                            q0, nq = QTILES[q]
                            keys = q0 + nq + 1
                            pe.matmul(ps[0:nq, bk, col:col + keys], qst[i][0:MAX_ROW, h, q0:q0 + nq],
                                      kst[i][0:MAX_ROW, h, 0:keys], start=True, stop=False)
                            mm = pe.matmul(ps[0:nq, bk, col + q0 + 1:col + keys], ident_b[:, 0:nq], causal[:, 0:nq],
                                           start=False, stop=True)
                        mm.then_inc(s_mm.sem, 1)

                    def scores_t(b, i, h):
                        bank = SC + 2 * (h % 2)
                        if h in (0, NH // 2):
                            max_in[h // (NH // 2)].wait(pe, b)
                        if h < 2:
                            max_ready.wait(pe, b, NH - 1 + h)
                        else:
                            exp_ready.wait(pe, b, h - 1)
                        k0, k1, k2 = (kst[i][0:STACK, h, 128 * k:128 * (k + 1)] for k in range(3))
                        q = qst[i][0:STACK, h]
                        n0 = T - EXPC
                        c1, c2 = n0, n0 + T - KTILES[1][2]
                        pe.matmul(ps[:, bank, 0:EXPC], k0, q[:, 0:EXPC], start=True, stop=False)
                        pe.matmul(ps[:, bank, 0:127], causal[:], ident_b[:, 1:128], start=False, stop=True)
                        pe.matmul(ps[:, bank + 1, 0:n0], k0, q[:, EXPC:T], start=True, stop=True)
                        pe.matmul(ps[:, bank + 1, c1:c2], k1, q[:, KTILES[1][2]:T], start=True, stop=False)
                        pe.matmul(ps[:, bank + 1, c1:c1 + 128], causal[:], ident_b[:], start=False, stop=True)
                        pe.matmul(ps[:, bank + 1, c2:EXPC], k2, q[:, KTILES[2][2]:T], start=True, stop=False)
                        pe.matmul(ps[:, bank + 1, c2:EXPC], causal[:], ident_b[:, 0:EXPC - c2], start=False,
                                  stop=True).then_inc(st_mm.sem, 1)

                    def values(b, i, g, k):
                        if k == 0:
                            exp_ready.wait(pe, b, 4 * g + 4)
                            if g == 0:
                                v_ready.wait(pe, b)
                                de_ready.wait(pe, b - 1)
                            else:
                                pv_ready.wait(pe, b, g)
                        _, nk, q0 = KTILES[k]
                        col = sum(T - KTILES[n][2] for n in range(k))
                        for s in range(4):
                            h = 4 * g + s
                            mm = pe.matmul(ps[STRIP * s:STRIP * (s + 1), BK6, q0:T], vaug[i][0:nk, k, h, :],
                                           prob[0:nk, h % 8, col:col + T - q0], start=(k == 0), stop=(k == 2),
                                           skip_group_check=True)
                        if k == 2:
                            mm.then_inc(pv_mm.sem, 1)

                    def token_values(b, tiles):
                        for t in tiles:
                            k0, nk, _ = KTILES[t]
                            for c in range(2):
                                k = HALF + 1 - c
                                mm = pe.matmul(ps[0:nk, (BK6, BK6, BK4)[t], D * (t % 2):D * (t % 2) + D],
                                               xt[0:k, c, k0:k0 + nk], wv[0:k, c, :], start=(c == 0), stop=(c == 1))
                            if t == 2:
                                mm.then_inc(v_mm.sem, 1)

                    def turn(dst_banks, src, n_src=None):
                        for c in range(2):
                            for t, (t0, nt) in enumerate(TTILES):
                                mm = pe.transpose(ps[0:HALF, dst_banks[c], t0:t0 + nt],
                                                  src[0:nt, t, HALF * c:HALF * (c + 1)], ident[0:nt, 0:nt])
                        return mm

                    def maxima(b, g):
                        for q, (q0, nq) in enumerate(QTILES):
                            mm = pe.transpose(ps[0:PARTS * NH // 2, (BK6, BK5)[g], :].bitcast(BF16)[:, q0:q0 + nq],
                                              mpart[g][0:nq, q].rearrange("p a h -> p (a h)"), ident_b[0:nq, 0:nq])
                        mm.then_inc(mt_mm.sem, 1)

                    def step(b, i):
                        moe, att, mid, front = has(b - 1), has(b), has(b + 1), has(b + 2)
                        todo = list(range(2 * WIN2)) if front else []
                        for h in range(NH):
                            if att:
                                scores(b, i, h)
                            if mid and h == 0:
                                xt_ready.wait(pe, b + 1)
                                yt_ready.wait(pe, b - 1)
                                token_values(b + 1, (0, 1))
                            if mid and h == 1:
                                token_values(b + 1, (2,))
                            for n in todo[:EMBED_AT[h]]:
                                embed(b + 2, i, n)
                            todo = todo[EMBED_AT[h]:]
                            if moe and h == 3:
                                z_ready.wait(pe, b - 1)
                                v_ready.wait(pe, b + 1)
                                h1_ready.wait(pe, b - 1)
                                turn((BK5, BK4), z).then_inc(zt_mm.sem, 1)
                            if moe and h in (7, 8):
                                zt_ready.wait(pe, b - 1)
                                for t in (0, 1) if h == 7 else (2,):
                                    t0, nt = TTILES[t]
                                    for c in range(2):
                                        mm = pe.matmul(ps[0:nt, BK5, NS * t:NS * (t + 1)], zt[:, c, t0:t0 + nt],
                                                       slots_t[:, c, :], start=(c == 0), stop=(c == 1))
                                if h == 8:
                                    mm.then_inc(l_mm.sem, 1)
                            if front and h in (5, 6):
                                square_strips(b + 2, range(4) if h == 5 else range(4, WIN2))
                            if att and h == 8:
                                v_ready.wait(pe, b + 1, apart=True)
                                mpart_ready.wait(pe, b, 1)
                                maxima(b, 0)
                            if moe and h == 10:
                                mt_ready[0].wait(pe, b, apart=True)
                                l_scaled.wait(pe, b - 1)
                                for t, (t0, nt) in enumerate(TTILES):
                                    mm = pe.transpose(ps[0:NS, BK6, t0:t0 + nt], logit[0:nt, t, :], ident[0:nt, 0:nt])
                                mm.then_inc(lt_mm.sem, 1)
                        for h in range(NH):
                            if att:
                                scores_t(b, i, h)
                            for n in todo[:EMBED_AT[NH + h]]:
                                embed(b + 2, i, n)
                            todo = todo[EMBED_AT[NH + h]:]
                            if front and h == 4:
                                square_sums(b + 2)
                            if att and h == 2:
                                l_scaled.wait(pe, b - 1, apart=True)
                                mpart_ready.wait(pe, b, 2)
                                maxima(b, 1)
                            if att and h in (5, 6, 7, 9, 10, 11):
                                values(b, i, h // 4 - 1, (h - 1) % 4)
                            if moe and h == 6:
                                zt_ready.wait(pe, b - 1, apart=True)
                                c_ready.wait(pe, b - 1)
                                for t, (t0, nt) in enumerate(TTILES):
                                    mm = pe.transpose(ps[0:NS, BK4, t0:t0 + nt], lexp[0:nt, t, :], ident[0:nt, 0:nt])
                                mm.then_inc(ct_mm.sem, 1)
                            if moe and h == 8:
                                ct_ready.wait(pe, b - 1, apart=True)
                                dn_ready.wait(pe, b - 1)
                                for t, (t0, nt) in enumerate(TTILES):
                                    mm = pe.transpose(ps[0:nt, BK4, NS * t:NS * (t + 1)], dexp[:, t0:t0 + nt],
                                                      ident[0:NS, 0:NS])
                                mm.then_inc(d_mm.sem, 1)
                        if moe:
                            dp_ready.wait(pe, b - 1)
                            mt_ready[1].wait(pe, b)
                            for c in range(2):
                                for t, (t0, nt) in enumerate(TTILES):
                                    mm = pe.matmul(ps[0:HALF, BK5, NS * c:NS * (c + 1)],
                                                   z[0:nt, t, HALF * c:HALF * (c + 1)], disp[0:nt, t, :],
                                                   start=(t == 0), stop=(t == 2))
                            mm.then_inc(ym_mm.sem, 1)
                        if front:
                            xhat_ready.wait(pe, b + 2)
                            dp_ready.wait(pe, b - 1)
                            turn((BK4, BK7), xhat).then_inc(xt_mm.sem, 1)

                        def project(side, e):
                            if side == 0 and e == 0:
                                xt_ready.wait(pe, b + 2)
                            if e == 0:
                                exp_ready.wait(pe, b, NH - 1 + side)
                            for c in range(2):
                                k = HALF + 1 - c
                                mm = pe.matmul(ps[0:HALF, SC + 2 * side + e, 0:T], wqk[0:k, c, 2 * side + e, :],
                                               xt[0:k, c, 1:KEYS], start=(c == 0), stop=(c == 1))
                            if e == 1:
                                mm.then_inc(qk_mm.sem, 1)

                        if att:
                            for k in range(3):
                                values(b, i, 2, k)
                        if front:
                            project(0, 0)
                            project(0, 1)
                        if att:
                            pv_ready.wait(pe, b)
                            for t, (t0, nt) in enumerate(TTILES):
                                if t == 0:
                                    xt_ready.wait(pe, b + 2)
                                    ym_ready.wait(pe, b - 1)
                                for g in range(3):
                                    mm = pe.transpose(ps[0:nt, (BK4, BK5, BK7)[t], 128 * g:128 * (g + 1)],
                                                      yraw[:, g, t0:t0 + nt], ident[:])
                                mm.then_inc(yr_mm.sem, 1)
                        if front:
                            project(1, 0)
                        if att:
                            yn_ready.wait(pe, b)
                            turn((BK6, BK4), ynorm).then_inc(yt_mm.sem, 1)
                        if front:
                            project(1, 1)
                        if att:
                            yt_ready.wait(pe, b)
                            for t, (t0, nt) in enumerate(TTILES):
                                for c in range(2):
                                    k = HALF + 1 - c
                                    mm = pe.matmul(ps[0:nt, (BK5, BK5, BK7)[t], D * (t % 2):D * (t % 2) + D],
                                                   yt[0:k, c, t0:t0 + nt], wp[0:k, c, :], start=(c == 0), stop=(c == 1))
                            mm.then_inc(proj_mm.sem, 1)

                    run(step, pe)

                @block.scalar
                def _(act):
                    def fn(out_, in_, f, **kw):
                        return nc.scalar.activation(out_, in_, f, **kw)

                    def split(b, which, done):
                        src, dst, need = ((rot, part[0], rot_ready), (rest, part[1], rest_ready))[which]
                        for side in range(2):
                            need.wait(act, b, side + 1)
                            if side == 0:
                                stack_in.wait(act, b - 1)
                            fn(dst[:, side], src[:, side], ACT.Copy).then_inc(done.sem, 1)

                    def step(b, i):
                        moe, att, front, mid = has(b - 1), has(b), has(b + 2), has(b + 1)
                        if mid:
                            split(b + 1, 0, p1_ready)
                        if mid:
                            v_mm.wait(act, b + 1)
                            fn(vaug[1 - i][:, 0:2, :, 0:HD], ps[:, BK6, 0:2 * D].rearrange("p (k h d) -> p k h d", k=2, h=NH),
                               ACT.Copy)
                            nk = KTILES[2][1]
                            fn(vaug[1 - i][0:nk, 2, :, 0:HD], ps[0:nk, BK4, 0:D].rearrange("p (h d) -> p h d", h=NH),
                               ACT.Copy).then_inc(v_ready.sem, 1)
                        if moe:
                            act.drain()
                            z_ready.wait(act, b - 1)
                            beta_ready.wait(act, b - 2)
                            for t, (_, nt) in enumerate(TTILES):
                                if t > 0:
                                    act.drain()
                                last = fn(lexp[0:nt].rearrange("p t s -> p (t s)"), z[0:nt, t, :], ACT.Square, accum_out=zss[0:nt, t:t + 1])
                            last.then_inc(zs_ready.sem, 1)
                        if moe:
                            zt_mm.wait(act, b - 1)
                            fn(zt[:, 0], ps[0:HALF, BK5, 0:T], ACT.Copy)
                            fn(zt[:, 1], ps[0:HALF, BK4, 0:T], ACT.Copy).then_inc(zt_ready.sem, 1)
                        if front:
                            strips_mm.wait(act, b + 2)
                            squares_mm.wait(act, b + 1)
                            fn(strips[:], ps[:, BK4, 0:PATCHES], ACT.Copy).then_inc(strips_ready.sem, 1)
                        if mid:
                            split(b + 1, 1, p2_ready)
                        if att:
                            mt_mm.wait(act, b, 1)
                            max_in[0].wait(act, b - 1)
                            fn(mt[0][:], ps[0:PARTS * NH // 2, BK6, :].bitcast(BF16)[:, 0:T], ACT.Copy).then_inc(mt_ready[0].sem, 1)
                        if moe:
                            l_mm.wait(act, b - 1)
                            beta_ready.wait(act, b - 1)
                            for t, (_, nt) in enumerate(TTILES):
                                last = fn(logit[0:nt, t, :], ps[0:nt, BK5, NS * t:NS * (t + 1)], ACT.Copy,
                                          scale=beta_t[0:nt, t:t + 1])
                            last.then_inc(l_scaled.sem, 1)
                        if moe:
                            lmax_ready.wait(act, b - 1)
                            for t, (_, nt) in enumerate(TTILES):
                                last = fn(lexp[0:nt, t, :], logit[0:nt, t, :], ACT.Exp, bias=lmax[0:nt, t:t + 1],
                                          accum_out=lsum[0:nt, t:t + 1])
                            last.then_inc(ce_ready.sem, 1)
                        if moe:
                            dmax_ready.wait(act, b - 1)
                            fn(dexp[:], ps[0:NS, BK6, 0:T], ACT.Exp, bias=dmax[:, 0:1],
                               accum_out=dsum[:, 0:1]).then_inc(de_ready.sem, 1)
                        for h in range(NH):
                            if att:
                                st_mm.wait(act, b, h + 1)
                                if h >= 8:
                                    pv_mm.wait(act, b, 1)
                                elif h % 4 == 0:
                                    pv_mm.wait(act, b - 1)
                                fn(prob[:, h % 8, :].rearrange("p (a q) -> p a q", a=2),
                                   ps[:, SC + 2 * (h % 2):SC + 2 * (h % 2) + 2, 0:EXPC], ACT.Exp).then_inc(exp_ready.sem, 1)
                            if moe and h == 6:
                                ct_mm.wait(act, b - 1)
                                c_out.wait(act, b - 2)
                                fn(comb[:], ps[0:NS, BK4, 0:T], ACT.Copy).then_inc(ct_ready.sem, 1)
                            if att and h in (7, 11):
                                heads_out(b, h // 4 - 1)
                            if moe and h == 11:
                                ym_mm.wait(act, b - 1)
                                fn(y_all[0:HALF, :, :, bass.ds(b - 1, 1)],
                                   ps[0:HALF, BK5, 0:2 * NS].rearrange("p (c s o) -> p c s o", c=2, o=1), ACT.Copy
                                   ).then_inc(ym_ready.sem, 1)
                            if front and h == 11:
                                xt_mm.wait(act, b + 2)
                                v_mm.wait(act, b + 1)
                                fn(xt[0:HALF, 0, 1:KEYS], ps[0:HALF, BK4, 0:T], ACT.Copy)
                                fn(xt[0:HALF, 1, 1:KEYS], ps[0:HALF, BK7, 0:T], ACT.Copy).then_inc(xt_ready.sem, 1)
                        if att:
                            heads_out(b, 2)
                            yt_mm.wait(act, b)
                            fn(yt[0:HALF, 0], ps[0:HALF, BK6, 0:T], ACT.Copy)
                            fn(yt[0:HALF, 1], ps[0:HALF, BK4, 0:T], ACT.Copy).then_inc(yt_ready.sem, 1)
                        if has(b + 3):
                            x_in.wait(act, b + 3)
                            strips_mm.wait(act, b + 2)
                            fn(xsq[:], xw_flat[1 - i], ACT.Square).then_inc(sq_ready.sem, 1)
                    def heads_out(b, g):
                        pv_mm.wait(act, b, g + 1)
                        if g == 0:
                            yr_mm.wait(act, b - 1)
                        fn(yraw[:, g, :], ps[:, BK6, 0:T], ACT.Copy).then_inc(pv_ready.sem, 1)

                    run(step, act)

                @block.vector
                def _(dve):
                    def over(tile):
                        return [tile[0:n, a:z_] for n, a, z_ in GROUPS]

                    def norm_stats(src, bnt, mv):
                        for t, (_, nt) in enumerate(TTILES):
                            dve.bn_stats(bnt[0:nt, t, :], src[0:nt, t, :])
                        dve.drain()
                        for t, (_, nt) in enumerate(TTILES):
                            last = dve.bn_aggr(mv[0:nt, t, :], bnt[0:nt, t, :])
                        return last

                    def step(b, i):
                        moe, att, front = has(b - 1), has(b), has(b + 2)
                        for h in range(NH):
                            if att:
                                bank = SC + 2 * (h % 2)
                                if h == 0:
                                    mpart_ready.wait(dve, b - 1)
                                s_mm.wait(dve, b, h + 1)
                                for q, bk, col in ((2, bank, 0), (0, bank + 1, 0), (1, bank + 1, QTILES[0][1] + 1)):
                                    q0, nq = QTILES[q]
                                    last = dve.tensor_reduce(negmax[0:nq, q, h:h + 1], ps[0:nq, bk, col:col + q0 + nq + 1],
                                                             AX.X, ALU.max, negate=True)
                                last.then_inc(max_ready.sem, 1)
                            if moe and h == 9:
                                l_scaled.wait(dve, b - 1)
                                for n, t0, t1 in GROUPS:
                                    last = dve.tensor_reduce(lmax[0:n, t0:t1], logit[0:n, t0:t1], AX.X, ALU.max, negate=True)
                                last.then_inc(lmax_ready.sem, 1)
                        if moe:
                            lt_mm.wait(dve, b - 1)
                            dve.tensor_reduce(dmax[:], ps[0:NS, BK6, 0:T], AX.X, ALU.max, negate=True).then_inc(dmax_ready.sem, 1)
                        if att:
                            mt_mm.wait(dve, b, 2)
                            max_in[1].wait(dve, b - 1)
                            dve.tensor_copy(mt[1][:], ps[0:PARTS * NH // 2, BK5, :].bitcast(BF16)[:, 0:T]).then_inc(mt_ready[1].sem, 1)
                        if moe:
                            ce_ready.wait(dve, b - 1)
                            dve.reciprocal(lrec[:], lsum[:])
                            dve.drain()
                            for n, t0, t1 in GROUPS:
                                last = dve.tensor_tensor(lexp[0:n, t0:t1], lexp[0:n, t0:t1], lrec[0:n, t0:t1].unsqueeze(
                                    2).broadcast_to((n, t1 - t0, NS)), ALU.mult)
                            last.then_inc(c_ready.sem, 1)
                        if moe:
                            de_ready.wait(dve, b - 1)
                            dve.reciprocal(drec[:], dsum[:])
                            dve.drain()
                            dve.tensor_scalar(dexp[:], dexp[:], drec[:, 0:1], None, ALU.mult).then_inc(dn_ready.sem, 1)
                        if front:
                            embed_mm.wait(dve, b + 2)
                            squares_mm.wait(dve, b + 2)
                            rstd1_ready.wait(dve, b + 1)
                            dve.tensor_copy(stat1[:, 0:2], ps[0:TILE, BK7, 0:2 * (D + 1)].rearrange(
                                "p (k d) -> p k d", k=2)[:, :, D])
                            dve.tensor_copy(stat1[:, 2:4], ps[0:TILE, BK7, 2 * (D + 1):2 * (D + 1) + 2]).then_inc(stat_ready.sem, 1)
                        if front:
                            rstd1_ready.wait(dve, b + 2)
                            held.wait(dve, b)
                            for t in range(2):
                                dve.scalar_tensor_tensor(out=h_new[i][0:TILE, t], in0=ps[0:TILE, BK7, (D + 1) * t:(D + 1) * t + D],
                                                         scalar=rstd1[:, t:t + 1], in1=hb[0:TILE], op0=ALU.mult, op1=ALU.add)
                            dve.drain()
                            txt_in.wait(dve, b + 2)
                            rstd2_ready.wait(dve, b + 1)
                            norm_stats(h_new[i], bn, mv1).then_inc(ln1_ready.sem, 1)
                        if moe:
                            d_mm.wait(dve, b - 1)
                            for n, t0, t1 in GROUPS:
                                last = dve.tensor_tensor(disp[0:n, t0:t1], ps[0:n, BK4, NS * t0:NS * t1].rearrange(
                                    "p (t s) -> p t s", s=NS), alpha[0:n, t0:t1].unsqueeze(2).broadcast_to(
                                    (n, t1 - t0, NS)), ALU.mult)
                            last.then_inc(dp_ready.sem, 1)
                        if front:
                            rstd2_ready.wait(dve, b + 2)
                            xt_mm.wait(dve, b + 1)
                            for t, (_, nt) in enumerate(TTILES):
                                last = dve.tensor_scalar(xhat[0:nt, t], h_new[i][0:nt, t], mv1[0:nt, t, 0:1],
                                                         rstd2[0:nt, t:t + 1], ALU.subtract, ALU.mult)
                            last.then_inc(xhat_ready.sem, 1)
                        if att:
                            for t, (_, nt) in enumerate(TTILES):
                                heads = ps[0:nt, (BK4, BK5, BK7)[t], 0:3 * 128].rearrange("p (h e) -> p h e", h=NH)
                                yr_mm.wait(dve, b, t + 1)
                                dve.reciprocal(rden[0:nt, t], heads[:, :, HD])
                                dve.drain()
                                dve.tensor_tensor(ynorm[0:nt, t].rearrange("p (h e) -> p h e", h=NH), heads[:, :, 0:HD],
                                                  rden[0:nt, t].unsqueeze(2).broadcast_to((nt, NH, HD)), ALU.mult
                                                  ).then_inc(yn_ready.sem, 1)
                        if front:
                            for side in range(2):
                                qk_mm.wait(dve, b + 2, side + 1)
                                if side == 0:
                                    rot_ready.wait(dve, b + 1)
                                    p3_ready.wait(dve, b + 1)
                                for table, dst in ((cos_t, by_cos), (sin_t, by_sin)):
                                    last = dve.tensor_tensor(dst[:, side], ps[0:HALF, SC + 2 * side:SC + 2 * side + 2, 0:T],
                                                             table[:].unsqueeze(1).broadcast_to((HALF, SE, T)), ALU.mult)
                                last.then_inc(rope_ready.sem, 1)
                        if att:
                            proj_mm.wait(dve, b)
                            held.wait(dve, b)
                            h_out.wait(dve, b - 1)
                            dve.tensor_tensor(h1[0:TILE, 0:2], ps[0:TILE, BK5, 0:2 * D].rearrange("p (t d) -> p t d", t=2),
                                              h_held[0:TILE, 0:2], ALU.add)
                            dve.tensor_tensor(h1[:, 2], ps[:, BK7, 0:D], h_held[:, 2], ALU.add).then_inc(h1_ready.sem, 1)
                            beta_ready.wait(dve, b - 1, apart=True)
                            dve.drain()
                            norm_stats(h1, bn2, mv2).then_inc(ln2_ready.sem, 1)
                            dve.drain()
                            ym_mm.wait(dve, b - 1)
                            zs_ready.wait(dve, b - 1)
                            for t, (_, nt) in enumerate(TTILES):
                                last = dve.scalar_tensor_tensor(out=z[0:nt, t], in0=h1[0:nt, t], scalar=mv2[0:nt, t, 0:1],
                                                                in1=nwb[0:nt], op0=ALU.subtract, op1=ALU.mult)
                            last.then_inc(z_ready.sem, 1)

                    run(step, dve)

                @block.gpsimd
                def _(pool):
                    def power(dst, src, e):
                        pool.drain()
                        return pool.tensor_tensor(dst, src, e, ALU.pow)

                    def maxima_parts(b, g):
                        six = negmax[:, :, NH // 2 * g:NH // 2 * (g + 1)]
                        max_ready.wait(pool, b, NH // 2 * (g + 1))
                        mt_mm.wait(pool, b - 1, g + 1)
                        pool.tensor_tensor(mpart[g][:, :, 0], six, zero[:], ALU.add)
                        pool.drain()
                        pool.tensor_tensor(mrest[:], six, mpart[g][:, :, 0], ALU.subtract)
                        pool.drain()
                        pool.tensor_copy(mpart[g][:, :, 1], mrest[:])
                        pool.drain()
                        pool.tensor_tensor(mpart[g][:, :, 2], mrest[:], mpart[g][:, :, 1], ALU.subtract
                                           ).then_inc(mpart_ready.sem, 1)
                        pool.drain()

                    def step(b, i):
                        moe, att, front, mid = has(b - 1), has(b), has(b + 2), has(b + 1)
                        if mid:
                            for side in range(2):
                                p1_ready.wait(pool, b + 1, side + 1)
                                pool.tensor_tensor(rest[:, side], rot[:, side], part[0][:, side], ALU.subtract
                                                   ).then_inc(rest_ready.sem, 1)
                        if moe:
                            ln2_ready.wait(pool, b - 1)
                            dp_ready.wait(pool, b - 2)
                            var = mv2[:, :, 1]
                            pool.tensor_tensor(alpha[:], var, eps[:], ALU.add)
                            power(alpha[:], alpha[:], neg_half[:])
                            pool.drain()
                            pool.tensor_tensor(pw[:], alpha[:], alpha[:], ALU.mult)
                            pool.drain()
                            pool.tensor_tensor(pw[:], var, pw[:], ALU.mult)
                            pool.drain()
                            pool.tensor_scalar(pw[:], pw[:], EPS, 1.0, ALU.add, ALU.mult)
                            power(pw[:], pw[:], neg_half[:])
                            pool.drain()
                            pool.tensor_tensor(alpha[:], alpha[:], pw[:], ALU.mult)
                            zs_ready.wait(pool, b - 1, apart=True)
                            power(pw[:], zss[:], pos_half[:])
                            pool.drain()
                            pool.tensor_tensor(pw[:], pw[:], alpha[:], ALU.mult)
                            pool.drain()
                            pool.tensor_scalar(pw[:], pw[:], 1e-5, 0.0, ALU.max, ALU.add)
                            power(pw[:], pw[:], neg_one[:])
                            pool.drain()
                            pool.tensor_tensor(beta_t[:], pw[:], alpha[:], ALU.mult).then_inc(beta_ready.sem, 1)
                        if att:
                            maxima_parts(b, 0)
                        if mid:
                            stack_in.wait(pool, b)
                            for side in range(2):
                                p2_ready.wait(pool, b + 1, side + 1)
                                pool.tensor_tensor(part[2][:, side], rest[:, side], part[1][:, side], ALU.subtract
                                                   ).then_inc(p3_ready.sem, 1)
                        if att:
                            maxima_parts(b, 1)
                        if front:
                            stat_ready.wait(pool, b + 2)
                            pool.tensor_tensor(rstd1[:], stat1[:, 0:2], stat1[:, 0:2], ALU.mult)
                            pool.drain()
                            pool.tensor_tensor(rstd1[:], stat1[:, 2:4], rstd1[:], ALU.subtract)
                            pool.drain()
                            pool.tensor_scalar(rstd1[:], rstd1[:], 0.0, EPS, ALU.max, ALU.add)
                            power(rstd1[:], rstd1[:], neg_half[0:TILE, 0:2]).then_inc(rstd1_ready.sem, 1)
                            ln1_ready.wait(pool, b + 2)
                            pool.tensor_tensor(rstd2[:], mv1[:, :, 1], eps[:], ALU.add)
                            power(rstd2[:], rstd2[:], neg_half[:]).then_inc(rstd2_ready.sem, 1)
                            for side in range(2):
                                rope_ready.wait(pool, b + 2, side + 1)
                                pool.tensor_tensor(rot[:, side, 0], by_cos[:, side, 0], by_sin[:, side, 1], ALU.subtract)
                                pool.tensor_tensor(rot[:, side, 1], by_sin[:, side, 0], by_cos[:, side, 1], ALU.add
                                                   ).then_inc(rot_ready.sem, 1)

                    run(step, pool)

        with ExitStack() as work:
            RING = 4
            w1 = [work.enter_context(nc.sbuf_tensor(f"w1_{i}", [HALF + 1, 2, F], F32)) for i in range(RING)]
            w2 = [work.enter_context(nc.sbuf_tensor(f"w2_{i}", [128, FC, D], F32)) for i in range(RING)]
            act_t = [work.enter_context(nc.sbuf_tensor(f"act_t{i}", [128, FC, B], F32)) for i in range(RING)]
            pair_out = [work.enter_context(nc.sbuf_tensor(f"pair_out{i}", [2 * B, D], F32)) for i in range(2)]
            w_in = [work.enter_context(nc.semaphore(f"w_in{i}")) for i in range(RING)]
            o_out = [work.enter_context(nc.semaphore(f"o_out{i}")) for i in range(2)]
            up_mm, gelu_ready, down_mm, pair_ready = (work.enter_context(nc.semaphore(n)) for n in
                                                      ("up_mm", "gelu_ready", "down_mm", "pair_ready"))
            block = work.enter_context(nc.Block())

            def one(s):
                return bass.ds(s, 1)

            def turns(engine, turn):
                turn(0, True)
                with engine.Fori(RING, NS - RING + 1, RING) as s:
                    turn(s, False)

            @block.sync
            def _(sp):
                def load(s, k):
                    sp.dma_start(w1[k][0:HALF], fc1[one(s)].rearrange("o (c p) f -> p (o c) f", c=2)).then_inc(w_in[k], 16)
                    sp.dma_start(w1[k][HALF:HALF + 1, 0, :], b1[one(s)]).then_inc(w_in[k], 16)
                    sp.dma_start(w2[k][:], fc2[one(s)].rearrange("o (c p) d -> p (o c) d", c=FC)).then_inc(w_in[k], 16)

                for k in range(RING):
                    load(k, k)
                with sp.Fori(0, NS - 2 * RING + 1, RING) as s:
                    for k in range(RING):
                        if k % 2 == 0:
                            sp.wait_ge(down_mm, s // 2 + k // 2 + 1)
                        load(s + RING + k, k)

            @block.tensor
            def _(pe):
                def turn(s, first):
                    for k in range(RING):
                        pe.wait_ge(w_in[k], 12 * s + 48)
                        if k == 0 and not first:
                            pe.wait_ge(gelu_ready, s)
                        for f in range(FC):
                            for c in range(2):
                                kk = HALF + 1 - c
                                mm = pe.matmul(ps[:, k, B * f:B * (f + 1)], w1[k][0:kk, c, 128 * f:128 * (f + 1)],
                                               y_all[0:kk, c, one(s + k), :].rearrange("p o b -> p (o b)"),
                                               start=(c == 0), stop=(c == 1))
                        mm.then_inc(up_mm, 1)
                        if k % 2 == 1:
                            pe.wait_ge(gelu_ready, s + k + 1)
                            pair = k // 2
                            if not first:
                                pe.wait_ge(pair_ready, s // 2 + pair)
                            for f in range(FC):
                                for j in range(2):
                                    mm = pe.matmul(ps[B * j:B * (j + 1), 4 + pair, 0:D], act_t[k - 1 + j][:, f, :],
                                                   w2[k - 1 + j][:, f, :], start=(f == 0), stop=(f == FC - 1),
                                                   skip_group_check=True)
                            mm.then_inc(down_mm, 1)

                turns(pe, turn)

            @block.scalar
            def _(act):
                def turn(s, first):
                    for k in range(RING):
                        act.wait_ge(up_mm, s + k + 1)
                        if k % 2 == 0 and not first:
                            act.wait_ge(down_mm, (s + k - 2) // 2)
                        nc.scalar.activation(act_t[k][:].rearrange("p f b -> p (f b)"), ps[:, k, 0:FC * B], ACT.Gelu
                                             ).then_inc(gelu_ready, 1)

                turns(act, turn)

            @block.vector
            def _(dve):
                def turn(s, first):
                    for pair in range(2):
                        dve.wait_ge(down_mm, s // 2 + pair + 1)
                        if not first:
                            dve.wait_ge(o_out[pair], 8 * s)
                        dve.tensor_copy(pair_out[pair][:], ps[:, 4 + pair, 0:D]).then_inc(pair_ready, 1)

                turns(dve, turn)

            @block.gpsimd
            def _(pool):
                def turn(s, first):
                    for pair in range(2):
                        pool.wait_ge(pair_ready, s // 2 + pair + 1)
                        for j in range(2):
                            pool.dma_start(oscr[:, one(s + 2 * pair + j), :].rearrange("b o d -> b (o d)"),
                                           pair_out[pair][B * j:B * (j + 1)]).then_inc(o_out[pair], 16)

                turns(pool, turn)
                for pair in range(2):
                    pool.wait_ge(o_out[pair], 8 * NS)

        with ExitStack() as work:
            N4 = 4
            h_i = [work.enter_context(nc.sbuf_tensor(f"h_i{i}", [TILE, 2 * N4, D], F32)) for i in range(2)]
            h_t = [work.enter_context(nc.sbuf_tensor(f"h_t{i}", [TXT, N4, D], F32)) for i in range(2)]
            cw = [work.enter_context(nc.sbuf_tensor(f"cw{i}", [NS, N4, T], F32)) for i in range(2)]
            ow = [work.enter_context(nc.sbuf_tensor(f"ow{i}", [NS, N4, D], F32)) for i in range(2)]
            b2_t = work.enter_context(nc.sbuf_tensor("b2_t", [NS, D], F32))
            in_sem = [work.enter_context(nc.semaphore(f"group_in{i}")) for i in range(2)]
            out_sem = [work.enter_context(nc.semaphore(f"group_out{i}")) for i in range(2)]
            b2_in, biased, mix_mm, summed = (work.enter_context(nc.semaphore(n)) for n in
                                             ("b2_in", "biased", "mix_mm", "summed"))
            block = work.enter_context(nc.Block())

            @block.sync
            def _(sp):
                sp.dma_start(b2_t[:], b2).then_inc(b2_in, 16)

                def load(b, k):
                    sp.dma_start(h_i[k][:], himg[bass.ds(2 * b, 2 * N4)].rearrange("k p d -> p k d")).then_inc(in_sem[k], 16)
                    sp.dma_start(h_t[k][:], htxt[bass.ds(b, N4)].rearrange("k p d -> p k d")).then_inc(in_sem[k], 16)
                    sp.dma_start(cw[k][:], cscr[bass.ds(b, N4)].rearrange("k s t -> s k t")).then_inc(in_sem[k], 16)
                    sp.dma_start(ow[k][:], oscr[bass.ds(b, N4)].rearrange("k s d -> s k d")).then_inc(in_sem[k], 16)

                load(0, 0)
                load(N4, 1)
                with sp.Fori(2 * N4, B - 2 * N4 + 1, 2 * N4) as b:
                    for k in range(2):
                        sp.wait_ge(out_sem[k], 10 * b)
                        load(b + N4 * k, k)

            @block.vector
            def _(dve):
                dve.wait_ge(b2_in, 16)
                with dve.Fori(0, B - 2 * N4 + 1, 2 * N4) as b:
                    for k in range(2):
                        dve.wait_ge(in_sem[k], 8 * b + 64)
                        dve.tensor_tensor(ow[k][:], ow[k][:], b2_t[:].unsqueeze(1).broadcast_to((NS, N4, D)), ALU.add
                                          ).then_inc(biased, 1)
                        for n in range(N4):
                            dve.wait_ge(mix_mm, b + N4 * k + n + 1)
                            bk = 2 * (n % 2)
                            dve.tensor_tensor(h_i[k][:, 2 * n:2 * n + 2], ps[0:TILE, bk, 0:2 * D].rearrange(
                                "p (t d) -> p t d", t=2), h_i[k][:, 2 * n:2 * n + 2], ALU.add)
                            dve.tensor_tensor(h_t[k][:, n], ps[:, bk + 1, 0:D], h_t[k][:, n], ALU.add).then_inc(summed, 1)

            @block.tensor
            def _(pe):
                def groups(b, first):
                    for k in range(2):
                        pe.wait_ge(biased, b // N4 + k + 1)
                        for n in range(N4):
                            if not (first and k == 0 and n < 2):
                                pe.wait_ge(summed, b + N4 * k + n - 1)
                            bk = 2 * (n % 2)
                            for t, (t0, nt) in enumerate(TTILES):
                                mm = pe.matmul(ps[0:nt, bk + t // 2, D * (t % 2):D * (t % 2) + D],
                                               cw[k][:, n, t0:t0 + nt], ow[k][:, n, :], start=True, stop=True)
                            mm.then_inc(mix_mm, 1)

                groups(0, True)
                with pe.Fori(2 * N4, B - 2 * N4 + 1, 2 * N4) as b:
                    groups(b, False)

            @block.scalar
            def _(act):
                with act.Fori(0, B - 2 * N4 + 1, 2 * N4) as b:
                    for k in range(2):
                        act.wait_ge(summed, b + N4 * (k + 1))
                        act.dma_start(out[bass.ds(b + N4 * k, N4), PATCHES:T].rearrange("k p d -> p k d"), h_t[k][:]
                                      ).then_inc(out_sem[k], 16)
                        for n in range(N4):
                            act.dma_start(out[bass.ds(b + N4 * k + n, 1), 0:PATCHES].rearrange(
                                "o (t p) d -> p (o t) d", t=2), h_i[k][:, 2 * n:2 * n + 2]).then_inc(out_sem[k], 16)
                for k in range(2):
                    act.wait_ge(out_sem[k], 10 * B)


_INS = ['x', 'txt', 'L0_tok_ln_gamma', 'L0_tok_ln_beta', 'L0_tok_W', 'L0_tok_b', 'L0_attn_norm_scale',
        'L0_attn_norm_bias', 'L0_attn_W_attn', 'L0_attn_b_attn', 'L0_attn_W_proj', 'L0_attn_b_proj', 'L0_attn_sinks',
        'L0_attn_rezero', 'L0_ffn_slots', 'L0_ffn_scale', 'L0_ffn_fc1_weight', 'L0_ffn_fc1_bias', 'L0_ffn_fc2_weight',
        'L0_ffn_fc2_bias', 'L0_ffn_norm_weight']


def _constants():
    import numpy as np

    half = np.arange(PAIR, dtype=np.float32) * 2 / np.float32(HD)
    freqs = (np.float32(1.0) / np.power(np.float32(10000.0), half)).astype(np.float32)
    angle = (np.arange(T, dtype=np.float32)[:, None] * freqs).astype(np.float32)
    by_pair = np.repeat(angle.T, NH, axis=0)
    i = np.arange(128)
    mult = np.zeros((ROWS, 2 * WIN2), np.float32)
    for c in range(C):
        for r in range(-1, PATCH + 1):
            p = C * PATCH + c if r < 0 else C * PATCH + C + c if r == PATCH else c * PATCH + r
            for q in range(-1, PATCH + 1):
                near = ((r, q), (r, q + 1), (r, q - 1), (r + 1, q), (r - 1, q))
                mult[p, q + 1] = sum(0 <= u < PATCH and 0 <= v < PATCH for u, v in near)
    mult = np.concatenate([mult[:, :WIN2], mult[:, WIN2:]]) / np.float32(KP)
    return {"ident": np.eye(128, dtype=np.float32),
            "causal": np.where(i[None, :] > i[:, None], np.float32(MASKED), np.float32(0.0)),
            "cos": np.cos(by_pair).astype(np.float32), "sin": np.sin(by_pair).astype(np.float32),
            "mult": mult.astype(np.float32)}


def kernel(**inputs):
    import numpy as _np
    import concourse.bacc as _bacc
    from concourse.bass_utils import run_bass_kernel_spmd as _run

    nc = _bacc.Bacc("TRN2", target_bir_lowering=False, num_devices=1)
    arrays, args = {}, []
    for name, a in [(n, inputs[n]) for n in _INS] + list(_constants().items()):
        a = _np.ascontiguousarray(a)
        arrays[f"in_{name}_dram"] = a
        args.append(nc.dram_tensor(f"in_{name}_dram", a.shape, mybir.dt.from_np(a.dtype), kind="ExternalInput").ap())
    args.append(nc.dram_tensor("out_0_dram", (B, T, D), F32, kind="ExternalOutput").ap())
    early_fusion_kernel(nc, *args)
    r = _run(nc, [arrays], core_ids=[0])
    return r.results[0]["out_0_dram"]
```

```python
from contextlib import ExitStack

import concourse.bass as bass
from concourse import mybir

F32 = mybir.dt.float32
BF16 = mybir.dt.bfloat16
ACT = mybir.ActivationFunctionType
ALU = mybir.AluOpType
AX = mybir.AxisListType

B = 64
C = 3
IMG = 224
PATCH = 16
GRID = IMG // PATCH
D = 192
HALF = D // 2
TXT = 128
PATCHES = GRID * GRID
T = PATCHES + TXT
TILE = PATCHES // 2
KP = PATCH * PATCH * 5 * C
ROWS = C * (PATCH + 2)
WIN2 = 9
EPS = 1e-5

NH = 12
HD = D // NH
PAIR = HD // 2
PARTS = 3
K_PART = [0, 0, 0, 1, 1, 2]
Q_PART = [0, 1, 2, 0, 1, 0]
SLOTS = len(K_PART)
SINK_ROW = SLOTS * HD
MAX_ROW = SINK_ROW + PARTS
STACK = MAX_ROW + PARTS
KEYS = T + 1
KTILES = [(0, 128, 0), (128, 128, 127), (256, KEYS - 256, 255)]
QTILES = [(0, 68), (68, 128), (196, 128)]
TTILES = [(0, TILE), (TILE, TILE), (2 * TILE, TXT)]
GROUPS = [(TILE, 0, 2), (TXT, 2, 3)]
STRIP = 32
EMBED_AT = [0, 5, 1, 0, 2, 0, 0, 0, 1, 0, 0, 4,
            1, 1, 1, 1, 1, 0, 0, 0, 0, 0, 0, 0]
EXPC = 295
MASKED = -1e30

NS = 64
F = 768
FC = F // 128
SQ, SE = 2, 2

SC, BK4, BK5, BK6, BK7 = 0, 4, 5, 6, 7


def early_fusion_kernel(nc, x, txt, gamma, beta, W, bias, nscale, nbias, Wa, ba, Wproj, bp, sinks, rezero, slots, scale,
                        fc1, b1, fc2, b2, nw, ident_c, causal_c, cos_c, sin_c, mult_c, out):
    wscr = nc.dram_tensor("centred_weights", (KP, D), F32, kind="Internal").ap()
    himg = nc.dram_tensor("residual_image", (2 * B, TILE, D), F32, kind="Internal").ap()
    htxt = nc.dram_tensor("residual_text", (B, TXT, D), F32, kind="Internal").ap()
    cscr = nc.dram_tensor("combine_weights", (B, NS, T), F32, kind="Internal").ap()
    oscr = nc.dram_tensor("expert_outputs", (B, NS, D), F32, kind="Internal").ap()

    with ExitStack() as ctx:
        def sb(name, shape, dt=F32, c=ctx):
            return c.enter_context(nc.sbuf_tensor(name, shape, dt))

        ps = ctx.enter_context(nc.psum_tensor("ps", [128, 8, 512], F32))
        ident = sb("ident", [128, 128])
        y_all = sb("y_all", [HALF + 1, 2, NS, B])

        with ExitStack() as layers:
            window_w = sb("window_w", [2 * ROWS, WIN2, D + 1], F32, layers)
            hb = sb("hb", [128, D], F32, layers)
            wqk = sb("wqk", [HALF + 1, 2, SQ * SE, HALF], F32, layers)
            wv = sb("wv", [HALF + 1, 2, D], F32, layers)
            wp = sb("wp", [HALF + 1, 2, D], F32, layers)
            nwb = sb("nwb", [128, D], F32, layers)
            slots_t = sb("slots_t", [HALF, 2, NS], F32, layers)
            sink_p = sb("sink_p", [1, PARTS, NH], BF16, layers)
            ident_b = sb("ident_b", [128, 128], BF16, layers)
            causal = sb("causal", [128, 128], BF16, layers)
            cos_t = sb("cos_t", [HALF, T], F32, layers)
            sin_t = sb("sin_t", [HALF, T], F32, layers)

            KN = KP // 128
            with ExitStack() as work:
                def tmp(name, shape, dt=F32):
                    return work.enter_context(nc.sbuf_tensor(name, shape, dt))

                def sem(name):
                    return work.enter_context(nc.semaphore(name))

                wn = tmp("wn", [128, KN, D])
                gm, bt = tmp("gm", [128, KN]), tmp("bt", [128, KN])
                wmean = tmp("wmean", [128, 128])
                biasb = tmp("biasb", [128, D])
                wa = tmp("wa", [HALF, 2, 3 * D])
                ns, nb = tmp("ns", [HALF, 2]), tmp("nb", [HALF, 2])
                bar = tmp("bar", [1, 3 * D])
                brow = tmp("brow", [1, SQ * SE, HALF])
                bvrow = tmp("bvrow", [1, D])
                rz = tmp("rz", [HALF + 1, 1])
                sl, slsq = tmp("sl", [NS, D]), tmp("slsq", [NS, D])
                scl, sn = tmp("scl", [NS, 1]), tmp("sn", [NS, 1])
                half_c = tmp("half_c", [NS, 1])
                sink_r = tmp("sink_r", [1, NH])
                sink_rest = tmp("sink_rest", [1, NH])
                causal_f = tmp("causal_f", [128, 128])
                shifted = [tmp(f"shifted{s}", [ROWS, PATCH, D]) for s in range(5)]
                acc = tmp("acc", [ROWS, PATCH + 2, D])

                loaded, zeroed, scaled, sums = sem("loaded"), sem("zeroed"), sem("scaled"), sem("sums")
                centred, stored, shifts_in = sem("centred"), sem("stored"), sem("shifts_in")
                window_sum, placed, bias_mm, bias_rows = sem("window_sum"), sem("placed"), sem("bias_mm"), sem("bias_rows")
                slot_sq, slot_norm, slot_ready, slot_mm = sem("slot_sq"), sem("slot_norm"), sem("slot_ready"), sem("slot_mm")

                def row(v):
                    return v.rearrange("(o d) -> o d", o=1)

                with nc.Block() as block:
                    @block.sync
                    def _(sp):
                        loads = [
                            (wn[:], W.rearrange("(p k) d -> p k d", k=KN)),
                            (gm[:], gamma.rearrange("(p k) -> p k", k=KN)),
                            (bt[:], beta.rearrange("(p k) -> p k", k=KN)),
                            (biasb[:], row(bias).broadcast_to((128, D))),
                            (wa[:], Wa.rearrange("(c p) n -> p c n", c=2)),
                            (bar[:], row(ba)),
                            (wp[0:HALF], Wproj.rearrange("(c p) n -> p c n", c=2)),
                            (wp[HALF:HALF + 1, 0, :], row(bp)),
                            (rz[:], row(rezero).broadcast_to((HALF + 1, 1))),
                            (nwb[:], row(nw).broadcast_to((128, D))),
                            (sl[:], slots),
                            (scl[:], scale.rearrange("(s o) -> s o", o=1)),
                            (sink_r[:], row(sinks)),
                            (ident[:], ident_c), (causal_f[:], causal_c),
                            (cos_t[:], cos_c), (sin_t[:], sin_c),
                        ]
                        for dst, src in loads:
                            sp.dma_start(dst, src).then_inc(loaded, 16)
                        for dst, src in ((ns, nscale), (nb, nbias)):
                            sp.dma_start(dst[:], src.rearrange("(c p) -> p c", c=2),
                                         allow_slow_non_contiguous=True).then_inc(loaded, 16)
                        sp.dma_start(window_w[:, :, D:D + 1], mult_c.unsqueeze(2), allow_slow_non_contiguous=True).then_inc(loaded, 16)
                        sp.wait_ge(loaded, 16 * 20)
                        sp.wait_ge(centred, 1)
                        sp.dma_start(wscr.rearrange("(p k) d -> p k d", k=KN), wn[:]).then_inc(stored, 16)
                        sp.wait_ge(stored, 16)
                        sp.wait_ge(zeroed, 2)
                        wv5 = wscr.rearrange("(r q s c) d -> s c r q d", r=PATCH, s=5, c=C)
                        n = 0
                        for s in range(5):
                            lo, hi = {3: (0, PATCH - 1), 4: (1, PATCH)}.get(s, (0, PATCH))
                            dr = {3: 1, 4: -1}.get(s, 0)
                            for c in range(C):
                                sp.dma_start(shifted[s][PATCH * c + lo:PATCH * c + hi], wv5[s, c, lo + dr:hi + dr]
                                             ).then_inc(shifts_in, 16)
                                n += 1
                        top = C * PATCH
                        sp.dma_start(shifted[3][top:top + C], wv5[3, :, 0]).then_inc(shifts_in, 16)
                        sp.dma_start(shifted[4][top + C:top + 2 * C], wv5[4, :, PATCH - 1]).then_inc(shifts_in, 16)
                        sp.wait_ge(shifts_in, 16 * (n + 2))
                        sp.wait_ge(window_sum, 1)
                        sp.dma_start(window_w[0:ROWS, :, 0:D], acc[:, 0:WIN2]).then_inc(placed, 16)
                        sp.dma_start(window_w[ROWS:2 * ROWS, :, 0:D], acc[:, WIN2:2 * WIN2]).then_inc(placed, 16)
                        sp.wait_ge(bias_rows, 1)
                        sp.dma_start(wqk[HALF:HALF + 1, 0], brow[:]).then_inc(placed, 16)
                        sp.dma_start(wv[HALF:HALF + 1, 0], bvrow[:]).then_inc(placed, 16)
                        sp.wait_ge(placed, 64)

                    @block.gpsimd
                    def _(pool):
                        pool.memset(wmean[:], 1.0 / KP)
                        pool.memset(half_c[:], 0.5)
                        for s in range(5):
                            pool.memset(shifted[s][:], 0.0)
                        pool.memset(acc[:], 0.0).then_inc(zeroed, 1)
                        pool.drain().then_inc(zeroed, 1)
                        pool.wait_ge(slot_sq, 1)
                        pool.tensor_tensor(sn[:], sn[:], half_c[:], ALU.pow).then_inc(slot_norm, 1)

                    @block.vector
                    def _(dve):
                        dve.wait_ge(loaded, 16 * 20)
                        dve.tensor_tensor_reduce(out=slsq[:], in0=sl[:], in1=sl[:], scale=1.0, scalar=0.0, op0=ALU.mult,
                                                 op1=ALU.add, accum_out=sn[:]).then_inc(slot_sq, 1)
                        dve.tensor_scalar(wp[:, 0, :], wp[:, 0, :], rz[:, 0:1], None, ALU.mult)
                        dve.tensor_scalar(wp[0:HALF, 1, :], wp[0:HALF, 1, :], rz[0:HALF, 0:1], None, ALU.mult)
                        dve.tensor_copy(ident_b[:], ident[:])
                        dve.tensor_copy(causal[:], causal_f[:])
                        dve.wait_ge(sums, 1)
                        dve.tensor_tensor(hb[:], ps[:, 0, 0:D], biasb[:], ALU.add)
                        dve.tensor_tensor(wn[:], wn[:], gm[:].unsqueeze(2).broadcast_to((128, KN, D)), ALU.mult
                                          ).then_inc(scaled, 1)
                        dve.wait_ge(slot_norm, 1)
                        dve.tensor_scalar(sn[:], sn[:], 1e-5, None, ALU.max)
                        dve.drain()
                        dve.reciprocal(sn[:], sn[:])
                        dve.drain()
                        dve.tensor_scalar(sl[:], sl[:], sn[:, 0:1], scl[:, 0:1], ALU.mult, ALU.mult).then_inc(slot_ready, 1)
                        dve.wait_ge(bias_mm, 1)
                        dve.tensor_tensor(bar[:, 0:512], ps[0:1, 2, :], bar[:, 0:512], ALU.add)
                        dve.tensor_tensor(bar[:, 512:3 * D], ps[0:1, 3, 0:3 * D - 512], bar[:, 512:3 * D], ALU.add)
                        for c in range(2):
                            dve.tensor_scalar(wa[:, c, :], wa[:, c, :], ns[:, c:c + 1], None, ALU.mult)
                        dve.drain()
                        for side in range(2):
                            k = 0.25 if side == 0 else 1.0
                            for e in range(2):
                                for c in range(2):
                                    src = wa[:, c, D * side:D * side + D].rearrange("p (h i e) -> p i h e", h=NH, e=2)[:, :, :, e]
                                    dve.tensor_scalar(wqk[0:HALF, c, 2 * side + e, :].rearrange("p (i h) -> p i h", h=NH),
                                                      src, k, None, ALU.mult)
                                src = bar[:, D * side:D * side + D].rearrange("p (h i e) -> p i h e", h=NH, e=2)[:, :, :, e]
                                dve.tensor_scalar(brow[:, 2 * side + e, :].rearrange("p (i h) -> p i h", h=NH), src, k, None,
                                                  ALU.mult)
                        dve.tensor_copy(wv[0:HALF], wa[:, :, 2 * D:3 * D])
                        dve.tensor_copy(bvrow[:], bar[:, 2 * D:3 * D])
                        dve.tensor_copy(sink_p[:, 0], sink_r[:])
                        dve.drain()
                        dve.tensor_tensor(sink_rest[:], sink_r[:], sink_p[:, 0], ALU.subtract)
                        dve.drain()
                        dve.tensor_copy(sink_p[:, 1], sink_rest[:])
                        dve.drain()
                        dve.tensor_tensor(sink_p[:, 2], sink_rest[:], sink_p[:, 1], ALU.subtract).then_inc(bias_rows, 1)
                        dve.wait_ge(sums, 2)
                        mean = ps[:, 1, 0:D].unsqueeze(1).broadcast_to((128, KN, D))
                        dve.tensor_tensor(wn[:], wn[:], mean, ALU.subtract).then_inc(centred, 1)
                        dve.wait_ge(slot_mm, 1)
                        dve.tensor_copy(slots_t[:], ps[0:HALF, 4, 0:2 * NS].rearrange("p (c s) -> p c s", c=2))
                        dve.wait_ge(shifts_in, 16 * 17)
                        for s, col in ((0, 1), (1, 0), (2, 2), (3, 1), (4, 1)):
                            dve.drain()
                            last = dve.tensor_tensor(acc[:, col:col + PATCH], acc[:, col:col + PATCH], shifted[s][:], ALU.add)
                        last.then_inc(window_sum, 1)

                    @block.tensor
                    def _(pe):
                        pe.wait_ge(loaded, 16 * 20)
                        pe.wait_ge(zeroed, 1)
                        for k in range(KN):
                            mm = pe.matmul(ps[:, 0, 0:D], bt[:, k:k + 1].broadcast_to((128, 128)), wn[:, k, :],
                                           start=(k == 0), stop=(k == KN - 1))
                        mm.then_inc(sums, 1)
                        for bank, lo, hi in ((2, 0, 512), (3, 512, 3 * D)):
                            for c in range(2):
                                mm = pe.matmul(ps[0:1, bank, 0:hi - lo], nb[:, c:c + 1], wa[:, c, lo:hi], start=(c == 0),
                                               stop=(c == 1))
                        mm.then_inc(bias_mm, 1)
                        pe.wait_ge(scaled, 1)
                        for k in range(KN):
                            mm = pe.matmul(ps[:, 1, 0:D], wmean[:], wn[:, k, :], start=(k == 0), stop=(k == KN - 1))
                        mm.then_inc(sums, 1)
                        pe.wait_ge(slot_ready, 1)
                        for c in range(2):
                            mm = pe.transpose(ps[0:HALF, 4, NS * c:NS * (c + 1)], sl[:, HALF * c:HALF * (c + 1)],
                                              ident[0:NS, 0:NS])
                        mm.then_inc(slot_mm, 1)

            with ExitStack() as work:
                def tmp(name, shape, dt=F32):
                    return work.enter_context(nc.sbuf_tensor(name, shape, dt))

                xw = [tmp(f"xw{i}", [2 * ROWS, GRID, IMG]) for i in range(2)]
                xw_flat = [t[:].rearrange("p i w -> p (i w)") for t in xw]
                strips, per_strip = tmp("strips", [128, PATCHES]), tmp("per_strip", [128, 1])
                xsq = tmp("xsq", [2 * ROWS, GRID * IMG])
                h_new = [tmp(f"h_new{i}", [128, 3, D]) for i in range(2)]
                h_held = tmp("h_held", [128, 3, D])
                h1 = tmp("h1", [128, 3, D])
                xhat = tmp("xhat", [128, 3, D])
                z = tmp("z", [128, 3, D])
                ynorm = xhat
                xt = tmp("xt", [HALF + 1, 2, KEYS])
                zt = tmp("zt", [HALF, 2, T])
                yt = tmp("yt", [HALF + 1, 2, T])
                by_cos, by_sin = tmp("by_cos", [HALF, SQ, SE, T]), tmp("by_sin", [HALF, SQ, SE, T])
                rot = tmp("rot", [HALF, SQ, SE, T])
                rest = by_cos
                part = [tmp(f"part{i}", [HALF, SQ, SE, T], BF16) for i in range(PARTS)]
                kst = [tmp(f"kst{i}", [128, NH, 3 * 128], BF16) for i in range(2)]
                qst = [tmp(f"qst{i}", [128, NH, T], BF16) for i in range(2)]
                vaug = [tmp(f"vaug{i}", [128, 3, NH, STRIP]) for i in range(2)]
                prob = tmp("prob", [128, 8, 2 * EXPC])
                yraw = tmp("yraw", [128, 3, T])
                negmax, mrest = tmp("negmax", [128, 3, NH]), tmp("mrest", [128, 3, NH // 2])
                mpart = [tmp(f"mpart{g}", [128, 3, PARTS, NH // 2], BF16) for g in range(2)]
                mt = [tmp(f"mt{g}", [PARTS * NH // 2, T], BF16) for g in range(2)]
                rden = tmp("rden", [128, 3, NH])
                stat1, rstd1 = tmp("stat1", [TILE, 4]), tmp("rstd1", [TILE, 2])
                bn, mv1, mv2 = tmp("bn", [128, 3, 6]), tmp("mv1", [128, 3, 2]), tmp("mv2", [128, 3, 2])
                bn2 = tmp("bn2", [128, 3, 6])
                rstd2 = tmp("rstd2", [128, 3])
                zss, alpha, beta_t = tmp("zss", [128, 3]), tmp("alpha", [128, 3]), tmp("beta_t", [128, 3])
                pw = tmp("pw", [128, 3])
                neg_half, pos_half, neg_one, eps = (tmp(n, [128, 3]) for n in ("neg_half", "pos_half", "neg_one", "eps"))
                zero = tmp("zero", [128, 3, NH // 2])
                logit, lexp = tmp("logit", [128, 3, NS]), tmp("lexp", [128, 3, NS])
                lmax, lsum, lrec = tmp("lmax", [128, 3]), tmp("lsum", [128, 3]), tmp("lrec", [128, 3])
                comb = tmp("comb", [NS, T])
                dexp, dmax, dsum, drec = tmp("dexp", [NS, T]), tmp("dmax", [NS, 1]), tmp("dsum", [NS, 1]), tmp("drec", [NS, 1])
                disp = tmp("disp", [128, 3, NS])

                class Signal:

                    def __init__(self, name, per):
                        self.sem, self.per = work.enter_context(nc.semaphore(name)), per

                    def wait(self, engine, batch, k=None, apart=False):
                        k = self.per if k is None else k
                        if isinstance(batch, int):
                            if batch < 0:
                                return
                            if batch >= B:
                                batch, k = B - 1, self.per
                        if apart:
                            engine.wait_ge(prepared, 1)
                        engine.wait_ge(self.sem, batch * self.per + k)

                x_in = Signal("x_in", 16 * 10)
                txt_in, held, c_out = (
                    Signal(n, 16) for n in ("txt_in", "held", "c_out"))
                stack_in = Signal("stack_in", 16 * 24)
                h_out = Signal("h_out", 16 * 2)
                max_in = [Signal(f"max_in{g}", 16) for g in range(2)]
                embed_mm, strips_mm, squares_mm, xt_mm, v_mm, yt_mm, proj_mm = (
                    Signal(n, 1) for n in ("embed_mm", "strips_mm", "squares_mm", "xt_mm", "v_mm", "yt_mm", "proj_mm"))
                zt_mm, l_mm, lt_mm, ct_mm, d_mm, ym_mm = (
                    Signal(n, 1) for n in ("zt_mm", "l_mm", "lt_mm", "ct_mm", "d_mm", "ym_mm"))
                s_mm, st_mm = (
                    Signal(n, NH) for n in ("s_mm", "st_mm"))
                mt_mm, qk_mm = (
                    Signal(n, 2) for n in ("mt_mm", "qk_mm"))
                pv_mm, yr_mm = (
                    Signal(n, 3) for n in ("pv_mm", "yr_mm"))
                sq_ready, strips_ready, xt_ready, v_ready, yt_ready, zt_ready, zs_ready = (
                    Signal(n, 1) for n in ("sq_ready", "strips_ready", "xt_ready", "v_ready", "yt_ready", "zt_ready", "zs_ready"))
                l_scaled, ce_ready, de_ready, ct_ready, ym_ready = (
                    Signal(n, 1) for n in ("l_scaled", "ce_ready", "de_ready", "ct_ready", "ym_ready"))
                exp_ready = Signal("exp_ready", NH)
                pv_ready = Signal("pv_ready", 3)
                p1_ready, p2_ready = (
                    Signal(n, 2) for n in ("p1_ready", "p2_ready"))
                stat_ready, ln1_ready, xhat_ready, h1_ready, ln2_ready, z_ready, lmax_ready = (
                    Signal(n, 1) for n in ("stat_ready", "ln1_ready", "xhat_ready", "h1_ready", "ln2_ready", "z_ready", "lmax_ready"))
                dmax_ready, c_ready, dn_ready, dp_ready = (
                    Signal(n, 1) for n in ("dmax_ready", "c_ready", "dn_ready", "dp_ready"))
                max_ready = Signal("max_ready", NH)
                yn_ready = Signal("yn_ready", 3)
                rope_ready = Signal("rope_ready", 2)
                mt_ready = [Signal(f"mt_ready{g}", 1) for g in range(2)]
                rstd1_ready, rstd2_ready, beta_ready = (
                    Signal(n, 1) for n in ("rstd1_ready", "rstd2_ready", "beta_ready"))
                rot_ready, rest_ready, p3_ready, mpart_ready = (
                    Signal(n, 2) for n in ("rot_ready", "rest_ready", "p3_ready", "mpart_ready"))

                prepared, sinks_in = (work.enter_context(nc.semaphore(n)) for n in ("prepared", "sinks_in"))
                with nc.Block() as block:
                    @block.vector
                    def _(dve):
                        for i in range(2):
                            dve.memset(kst[i][SINK_ROW:128], 1.0)
                            dve.memset(kst[i][0:SINK_ROW, :, KEYS:3 * 128], 0.0)
                            dve.memset(kst[i][0:SINK_ROW, :, 0:1], 0.0)
                            dve.memset(vaug[i][:], 0.0)
                        for t in (xw[0], xt, *h_new, mv1, mv2, negmax, zss, stat1):
                            dve.memset(t[:], 0.0)
                        dve.memset(neg_half[:], -0.5)
                        dve.memset(eps[:], EPS)
                        dve.memset(zero[:], 0.0)
                        dve.memset(per_strip[:], 1.0 / STRIP)
                        dve.memset(pos_half[:], 0.5)
                        dve.memset(neg_one[:], -1.0)
                        for t in (lmax, lsum, mrest, rstd2):
                            dve.memset(t[:], 1.0)
                        dve.drain()
                        for i in range(2):
                            dve.memset(vaug[i][:, :, :, HD:HD + 1], 1.0)
                            dve.memset(kst[i][SINK_ROW:MAX_ROW], 0.0)
                        dve.memset(xt[HALF:HALF + 1, 0, 1:KEYS], 1.0)
                        dve.drain().then_inc(prepared, 1)

                    @block.gpsimd
                    def _(pool):
                        pool.memset(xw[1][:], 0.0)
                        for i in range(2):
                            pool.drain()
                            pool.memset(qst[i][SINK_ROW:128], 1.0)
                        pool.drain()
                        pool.memset(yt[HALF:HALF + 1, 0], 1.0)
                        pool.drain()
                        pool.memset(y_all[HALF:HALF + 1, 0], 1.0)

                    @block.sync
                    def _(sp):
                        sp.wait_ge(prepared, 1)
                        for i in range(2):
                            sp.dma_start(kst[i][SINK_ROW:MAX_ROW, :, 0:1], sink_p[:],
                                         allow_slow_non_contiguous=True).then_inc(sinks_in, 16)
                        sp.wait_ge(sinks_in, 32)

                def run(step, engine):
                    for b in range(-3, 3):
                        step(b, b % 2)
                    with engine.Fori(3, B - 4, 2) as b:
                        step(b, 1)
                        step(b + 1, 0)
                    for b in (B - 3, B - 2, B - 1, B):
                        step(b, b % 2)

                def has(batch):
                    return not isinstance(batch, int) or 0 <= batch < B

                block = work.enter_context(nc.Block())

                @block.sync
                def _(sp):
                    def one(t):
                        return t if isinstance(t, slice) else bass.ds(t, 1)

                    def load_image(b, i):
                        embed_mm.wait(sp, b - 2)
                        x_in.wait(sp, b - 1)
                        xb = x[one(b)].rearrange("o c (i r) w -> (o c) r i w", r=PATCH)
                        top = C * PATCH
                        for r0, c0, w0, wn_ in ((0, 1, 0, 216), (ROWS, 0, 8, 216)):
                            for c in range(C):
                                sp.dma_start(xw[i][r0 + PATCH * c:r0 + PATCH * (c + 1), :, c0:c0 + wn_],
                                             xb[c, :, :, w0:w0 + wn_]).then_inc(x_in.sem, 16)
                            sp.dma_start(xw[i][r0 + top:r0 + top + C, 1:GRID, c0:c0 + wn_],
                                         xb[:, PATCH - 1, 0:GRID - 1, w0:w0 + wn_]).then_inc(x_in.sem, 16)
                            sp.dma_start(xw[i][r0 + top + C:r0 + top + 2 * C, 0:GRID - 1, c0:c0 + wn_],
                                         xb[:, 0, 1:GRID, w0:w0 + wn_]).then_inc(x_in.sem, 16)

                    def store_maxima(b, i, g):
                        mt_ready[g].wait(sp, b)
                        max_in[g].wait(sp, b - 1)
                        st_mm.wait(sp, b - 2)
                        sp.dma_start(qst[i][MAX_ROW:STACK, NH // 2 * g:NH // 2 * (g + 1), :], mt[g][:]
                            ).then_inc(max_in[g].sem, 16)

                    def stack(b, i, p, side):
                        st, which = ((qst[i], Q_PART), (kst[i], K_PART))[side]
                        for slot in range(SLOTS):
                            if which[slot] == p:
                                for e in range(SE):
                                    r = HD * slot + PAIR * e
                                    dst = st[r:r + PAIR] if side == 0 else st[r:r + PAIR, :, 1:KEYS]
                                    sp.dma_start(dst, part[p][:, side, e, :]).then_inc(stack_in.sem, 16)

                    def step(b, i):
                        if has(b):
                            xhat_ready.wait(sp, b)
                            h1_ready.wait(sp, b - 1, apart=True)
                            sp.dma_start(h_held[:], h_new[i][:]).then_inc(held.sem, 16)
                        if has(b + 1):
                            stack_in.wait(sp, b)
                            st_mm.wait(sp, b - 1)
                            p1_ready.wait(sp, b + 1)
                            stack(b + 1, 1 - i, 0, 0)
                            stack(b + 1, 1 - i, 0, 1)
                        if has(b):
                            store_maxima(b, i, 0)
                        if has(b + 2):
                            held.wait(sp, b)
                            txt_in.wait(sp, b + 1)
                            xhat_ready.wait(sp, b)
                            sp.dma_start(h_new[i][:, 2, :], txt[one(b + 2)].rearrange("o t d -> (o t) d")
                                ).then_inc(txt_in.sem, 16)
                        if has(b + 1):
                            p2_ready.wait(sp, b + 1)
                            stack(b + 1, 1 - i, 1, 0)
                        if has(b):
                            store_maxima(b, i, 1)
                        if has(b + 1):
                            stack(b + 1, 1 - i, 1, 1)
                            p3_ready.wait(sp, b + 1)
                            stack(b + 1, 1 - i, 2, 0)
                            stack(b + 1, 1 - i, 2, 1)
                        if has(b + 3):
                            load_image(b + 3, 1 - i)
                        if has(b - 1):
                            ct_ready.wait(sp, b - 1)
                            c_out.wait(sp, b - 2)
                            sp.dma_start(cscr[one(b - 1)].rearrange("o s t -> (o s) t"), comb[:]).then_inc(c_out.sem, 16)
                        if has(b):
                            h1_ready.wait(sp, b)
                            h_out.wait(sp, b - 1)
                            sp.dma_start(himg[bass.ds(2 * b, 2)].rearrange("k p d -> p k d"), h1[0:TILE, 0:2]
                                ).then_inc(h_out.sem, 16)
                            sp.dma_start(htxt[one(b)].rearrange("o p d -> (o p) d"), h1[:, 2]).then_inc(h_out.sem, 16)

                    run(step, sp)
                    c_out.wait(sp, B - 1)
                    h_out.wait(sp, B - 1)

                @block.tensor
                def _(pe):
                    def embed(b, i, n):
                        if n == 0:
                            x_in.wait(pe, b)
                            h1_ready.wait(pe, b - 3)
                        half, q = divmod(n, WIN2)
                        lo = TILE * PATCH * half + q
                        mm = pe.matmul(ps[0:TILE, BK7, half * (D + 1):(half + 1) * (D + 1)],
                                       xw_flat[i][:, lo:lo + PATCH * (TILE - 1) + 1:PATCH], window_w[:, q, :],
                                       start=(q == 0), stop=(q == WIN2 - 1))
                        if n == 2 * WIN2 - 1:
                            mm.then_inc(embed_mm.sem, 1)

                    def square_strips(b, columns):
                        if columns[0] == 0:
                            sq_ready.wait(pe, b)
                            v_ready.wait(pe, b - 1)
                            zt_ready.wait(pe, b - 3)
                        for q in columns:
                            s = q % 4
                            mm = pe.matmul(ps[STRIP * s:STRIP * (s + 1), BK4, 0:PATCHES],
                                           window_w[:, q, D:D + 1].broadcast_to((2 * ROWS, STRIP)),
                                           xsq[:, q:q + PATCH * (PATCHES - 1) + 1:PATCH], start=(q < 4), stop=(q + 4 >= WIN2),
                                           skip_group_check=True)
                        if q == WIN2 - 1:
                            mm.then_inc(strips_mm.sem, 1)

                    def square_sums(b):
                        strips_ready.wait(pe, b)
                        for half in range(2):
                            col = 2 * (D + 1) + half
                            mm = pe.matmul(ps[0:TILE, BK7, col:col + 1], strips[:, TILE * half:TILE * (half + 1)],
                                           per_strip[:], start=True, stop=True)
                        mm.then_inc(squares_mm.sem, 1)

                    def scores(b, i, h):
                        bank = SC + 2 * (h % 2)
                        if h == 0:
                            stack_in.wait(pe, b)
                        if h < 2:
                            rope_ready.wait(pe, b + 1, h + 1)
                        else:
                            max_ready.wait(pe, b, h - 1)
                        for q, bk, col in ((2, bank, 0), (0, bank + 1, 0), (1, bank + 1, QTILES[0][1] + 1)):
                            q0, nq = QTILES[q]
                            keys = q0 + nq + 1
                            pe.matmul(ps[0:nq, bk, col:col + keys], qst[i][0:MAX_ROW, h, q0:q0 + nq],
                                      kst[i][0:MAX_ROW, h, 0:keys], start=True, stop=False)
                            mm = pe.matmul(ps[0:nq, bk, col + q0 + 1:col + keys], ident_b[:, 0:nq], causal[:, 0:nq],
                                           start=False, stop=True)
                        mm.then_inc(s_mm.sem, 1)

                    def scores_t(b, i, h):
                        bank = SC + 2 * (h % 2)
                        if h in (0, NH // 2):
                            max_in[h // (NH // 2)].wait(pe, b)
                        if h < 2:
                            max_ready.wait(pe, b, NH - 1 + h)
                        else:
                            exp_ready.wait(pe, b, h - 1)
                        k0, k1, k2 = (kst[i][0:STACK, h, 128 * k:128 * (k + 1)] for k in range(3))
                        q = qst[i][0:STACK, h]
                        n0 = T - EXPC
                        c1, c2 = n0, n0 + T - KTILES[1][2]
                        pe.matmul(ps[:, bank, 0:EXPC], k0, q[:, 0:EXPC], start=True, stop=False)
                        pe.matmul(ps[:, bank, 0:127], causal[:], ident_b[:, 1:128], start=False, stop=True)
                        pe.matmul(ps[:, bank + 1, 0:n0], k0, q[:, EXPC:T], start=True, stop=True)
                        pe.matmul(ps[:, bank + 1, c1:c2], k1, q[:, KTILES[1][2]:T], start=True, stop=False)
                        pe.matmul(ps[:, bank + 1, c1:c1 + 128], causal[:], ident_b[:], start=False, stop=True)
                        pe.matmul(ps[:, bank + 1, c2:EXPC], k2, q[:, KTILES[2][2]:T], start=True, stop=False)
                        pe.matmul(ps[:, bank + 1, c2:EXPC], causal[:], ident_b[:, 0:EXPC - c2], start=False,
                                  stop=True).then_inc(st_mm.sem, 1)

                    def values(b, i, g, k):
                        if k == 0:
                            exp_ready.wait(pe, b, 4 * g + 4)
                            if g == 0:
                                v_ready.wait(pe, b)
                                de_ready.wait(pe, b - 1)
                            else:
                                pv_ready.wait(pe, b, g)
                        _, nk, q0 = KTILES[k]
                        col = sum(T - KTILES[n][2] for n in range(k))
                        for s in range(4):
                            h = 4 * g + s
                            mm = pe.matmul(ps[STRIP * s:STRIP * (s + 1), BK6, q0:T], vaug[i][0:nk, k, h, :],
                                           prob[0:nk, h % 8, col:col + T - q0], start=(k == 0), stop=(k == 2),
                                           skip_group_check=True)
                        if k == 2:
                            mm.then_inc(pv_mm.sem, 1)

                    def token_values(b, tiles):
                        for t in tiles:
                            k0, nk, _ = KTILES[t]
                            for c in range(2):
                                k = HALF + 1 - c
                                mm = pe.matmul(ps[0:nk, (BK6, BK6, BK4)[t], D * (t % 2):D * (t % 2) + D],
                                               xt[0:k, c, k0:k0 + nk], wv[0:k, c, :], start=(c == 0), stop=(c == 1))
                            if t == 2:
                                mm.then_inc(v_mm.sem, 1)

                    def turn(dst_banks, src, n_src=None):
                        for c in range(2):
                            for t, (t0, nt) in enumerate(TTILES):
                                mm = pe.transpose(ps[0:HALF, dst_banks[c], t0:t0 + nt],
                                                  src[0:nt, t, HALF * c:HALF * (c + 1)], ident[0:nt, 0:nt])
                        return mm

                    def maxima(b, g):
                        for q, (q0, nq) in enumerate(QTILES):
                            mm = pe.transpose(ps[0:PARTS * NH // 2, (BK6, BK5)[g], :].bitcast(BF16)[:, q0:q0 + nq],
                                              mpart[g][0:nq, q].rearrange("p a h -> p (a h)"), ident_b[0:nq, 0:nq])
                        mm.then_inc(mt_mm.sem, 1)

                    def step(b, i):
                        moe, att, mid, front = has(b - 1), has(b), has(b + 1), has(b + 2)
                        todo = list(range(2 * WIN2)) if front else []
                        for h in range(NH):
                            if att:
                                scores(b, i, h)
                            if mid and h == 0:
                                xt_ready.wait(pe, b + 1)
                                yt_ready.wait(pe, b - 1)
                                token_values(b + 1, (0, 1))
                            if mid and h == 1:
                                token_values(b + 1, (2,))
                            for n in todo[:EMBED_AT[h]]:
                                embed(b + 2, i, n)
                            todo = todo[EMBED_AT[h]:]
                            if moe and h == 3:
                                z_ready.wait(pe, b - 1)
                                v_ready.wait(pe, b + 1)
                                h1_ready.wait(pe, b - 1)
                                turn((BK5, BK4), z).then_inc(zt_mm.sem, 1)
                            if moe and h in (7, 8):
                                zt_ready.wait(pe, b - 1)
                                for t in (0, 1) if h == 7 else (2,):
                                    t0, nt = TTILES[t]
                                    for c in range(2):
                                        mm = pe.matmul(ps[0:nt, BK5, NS * t:NS * (t + 1)], zt[:, c, t0:t0 + nt],
                                                       slots_t[:, c, :], start=(c == 0), stop=(c == 1))
                                if h == 8:
                                    mm.then_inc(l_mm.sem, 1)
                            if front and h in (5, 6):
                                square_strips(b + 2, range(4) if h == 5 else range(4, WIN2))
                            if att and h == 8:
                                v_ready.wait(pe, b + 1, apart=True)
                                mpart_ready.wait(pe, b, 1)
                                maxima(b, 0)
                            if moe and h == 10:
                                mt_ready[0].wait(pe, b, apart=True)
                                l_scaled.wait(pe, b - 1)
                                for t, (t0, nt) in enumerate(TTILES):
                                    mm = pe.transpose(ps[0:NS, BK6, t0:t0 + nt], logit[0:nt, t, :], ident[0:nt, 0:nt])
                                mm.then_inc(lt_mm.sem, 1)
                        for h in range(NH):
                            if att:
                                scores_t(b, i, h)
                            for n in todo[:EMBED_AT[NH + h]]:
                                embed(b + 2, i, n)
                            todo = todo[EMBED_AT[NH + h]:]
                            if front and h == 4:
                                square_sums(b + 2)
                            if att and h == 2:
                                l_scaled.wait(pe, b - 1, apart=True)
                                mpart_ready.wait(pe, b, 2)
                                maxima(b, 1)
                            if att and h in (5, 6, 7, 9, 10, 11):
                                values(b, i, h // 4 - 1, (h - 1) % 4)
                            if moe and h == 6:
                                zt_ready.wait(pe, b - 1, apart=True)
                                c_ready.wait(pe, b - 1)
                                for t, (t0, nt) in enumerate(TTILES):
                                    mm = pe.transpose(ps[0:NS, BK4, t0:t0 + nt], lexp[0:nt, t, :], ident[0:nt, 0:nt])
                                mm.then_inc(ct_mm.sem, 1)
                            if moe and h == 8:
                                ct_ready.wait(pe, b - 1, apart=True)
                                dn_ready.wait(pe, b - 1)
                                for t, (t0, nt) in enumerate(TTILES):
                                    mm = pe.transpose(ps[0:nt, BK4, NS * t:NS * (t + 1)], dexp[:, t0:t0 + nt],
                                                      ident[0:NS, 0:NS])
                                mm.then_inc(d_mm.sem, 1)
                        if moe:
                            dp_ready.wait(pe, b - 1)
                            mt_ready[1].wait(pe, b)
                            for c in range(2):
                                for t, (t0, nt) in enumerate(TTILES):
                                    mm = pe.matmul(ps[0:HALF, BK5, NS * c:NS * (c + 1)],
                                                   z[0:nt, t, HALF * c:HALF * (c + 1)], disp[0:nt, t, :],
                                                   start=(t == 0), stop=(t == 2))
                            mm.then_inc(ym_mm.sem, 1)
                        if front:
                            xhat_ready.wait(pe, b + 2)
                            dp_ready.wait(pe, b - 1)
                            turn((BK4, BK7), xhat).then_inc(xt_mm.sem, 1)

                        def project(side, e):
                            if side == 0 and e == 0:
                                xt_ready.wait(pe, b + 2)
                            if e == 0:
                                exp_ready.wait(pe, b, NH - 1 + side)
                            for c in range(2):
                                k = HALF + 1 - c
                                mm = pe.matmul(ps[0:HALF, SC + 2 * side + e, 0:T], wqk[0:k, c, 2 * side + e, :],
                                               xt[0:k, c, 1:KEYS], start=(c == 0), stop=(c == 1))
                            if e == 1:
                                mm.then_inc(qk_mm.sem, 1)

                        if att:
                            for k in range(3):
                                values(b, i, 2, k)
                        if front:
                            project(0, 0)
                            project(0, 1)
                        if att:
                            pv_ready.wait(pe, b)
                            for t, (t0, nt) in enumerate(TTILES):
                                if t == 0:
                                    xt_ready.wait(pe, b + 2)
                                    ym_ready.wait(pe, b - 1)
                                for g in range(3):
                                    mm = pe.transpose(ps[0:nt, (BK4, BK5, BK7)[t], 128 * g:128 * (g + 1)],
                                                      yraw[:, g, t0:t0 + nt], ident[:])
                                mm.then_inc(yr_mm.sem, 1)
                        if front:
                            project(1, 0)
                        if att:
                            yn_ready.wait(pe, b)
                            turn((BK6, BK4), ynorm).then_inc(yt_mm.sem, 1)
                        if front:
                            project(1, 1)
                        if att:
                            yt_ready.wait(pe, b)
                            for t, (t0, nt) in enumerate(TTILES):
                                for c in range(2):
                                    k = HALF + 1 - c
                                    mm = pe.matmul(ps[0:nt, (BK5, BK5, BK7)[t], D * (t % 2):D * (t % 2) + D],
                                                   yt[0:k, c, t0:t0 + nt], wp[0:k, c, :], start=(c == 0), stop=(c == 1))
                            mm.then_inc(proj_mm.sem, 1)

                    run(step, pe)

                @block.scalar
                def _(act):
                    def fn(out_, in_, f, **kw):
                        return nc.scalar.activation(out_, in_, f, **kw)

                    def split(b, which, done):
                        src, dst, need = ((rot, part[0], rot_ready), (rest, part[1], rest_ready))[which]
                        for side in range(2):
                            need.wait(act, b, side + 1)
                            if side == 0:
                                stack_in.wait(act, b - 1)
                            fn(dst[:, side], src[:, side], ACT.Copy).then_inc(done.sem, 1)

                    def step(b, i):
                        moe, att, front, mid = has(b - 1), has(b), has(b + 2), has(b + 1)
                        if mid:
                            split(b + 1, 0, p1_ready)
                        if mid:
                            v_mm.wait(act, b + 1)
                            fn(vaug[1 - i][:, 0:2, :, 0:HD], ps[:, BK6, 0:2 * D].rearrange("p (k h d) -> p k h d", k=2, h=NH),
                               ACT.Copy)
                            nk = KTILES[2][1]
                            fn(vaug[1 - i][0:nk, 2, :, 0:HD], ps[0:nk, BK4, 0:D].rearrange("p (h d) -> p h d", h=NH),
                               ACT.Copy).then_inc(v_ready.sem, 1)
                        if moe:
                            act.drain()
                            z_ready.wait(act, b - 1)
                            beta_ready.wait(act, b - 2)
                            for t, (_, nt) in enumerate(TTILES):
                                if t > 0:
                                    act.drain()
                                last = fn(lexp[0:nt].rearrange("p t s -> p (t s)"), z[0:nt, t, :], ACT.Square,
                                          accum_out=zss[0:nt, t:t + 1])
                            last.then_inc(zs_ready.sem, 1)
                        if moe:
                            zt_mm.wait(act, b - 1)
                            fn(zt[:, 0], ps[0:HALF, BK5, 0:T], ACT.Copy)
                            fn(zt[:, 1], ps[0:HALF, BK4, 0:T], ACT.Copy).then_inc(zt_ready.sem, 1)
                        if front:
                            strips_mm.wait(act, b + 2)
                            squares_mm.wait(act, b + 1)
                            fn(strips[:], ps[:, BK4, 0:PATCHES], ACT.Copy).then_inc(strips_ready.sem, 1)
                        if mid:
                            split(b + 1, 1, p2_ready)
                        if att:
                            mt_mm.wait(act, b, 1)
                            max_in[0].wait(act, b - 1)
                            fn(mt[0][:], ps[0:PARTS * NH // 2, BK6, :].bitcast(BF16)[:, 0:T], ACT.Copy
                                ).then_inc(mt_ready[0].sem, 1)
                        if moe:
                            l_mm.wait(act, b - 1)
                            beta_ready.wait(act, b - 1)
                            for t, (_, nt) in enumerate(TTILES):
                                last = fn(logit[0:nt, t, :], ps[0:nt, BK5, NS * t:NS * (t + 1)], ACT.Copy,
                                          scale=beta_t[0:nt, t:t + 1])
                            last.then_inc(l_scaled.sem, 1)
                        if moe:
                            lmax_ready.wait(act, b - 1)
                            for t, (_, nt) in enumerate(TTILES):
                                last = fn(lexp[0:nt, t, :], logit[0:nt, t, :], ACT.Exp, bias=lmax[0:nt, t:t + 1],
                                          accum_out=lsum[0:nt, t:t + 1])
                            last.then_inc(ce_ready.sem, 1)
                        if moe:
                            dmax_ready.wait(act, b - 1)
                            fn(dexp[:], ps[0:NS, BK6, 0:T], ACT.Exp, bias=dmax[:, 0:1],
                               accum_out=dsum[:, 0:1]).then_inc(de_ready.sem, 1)
                        for h in range(NH):
                            if att:
                                st_mm.wait(act, b, h + 1)
                                if h >= 8:
                                    pv_mm.wait(act, b, 1)
                                elif h % 4 == 0:
                                    pv_mm.wait(act, b - 1)
                                fn(prob[:, h % 8, :].rearrange("p (a q) -> p a q", a=2),
                                   ps[:, SC + 2 * (h % 2):SC + 2 * (h % 2) + 2, 0:EXPC], ACT.Exp).then_inc(exp_ready.sem, 1)
                            if moe and h == 6:
                                ct_mm.wait(act, b - 1)
                                c_out.wait(act, b - 2)
                                fn(comb[:], ps[0:NS, BK4, 0:T], ACT.Copy).then_inc(ct_ready.sem, 1)
                            if att and h in (7, 11):
                                heads_out(b, h // 4 - 1)
                            if moe and h == 11:
                                ym_mm.wait(act, b - 1)
                                fn(y_all[0:HALF, :, :, bass.ds(b - 1, 1)],
                                   ps[0:HALF, BK5, 0:2 * NS].rearrange("p (c s o) -> p c s o", c=2, o=1), ACT.Copy
                                   ).then_inc(ym_ready.sem, 1)
                            if front and h == 11:
                                xt_mm.wait(act, b + 2)
                                v_mm.wait(act, b + 1)
                                fn(xt[0:HALF, 0, 1:KEYS], ps[0:HALF, BK4, 0:T], ACT.Copy)
                                fn(xt[0:HALF, 1, 1:KEYS], ps[0:HALF, BK7, 0:T], ACT.Copy).then_inc(xt_ready.sem, 1)
                        if att:
                            heads_out(b, 2)
                            yt_mm.wait(act, b)
                            fn(yt[0:HALF, 0], ps[0:HALF, BK6, 0:T], ACT.Copy)
                            fn(yt[0:HALF, 1], ps[0:HALF, BK4, 0:T], ACT.Copy).then_inc(yt_ready.sem, 1)
                        if has(b + 3):
                            x_in.wait(act, b + 3)
                            strips_mm.wait(act, b + 2)
                            fn(xsq[:], xw_flat[1 - i], ACT.Square).then_inc(sq_ready.sem, 1)
                    def heads_out(b, g):
                        pv_mm.wait(act, b, g + 1)
                        if g == 0:
                            yr_mm.wait(act, b - 1)
                        fn(yraw[:, g, :], ps[:, BK6, 0:T], ACT.Copy).then_inc(pv_ready.sem, 1)

                    run(step, act)

                @block.vector
                def _(dve):
                    def norm_stats(src, bnt, mv):
                        for t, (_, nt) in enumerate(TTILES):
                            dve.bn_stats(bnt[0:nt, t, :], src[0:nt, t, :])
                        dve.drain()
                        for t, (_, nt) in enumerate(TTILES):
                            last = dve.bn_aggr(mv[0:nt, t, :], bnt[0:nt, t, :])
                        return last

                    def step(b, i):
                        moe, att, front = has(b - 1), has(b), has(b + 2)
                        for h in range(NH):
                            if att:
                                bank = SC + 2 * (h % 2)
                                if h == 0:
                                    mpart_ready.wait(dve, b - 1)
                                s_mm.wait(dve, b, h + 1)
                                for q, bk, col in ((2, bank, 0), (0, bank + 1, 0), (1, bank + 1, QTILES[0][1] + 1)):
                                    q0, nq = QTILES[q]
                                    last = dve.tensor_reduce(negmax[0:nq, q, h:h + 1], ps[0:nq, bk, col:col + q0 + nq + 1],
                                                             AX.X, ALU.max, negate=True)
                                last.then_inc(max_ready.sem, 1)
                            if moe and h == 9:
                                l_scaled.wait(dve, b - 1)
                                for n, t0, t1 in GROUPS:
                                    last = dve.tensor_reduce(lmax[0:n, t0:t1], logit[0:n, t0:t1], AX.X, ALU.max, negate=True)
                                last.then_inc(lmax_ready.sem, 1)
                        if moe:
                            lt_mm.wait(dve, b - 1)
                            dve.tensor_reduce(dmax[:], ps[0:NS, BK6, 0:T], AX.X, ALU.max, negate=True
                                ).then_inc(dmax_ready.sem, 1)
                        if att:
                            mt_mm.wait(dve, b, 2)
                            max_in[1].wait(dve, b - 1)
                            dve.tensor_copy(mt[1][:], ps[0:PARTS * NH // 2, BK5, :].bitcast(BF16)[:, 0:T]
                                ).then_inc(mt_ready[1].sem, 1)
                        if moe:
                            ce_ready.wait(dve, b - 1)
                            dve.reciprocal(lrec[:], lsum[:])
                            dve.drain()
                            for n, t0, t1 in GROUPS:
                                last = dve.tensor_tensor(lexp[0:n, t0:t1], lexp[0:n, t0:t1], lrec[0:n, t0:t1].unsqueeze(
                                    2).broadcast_to((n, t1 - t0, NS)), ALU.mult)
                            last.then_inc(c_ready.sem, 1)
                        if moe:
                            de_ready.wait(dve, b - 1)
                            dve.reciprocal(drec[:], dsum[:])
                            dve.drain()
                            dve.tensor_scalar(dexp[:], dexp[:], drec[:, 0:1], None, ALU.mult).then_inc(dn_ready.sem, 1)
                        if front:
                            embed_mm.wait(dve, b + 2)
                            squares_mm.wait(dve, b + 2)
                            rstd1_ready.wait(dve, b + 1)
                            dve.tensor_copy(stat1[:, 0:2], ps[0:TILE, BK7, 0:2 * (D + 1)].rearrange(
                                "p (k d) -> p k d", k=2)[:, :, D])
                            dve.tensor_copy(stat1[:, 2:4], ps[0:TILE, BK7, 2 * (D + 1):2 * (D + 1) + 2]
                                ).then_inc(stat_ready.sem, 1)
                        if front:
                            rstd1_ready.wait(dve, b + 2)
                            held.wait(dve, b)
                            for t in range(2):
                                dve.scalar_tensor_tensor(out=h_new[i][0:TILE, t], in0=ps[0:TILE, BK7, (D + 1) * t:(D + 1) * t + D],
                                                         scalar=rstd1[:, t:t + 1], in1=hb[0:TILE], op0=ALU.mult, op1=ALU.add)
                            dve.drain()
                            txt_in.wait(dve, b + 2)
                            rstd2_ready.wait(dve, b + 1)
                            norm_stats(h_new[i], bn, mv1).then_inc(ln1_ready.sem, 1)
                        if moe:
                            d_mm.wait(dve, b - 1)
                            for n, t0, t1 in GROUPS:
                                last = dve.tensor_tensor(disp[0:n, t0:t1], ps[0:n, BK4, NS * t0:NS * t1].rearrange(
                                    "p (t s) -> p t s", s=NS), alpha[0:n, t0:t1].unsqueeze(2).broadcast_to(
                                    (n, t1 - t0, NS)), ALU.mult)
                            last.then_inc(dp_ready.sem, 1)
                        if front:
                            rstd2_ready.wait(dve, b + 2)
                            xt_mm.wait(dve, b + 1)
                            for t, (_, nt) in enumerate(TTILES):
                                last = dve.tensor_scalar(xhat[0:nt, t], h_new[i][0:nt, t], mv1[0:nt, t, 0:1],
                                                         rstd2[0:nt, t:t + 1], ALU.subtract, ALU.mult)
                            last.then_inc(xhat_ready.sem, 1)
                        if att:
                            for t, (_, nt) in enumerate(TTILES):
                                heads = ps[0:nt, (BK4, BK5, BK7)[t], 0:3 * 128].rearrange("p (h e) -> p h e", h=NH)
                                yr_mm.wait(dve, b, t + 1)
                                dve.reciprocal(rden[0:nt, t], heads[:, :, HD])
                                dve.drain()
                                dve.tensor_tensor(ynorm[0:nt, t].rearrange("p (h e) -> p h e", h=NH), heads[:, :, 0:HD],
                                                  rden[0:nt, t].unsqueeze(2).broadcast_to((nt, NH, HD)), ALU.mult
                                                  ).then_inc(yn_ready.sem, 1)
                        if front:
                            for side in range(2):
                                qk_mm.wait(dve, b + 2, side + 1)
                                if side == 0:
                                    rot_ready.wait(dve, b + 1)
                                    p3_ready.wait(dve, b + 1)
                                for table, dst in ((cos_t, by_cos), (sin_t, by_sin)):
                                    last = dve.tensor_tensor(dst[:, side], ps[0:HALF, SC + 2 * side:SC + 2 * side + 2, 0:T],
                                                             table[:].unsqueeze(1).broadcast_to((HALF, SE, T)), ALU.mult)
                                last.then_inc(rope_ready.sem, 1)
                        if att:
                            proj_mm.wait(dve, b)
                            held.wait(dve, b)
                            h_out.wait(dve, b - 1)
                            dve.tensor_tensor(h1[0:TILE, 0:2], ps[0:TILE, BK5, 0:2 * D].rearrange("p (t d) -> p t d", t=2),
                                              h_held[0:TILE, 0:2], ALU.add)
                            dve.tensor_tensor(h1[:, 2], ps[:, BK7, 0:D], h_held[:, 2], ALU.add).then_inc(h1_ready.sem, 1)
                            beta_ready.wait(dve, b - 1, apart=True)
                            dve.drain()
                            norm_stats(h1, bn2, mv2).then_inc(ln2_ready.sem, 1)
                            dve.drain()
                            ym_mm.wait(dve, b - 1)
                            zs_ready.wait(dve, b - 1)
                            for t, (_, nt) in enumerate(TTILES):
                                last = dve.scalar_tensor_tensor(out=z[0:nt, t], in0=h1[0:nt, t], scalar=mv2[0:nt, t, 0:1],
                                                                in1=nwb[0:nt], op0=ALU.subtract, op1=ALU.mult)
                            last.then_inc(z_ready.sem, 1)

                    run(step, dve)

                @block.gpsimd
                def _(pool):
                    def power(dst, src, e):
                        pool.drain()
                        return pool.tensor_tensor(dst, src, e, ALU.pow)

                    def maxima_parts(b, g):
                        six = negmax[:, :, NH // 2 * g:NH // 2 * (g + 1)]
                        max_ready.wait(pool, b, NH // 2 * (g + 1))
                        mt_mm.wait(pool, b - 1, g + 1)
                        pool.tensor_tensor(mpart[g][:, :, 0], six, zero[:], ALU.add)
                        pool.drain()
                        pool.tensor_tensor(mrest[:], six, mpart[g][:, :, 0], ALU.subtract)
                        pool.drain()
                        pool.tensor_copy(mpart[g][:, :, 1], mrest[:])
                        pool.drain()
                        pool.tensor_tensor(mpart[g][:, :, 2], mrest[:], mpart[g][:, :, 1], ALU.subtract
                                           ).then_inc(mpart_ready.sem, 1)
                        pool.drain()

                    def step(b, i):
                        moe, att, front, mid = has(b - 1), has(b), has(b + 2), has(b + 1)
                        if mid:
                            for side in range(2):
                                p1_ready.wait(pool, b + 1, side + 1)
                                pool.tensor_tensor(rest[:, side], rot[:, side], part[0][:, side], ALU.subtract
                                                   ).then_inc(rest_ready.sem, 1)
                        if moe:
                            ln2_ready.wait(pool, b - 1)
                            dp_ready.wait(pool, b - 2)
                            var = mv2[:, :, 1]
                            pool.tensor_tensor(alpha[:], var, eps[:], ALU.add)
                            power(alpha[:], alpha[:], neg_half[:])
                            pool.drain()
                            pool.tensor_tensor(pw[:], alpha[:], alpha[:], ALU.mult)
                            pool.drain()
                            pool.tensor_tensor(pw[:], var, pw[:], ALU.mult)
                            pool.drain()
                            pool.tensor_scalar(pw[:], pw[:], EPS, 1.0, ALU.add, ALU.mult)
                            power(pw[:], pw[:], neg_half[:])
                            pool.drain()
                            pool.tensor_tensor(alpha[:], alpha[:], pw[:], ALU.mult)
                            zs_ready.wait(pool, b - 1, apart=True)
                            power(pw[:], zss[:], pos_half[:])
                            pool.drain()
                            pool.tensor_tensor(pw[:], pw[:], alpha[:], ALU.mult)
                            pool.drain()
                            pool.tensor_scalar(pw[:], pw[:], 1e-5, 0.0, ALU.max, ALU.add)
                            power(pw[:], pw[:], neg_one[:])
                            pool.drain()
                            pool.tensor_tensor(beta_t[:], pw[:], alpha[:], ALU.mult).then_inc(beta_ready.sem, 1)
                        if att:
                            maxima_parts(b, 0)
                        if mid:
                            stack_in.wait(pool, b)
                            for side in range(2):
                                p2_ready.wait(pool, b + 1, side + 1)
                                pool.tensor_tensor(part[2][:, side], rest[:, side], part[1][:, side], ALU.subtract
                                                   ).then_inc(p3_ready.sem, 1)
                        if att:
                            maxima_parts(b, 1)
                        if front:
                            stat_ready.wait(pool, b + 2)
                            pool.tensor_tensor(rstd1[:], stat1[:, 0:2], stat1[:, 0:2], ALU.mult)
                            pool.drain()
                            pool.tensor_tensor(rstd1[:], stat1[:, 2:4], rstd1[:], ALU.subtract)
                            pool.drain()
                            pool.tensor_scalar(rstd1[:], rstd1[:], 0.0, EPS, ALU.max, ALU.add)
                            power(rstd1[:], rstd1[:], neg_half[0:TILE, 0:2]).then_inc(rstd1_ready.sem, 1)
                            ln1_ready.wait(pool, b + 2)
                            pool.tensor_tensor(rstd2[:], mv1[:, :, 1], eps[:], ALU.add)
                            power(rstd2[:], rstd2[:], neg_half[:]).then_inc(rstd2_ready.sem, 1)
                            for side in range(2):
                                rope_ready.wait(pool, b + 2, side + 1)
                                pool.tensor_tensor(rot[:, side, 0], by_cos[:, side, 0], by_sin[:, side, 1], ALU.subtract)
                                pool.tensor_tensor(rot[:, side, 1], by_sin[:, side, 0], by_cos[:, side, 1], ALU.add
                                                   ).then_inc(rot_ready.sem, 1)

                    run(step, pool)

        with ExitStack() as work:
            def tiles(name, shape, n):
                return [work.enter_context(nc.sbuf_tensor(f"{name}{i}", shape, F32)) for i in range(n)]

            def sems(name, n):
                return [work.enter_context(nc.semaphore(f"{name}{i}")) for i in range(n)]

            RING = 8
            PAIRS = RING // 2
            w1, w2 = tiles("w1_", [HALF + 1, 2, F], RING), tiles("w2_", [128, FC, D], RING)
            act_t, pair_out = tiles("act_t", [128, FC, B], RING), tiles("pair_out", [2 * B, D], PAIRS)
            biases = tiles("biases", [2 * B, D], PAIRS)
            w_in, bias_in, o_out = sems("w_in", RING), sems("bias_in", PAIRS), sems("o_out", PAIRS)
            up_mm, gelu_ready, down_mm, pair_ready = (work.enter_context(nc.semaphore(n)) for n in
                                                      ("up_mm", "gelu_ready", "down_mm", "pair_ready"))
            GROUP, BUFS = 4, 4
            SPAN = GROUP * BUFS
            h_i, h_t = tiles("h_i", [TILE, 2 * GROUP, D], BUFS), tiles("h_t", [TXT, GROUP, D], BUFS)
            DUO = GROUP // 2
            cw, ow = tiles("cw", [2 * NS, DUO, T], BUFS), tiles("ow", [2 * NS, DUO, 2, D], BUFS)
            in_sem, out_sem = sems("group_in", BUFS), sems("group_out", BUFS)
            zeroed, mix_mm, summed = (work.enter_context(nc.semaphore(n)) for n in ("ow_zeroed", "mix_mm", "summed"))
            block = work.enter_context(nc.Block())

            def one(s):
                return bass.ds(s, 1)

            def turns(engine, turn):
                turn(0, True)
                with engine.Fori(RING, NS - RING + 1, RING) as s:
                    turn(s, False)

            def spans(engine, span):
                span(0, True)
                with engine.Fori(SPAN, B - SPAN + 1, SPAN) as b:
                    span(b, False)

            @block.sync
            def _(sp):
                cscr_j = [cscr.rearrange("(k j) s t -> j k s t", j=2)[j] for j in range(2)]
                oscr_j = [oscr.rearrange("(k j) s d -> j k s d", j=2)[j] for j in range(2)]

                def load_slot(s, k):
                    sp.dma_start(w1[k][0:HALF], fc1[one(s)].rearrange("o (c p) f -> p (o c) f", c=2)).then_inc(w_in[k], 16)
                    sp.dma_start(w1[k][HALF:HALF + 1, 0, :], b1[one(s)]).then_inc(w_in[k], 16)
                    sp.dma_start(w2[k][:], fc2[one(s)].rearrange("o (c p) d -> p (o c) d", c=FC)).then_inc(w_in[k], 16)

                def load_biases(s, p):
                    for j in range(2):
                        sp.dma_start(biases[p][B * j:B * (j + 1), :], b2[one(s + 2 * p + j)].broadcast_to((B, D))
                                     ).then_inc(bias_in[p], 16)

                def store_pair(s, p):
                    sp.wait_ge(pair_ready, s // 2 + p + 1)
                    sp.dma_start(oscr[:, bass.ds(s + 2 * p, 2), :].rearrange("b o d -> o b d"), pair_out[p][:]
                                 ).then_inc(o_out[p], 16)

                def load_group(b, k):
                    sp.dma_start(h_i[k][:], himg[bass.ds(2 * b, 2 * GROUP)].rearrange("k p d -> p k d")).then_inc(in_sem[k], 16)
                    sp.dma_start(h_t[k][:], htxt[bass.ds(b, GROUP)].rearrange("k p d -> p k d")).then_inc(in_sem[k], 16)
                    for j in range(2):
                        sp.dma_start(cw[k][NS * j:NS * (j + 1)], cscr_j[j][bass.ds(b // 2, DUO)].rearrange("k s t -> s k t")
                                     ).then_inc(in_sem[k], 16)

                def load_outputs(b, k):
                    for j in range(2):
                        sp.dma_start(ow[k][NS * j:NS * (j + 1), :, j, :], oscr_j[j][bass.ds(b // 2, DUO)].rearrange(
                            "k s d -> s k d")).then_inc(in_sem[k], 16)

                for k in range(RING):
                    load_slot(k, k)
                for p in range(PAIRS):
                    load_biases(0, p)
                with sp.Fori(0, NS - 2 * RING + 1, RING) as s:
                    for p in range(PAIRS):
                        sp.wait_ge(down_mm, s // 2 + p + 1)
                        load_slot(s + RING + 2 * p, 2 * p)
                        load_slot(s + RING + 2 * p + 1, 2 * p + 1)
                        store_pair(s, p)
                        load_biases(s + RING, p)
                for k in range(BUFS):
                    load_group(GROUP * k, k)
                for p in range(PAIRS):
                    store_pair(NS - RING, p)
                for p in range(PAIRS):
                    sp.wait_ge(o_out[p], 16 * (NS // RING))
                sp.wait_ge(zeroed, 1)
                for k in range(BUFS):
                    load_outputs(GROUP * k, k)
                with sp.Fori(SPAN, B - SPAN + 1, SPAN) as b:
                    for k in range(BUFS):
                        sp.wait_ge(out_sem[k], 48 // SPAN * b)
                        load_group(b + GROUP * k, k)
                        load_outputs(b + GROUP * k, k)

            @block.tensor
            def _(pe):
                def down(p):
                    for f in range(FC):
                        for j in range(2):
                            mm = pe.matmul(ps[B * j:B * (j + 1), 4 + p, 0:D], act_t[2 * p + j][:, f, :],
                                           w2[2 * p + j][:, f, :], start=(f == 0), stop=(f == FC - 1),
                                           skip_group_check=True)
                    mm.then_inc(down_mm, 1)

                def turn(s, first):
                    for k in range(RING):
                        pe.wait_ge(w_in[k], 48 // RING * s + 48)
                        if not first or k >= 4:
                            pe.wait_ge(gelu_ready, s + k - 3)
                        for f in range(FC):
                            for c in range(2):
                                kk = HALF + 1 - c
                                mm = pe.matmul(ps[:, k % 4, B * f:B * (f + 1)], w1[k][0:kk, c, 128 * f:128 * (f + 1)],
                                               y_all[0:kk, c, one(s + k), :].rearrange("p o b -> p (o b)"),
                                               start=(c == 0), stop=(c == 1))
                        mm.then_inc(up_mm, 1)
                        if k % 2 == 1 and not (first and k == 1):
                            pe.wait_ge(gelu_ready, s + k - 1)
                            if not first:
                                pe.wait_ge(pair_ready, (s + k - RING + (1 if k == 1 else -1)) // 2)
                            down((k // 2 - 1) % PAIRS)

                turns(pe, turn)
                pe.wait_ge(gelu_ready, NS)
                pe.wait_ge(pair_ready, NS // 2 - PAIRS)
                down(PAIRS - 1)

                pe.wait_ge(pair_ready, NS // 2)

                def span(b, first):
                    for k in range(BUFS):
                        pe.wait_ge(in_sem[k], 96 // SPAN * b + 96)
                        for q in range(DUO):
                            if not (first and k == 0):
                                pe.wait_ge(summed, (b + GROUP * k + 2 * q - 2) // 2)
                            for t, (t0, nt) in enumerate(TTILES):
                                mm = pe.matmul(ps[0:nt, 3 * (q % 2) + t, 0:2 * D], cw[k][:, q, t0:t0 + nt],
                                               ow[k][:, q].rearrange("p j d -> p (j d)"), start=True, stop=True)
                            mm.then_inc(mix_mm, 1)

                spans(pe, span)

            @block.scalar
            def _(act):
                def turn(s, first):
                    for k in range(RING):
                        act.wait_ge(up_mm, s + k + 1)
                        if k % 2 == 0 and not first:
                            act.wait_ge(down_mm, (s + k - RING + 2) // 2)
                        nc.scalar.activation(act_t[k][:].rearrange("p f b -> p (f b)"), ps[:, k % 4, 0:FC * B], ACT.Gelu
                                             ).then_inc(gelu_ready, 1)

                turns(act, turn)

                def span(b, first):
                    for k in range(BUFS):
                        act.wait_ge(summed, b // 2 + DUO * (k + 1))
                        bg = b + GROUP * k
                        act.dma_start(out[bass.ds(bg, GROUP), PATCHES:T].rearrange("k p d -> p k d"), h_t[k][:]
                                      ).then_inc(out_sem[k], 16)
                        for t in range(2):
                            act.dma_start(out[bass.ds(bg, GROUP), TILE * t:TILE * (t + 1)].rearrange("k p d -> p k d"),
                                          h_i[k][:, t:2 * GROUP:2]).then_inc(out_sem[k], 16)

                spans(act, span)
                for k in range(BUFS):
                    act.wait_ge(out_sem[k], 48 // SPAN * B)

            @block.gpsimd
            def _(pool):
                for k in range(BUFS):
                    pool.memset(ow[k][:], 0.0)
                pool.drain().then_inc(zeroed, 1)

            @block.vector
            def _(dve):
                def turn(s, first):
                    for p in range(PAIRS):
                        dve.wait_ge(down_mm, s // 2 + p + 1)
                        if not first:
                            dve.wait_ge(o_out[p], 16 // RING * s)
                        dve.wait_ge(bias_in[p], 32 // RING * s + 32)
                        dve.tensor_tensor(pair_out[p][:], ps[:, 4 + p, 0:D], biases[p][:], ALU.add).then_inc(pair_ready, 1)

                turns(dve, turn)

                def span(b, first):
                    for k in range(BUFS):
                        dve.wait_ge(in_sem[k], 96 // SPAN * b + 96)
                        for q in range(DUO):
                            dve.wait_ge(mix_mm, b // 2 + DUO * k + q + 1)
                            sums = [ps[0:nt, 3 * (q % 2) + t, 0:2 * D].rearrange("p (j d) -> p j d", j=2)
                                    for t, (_, nt) in enumerate(TTILES)]
                            for t in range(2):
                                held_t = h_i[k][:, 4 * q + t:4 * q + t + 3:2]
                                dve.tensor_tensor(held_t, sums[t], held_t, ALU.add)
                            held_t = h_t[k][:, 2 * q:2 * q + 2]
                            dve.tensor_tensor(held_t, sums[2], held_t, ALU.add).then_inc(summed, 1)

                spans(dve, span)


_INS = ['x', 'txt', 'L0_tok_ln_gamma', 'L0_tok_ln_beta', 'L0_tok_W', 'L0_tok_b', 'L0_attn_norm_scale',
        'L0_attn_norm_bias', 'L0_attn_W_attn', 'L0_attn_b_attn', 'L0_attn_W_proj', 'L0_attn_b_proj', 'L0_attn_sinks',
        'L0_attn_rezero', 'L0_ffn_slots', 'L0_ffn_scale', 'L0_ffn_fc1_weight', 'L0_ffn_fc1_bias', 'L0_ffn_fc2_weight',
        'L0_ffn_fc2_bias', 'L0_ffn_norm_weight']


def _constants():
    import numpy as np

    half = np.arange(PAIR, dtype=np.float32) * 2 / np.float32(HD)
    freqs = (np.float32(1.0) / np.power(np.float32(10000.0), half)).astype(np.float32)
    angle = (np.arange(T, dtype=np.float32)[:, None] * freqs).astype(np.float32)
    by_pair = np.repeat(angle.T, NH, axis=0)
    i = np.arange(128)
    mult = np.zeros((ROWS, 2 * WIN2), np.float32)
    for c in range(C):
        for r in range(-1, PATCH + 1):
            p = C * PATCH + c if r < 0 else C * PATCH + C + c if r == PATCH else c * PATCH + r
            for q in range(-1, PATCH + 1):
                near = ((r, q), (r, q + 1), (r, q - 1), (r + 1, q), (r - 1, q))
                mult[p, q + 1] = sum(0 <= u < PATCH and 0 <= v < PATCH for u, v in near)
    mult = np.concatenate([mult[:, :WIN2], mult[:, WIN2:]]) / np.float32(KP)
    return {"ident": np.eye(128, dtype=np.float32),
            "causal": np.where(i[None, :] > i[:, None], np.float32(MASKED), np.float32(0.0)),
            "cos": np.cos(by_pair).astype(np.float32), "sin": np.sin(by_pair).astype(np.float32),
            "mult": mult.astype(np.float32)}


def kernel(**inputs):
    import numpy as _np
    import concourse.bacc as _bacc
    from concourse.bass_utils import run_bass_kernel_spmd as _run

    nc = _bacc.Bacc("TRN2", target_bir_lowering=False, num_devices=1)
    arrays, args = {}, []
    for name, a in [(n, inputs[n]) for n in _INS] + list(_constants().items()):
        a = _np.ascontiguousarray(a)
        arrays[f"in_{name}_dram"] = a
        args.append(nc.dram_tensor(f"in_{name}_dram", a.shape, mybir.dt.from_np(a.dtype), kind="ExternalInput").ap())
    args.append(nc.dram_tensor("out_0_dram", (B, T, D), F32, kind="ExternalOutput").ap())
    early_fusion_kernel(nc, *args)
    r = _run(nc, [arrays], core_ids=[0])
    return r.results[0]["out_0_dram"]
```
